# Optimizing a Trainium2 kernel written in Bass

```python
import numpy as np
import jax
import jax.numpy as jnp

def _softmax(x, axis=-1):
    return jax.nn.softmax(x, axis=axis)

def _gelu(x):
    return jax.nn.gelu(x, approximate=True)

def _silu(x):
    return jax.nn.silu(x)

def _sigmoid(x):
    return jax.nn.sigmoid(x)

def _layernorm(x, axis=-1, eps=1e-05):
    m = jnp.mean(x, axis=axis, keepdims=True)
    v = jnp.var(x, axis=axis, keepdims=True)
    return (x - m) / jnp.sqrt(v + eps)

def _scatter_add(tgt, idx, src, axis=0):
    return tgt.at[idx].add(src)

def _segment_sum(src, seg, n):
    return jax.ops.segment_sum(src, seg, n)
kernel_name = 'mk_seq_postln_d2_jaxref_r8_014910'

def setup_inputs(seed: int=0):
    np.random.seed(seed)
    _w = jnp.asarray

    def _L0_attn_setup():
        import jax, jax.numpy as jnp
        from jax import lax
        import numpy as np
        DIM = 128
        H = 8
        DK = 128
        DV = 32
        GATE_NORM = 16.0

        def _gla(x, Wq, Wk, Wv, Wo, Wg, bg, Wog):
            B, S, D = x.shape
            q = (x @ Wq).reshape(B, S, H, DK)
            k = (x @ Wk).reshape(B, S, H, DK) * DK ** (-0.5)
            v = (x @ Wv).reshape(B, S, H, DV)
            alpha = jax.nn.sigmoid((x @ Wg + bg) / GATE_NORM)

            def step(state, inp):
                qt, kt, vt, at = inp
                state = at[..., None, None] * state + kt[..., None] * vt[:, :, None, :]
                out_t = jnp.einsum('bhk,bhkv->bhv', qt, state)
                return (state, out_t)
            state0 = jnp.zeros((B, H, DK, DV), x.dtype)
            xs = (jnp.moveaxis(q, 1, 0), jnp.moveaxis(k, 1, 0), jnp.moveaxis(v, 1, 0), jnp.moveaxis(alpha, 1, 0))
            _, outs = lax.scan(step, state0, xs)
            out = jnp.moveaxis(outs, 0, 1).reshape(B, S, H * DV)
            og = jax.nn.sigmoid(x @ Wog)
            return out * og @ Wo
        key = jax.random.key(seed)
        ks = jax.random.split(key, 8)
        B, S = (2, 512)

        def xavier(k, shape, gain=1.0):
            fan_in, fan_out = (shape[0], shape[1])
            lim = gain * np.sqrt(6.0 / (fan_in + fan_out))
            return jax.random.uniform(k, shape, jnp.float32, -lim, lim)
        g = 2 ** (-2.5)
        return {'x': jax.random.normal(ks[0], (B, S, DIM), jnp.float32), 'Wq': xavier(ks[1], (DIM, H * DK), g), 'Wk': xavier(ks[2], (DIM, H * DK), g), 'Wv': xavier(ks[3], (DIM, H * DV), g), 'Wo': xavier(ks[4], (H * DV, DIM)), 'Wg': xavier(ks[5], (DIM, H)), 'bg': jnp.zeros((H,), jnp.float32), 'Wog': xavier(ks[6], (DIM, H * DV))}
    _L0_attn_in = _L0_attn_setup()

    def _L0_ffn_setup():
        import jax, jax.numpy as jnp
        import numpy as np
        FP8_MAX = 448.0

        def quant_fp8(x):
            amax = jnp.max(jnp.abs(x)).astype(jnp.float32)
            scale = jnp.minimum(FP8_MAX / jnp.maximum(amax, 1e-12), FP8_MAX)
            x_fp8 = jnp.clip(x * scale, -FP8_MAX, FP8_MAX).astype(jnp.float8_e4m3fn)
            return (x_fp8, 1.0 / scale)
        key = jax.random.key(seed)
        k1, k2, k3 = jax.random.split(key, 3)
        B, S, IN, OUT = (4, 1024, 128, 128)
        input = jax.random.normal(k1, (B, S, IN), dtype=jnp.float32)
        bound = 1.0 / np.sqrt(IN)
        weight = jax.random.uniform(k2, (OUT, IN), dtype=jnp.float32, minval=-bound, maxval=bound)
        bias = jax.random.uniform(k3, (OUT,), dtype=jnp.float32, minval=-bound, maxval=bound)
        return {'input': input, 'weight': weight, 'bias': bias}
    _L0_ffn_in = _L0_ffn_setup()

    def _L1_attn_setup():
        import jax, jax.numpy as jnp
        import numpy as np
        SLOPE = 25.0
        THR = 1.0
        BETA = 0.95
        SPIKE_STEPS = 4
        NUM_HEADS = 16

        @jax.custom_vjp
        def spike(u):
            return (u > 0).astype(u.dtype)

        def _spike_fwd(u):
            return (spike(u), u)

        def _spike_bwd(u, g):
            return (g / (SLOPE * jnp.abs(u) + 1.0) ** 2,)
        spike.defvjp(_spike_fwd, _spike_bwd)

        def lif_mean(cur):

            def step(mem, _):
                reset = jax.lax.stop_gradient(spike(mem - THR))
                mem = BETA * mem + cur - reset * THR
                return (mem, spike(mem - THR))
            _, spk = jax.lax.scan(step, jnp.zeros_like(cur), None, length=SPIKE_STEPS)
            return spk.mean(axis=0)
        B, S, D = (2, 256, 128)
        key = jax.random.key(seed)
        ks = jax.random.split(key, 9)
        std = 1.0 / np.sqrt(D)
        mkw = lambda k: jax.random.uniform(k, (D, D), jnp.float32, -std, std)
        mkb = lambda k: jax.random.uniform(k, (D,), jnp.float32, -std, std)
        return {'x': jax.random.normal(ks[0], (B, S, D), jnp.float32), 'q_w': mkw(ks[1]), 'q_b': mkb(ks[2]), 'k_w': mkw(ks[3]), 'k_b': mkb(ks[4]), 'v_w': mkw(ks[5]), 'v_b': mkb(ks[6]), 'o_w': mkw(ks[7]), 'o_b': mkb(ks[8])}
    _L1_attn_in = _L1_attn_setup()

    def _L1_ffn_setup():
        import jax, jax.numpy as jnp
        import numpy as np
        HIDDEN = 128
        N_ROUTED = 16
        N_SHARED = 2
        TOP_K = 2
        MID_R = HIDDEN // 4
        MID_S = HIDDEN // 2
        key = jax.random.key(seed)
        ks = jax.random.split(key, 8)
        s = 0.02
        return {'x': jax.random.normal(ks[0], (2, 128, HIDDEN), dtype=jnp.float32), 'router_w': jax.random.normal(ks[1], (HIDDEN, N_ROUTED), dtype=jnp.float32) * s, 'wg_r': jax.random.normal(ks[2], (N_ROUTED, HIDDEN, MID_R), dtype=jnp.float32) * s, 'wu_r': jax.random.normal(ks[3], (N_ROUTED, HIDDEN, MID_R), dtype=jnp.float32) * s, 'wd_r': jax.random.normal(ks[4], (N_ROUTED, MID_R, HIDDEN), dtype=jnp.float32) * s, 'wg_s': jax.random.normal(ks[5], (N_SHARED, HIDDEN, MID_S), dtype=jnp.float32) * s, 'wu_s': jax.random.normal(ks[6], (N_SHARED, HIDDEN, MID_S), dtype=jnp.float32) * s, 'wd_s': jax.random.normal(ks[7], (N_SHARED, MID_S, HIDDEN), dtype=jnp.float32) * s}
    _L1_ffn_in = _L1_ffn_setup()
    _d = {'L0_attn_x': _L0_attn_in['x'], 'L0_attn_Wq': _L0_attn_in['Wq'], 'L0_attn_Wk': _L0_attn_in['Wk'], 'L0_attn_Wv': _L0_attn_in['Wv'], 'L0_attn_Wo': _L0_attn_in['Wo'], 'L0_attn_Wg': _L0_attn_in['Wg'], 'L0_attn_bg': _L0_attn_in['bg'], 'L0_attn_Wog': _L0_attn_in['Wog'], 'L0_ffn_weight': _L0_ffn_in['weight'], 'L0_ffn_bias': _L0_ffn_in['bias'], 'L1_attn_q_w': _L1_attn_in['q_w'], 'L1_attn_q_b': _L1_attn_in['q_b'], 'L1_attn_k_w': _L1_attn_in['k_w'], 'L1_attn_k_b': _L1_attn_in['k_b'], 'L1_attn_v_w': _L1_attn_in['v_w'], 'L1_attn_v_b': _L1_attn_in['v_b'], 'L1_attn_o_w': _L1_attn_in['o_w'], 'L1_attn_o_b': _L1_attn_in['o_b'], 'L1_ffn_router_w': _L1_ffn_in['router_w'], 'L1_ffn_wg_r': _L1_ffn_in['wg_r'], 'L1_ffn_wu_r': _L1_ffn_in['wu_r'], 'L1_ffn_wd_r': _L1_ffn_in['wd_r'], 'L1_ffn_wg_s': _L1_ffn_in['wg_s'], 'L1_ffn_wu_s': _L1_ffn_in['wu_s'], 'L1_ffn_wd_s': _L1_ffn_in['wd_s']}
    _x0 = _d['L0_attn_x']
    _d['L0_attn_x'] = jax.random.normal(jax.random.fold_in(jax.random.key(seed), 1), (8, 256, 128), dtype=_x0.dtype)
    del _x0
    return _d

def reference(L0_attn_x, L0_attn_Wq, L0_attn_Wk, L0_attn_Wv, L0_attn_Wo, L0_attn_Wg, L0_attn_bg, L0_attn_Wog, L0_ffn_weight, L0_ffn_bias, L1_attn_q_w, L1_attn_q_b, L1_attn_k_w, L1_attn_k_b, L1_attn_v_w, L1_attn_v_b, L1_attn_o_w, L1_attn_o_b, L1_ffn_router_w, L1_ffn_wg_r, L1_ffn_wu_r, L1_ffn_wd_r, L1_ffn_wg_s, L1_ffn_wu_s, L1_ffn_wd_s):

    def _L0_attn_ref(x, Wq, Wk, Wv, Wo, Wg, bg, Wog):
        import jax, jax.numpy as jnp
        from jax import lax
        import numpy as np
        DIM = 128
        H = 8
        DK = 128
        DV = 32
        GATE_NORM = 16.0

        def _gla(x, Wq, Wk, Wv, Wo, Wg, bg, Wog):
            B, S, D = x.shape
            q = (x @ Wq).reshape(B, S, H, DK)
            k = (x @ Wk).reshape(B, S, H, DK) * DK ** (-0.5)
            v = (x @ Wv).reshape(B, S, H, DV)
            alpha = jax.nn.sigmoid((x @ Wg + bg) / GATE_NORM)

            def step(state, inp):
                qt, kt, vt, at = inp
                state = at[..., None, None] * state + kt[..., None] * vt[:, :, None, :]
                out_t = jnp.einsum('bhk,bhkv->bhv', qt, state)
                return (state, out_t)
            state0 = jnp.zeros((B, H, DK, DV), x.dtype)
            xs = (jnp.moveaxis(q, 1, 0), jnp.moveaxis(k, 1, 0), jnp.moveaxis(v, 1, 0), jnp.moveaxis(alpha, 1, 0))
            _, outs = lax.scan(step, state0, xs)
            out = jnp.moveaxis(outs, 0, 1).reshape(B, S, H * DV)
            og = jax.nn.sigmoid(x @ Wog)
            return out * og @ Wo
        return _gla(x, Wq, Wk, Wv, Wo, Wg, bg, Wog)

    def _L0_ffn_ref(input, weight, bias):
        import jax, jax.numpy as jnp
        import numpy as np
        FP8_MAX = 448.0

        def quant_fp8(x):
            amax = jnp.max(jnp.abs(x)).astype(jnp.float32)
            scale = jnp.minimum(FP8_MAX / jnp.maximum(amax, 1e-12), FP8_MAX)
            x_fp8 = jnp.clip(x * scale, -FP8_MAX, FP8_MAX).astype(jnp.float8_e4m3fn)
            return (x_fp8, 1.0 / scale)
        prev_shape = input.shape
        x2d = input.reshape(-1, weight.shape[1])
        w_fp8, w_scale = quant_fp8(weight)
        x_fp8, x_scale = quant_fp8(x2d)
        acc = jnp.matmul(x_fp8.astype(jnp.float32), w_fp8.astype(jnp.float32).T)
        out2d = (acc * (x_scale * w_scale) + bias).astype(jnp.bfloat16)
        out = out2d.reshape(*prev_shape[:-1], weight.shape[0]).astype(input.dtype)
        return out

    def _L1_attn_ref(x, q_w, q_b, k_w, k_b, v_w, v_b, o_w, o_b):
        import jax, jax.numpy as jnp
        import numpy as np
        SLOPE = 25.0
        THR = 1.0
        BETA = 0.95
        SPIKE_STEPS = 4
        NUM_HEADS = 16

        @jax.custom_vjp
        def spike(u):
            return (u > 0).astype(u.dtype)

        def _spike_fwd(u):
            return (spike(u), u)

        def _spike_bwd(u, g):
            return (g / (SLOPE * jnp.abs(u) + 1.0) ** 2,)
        spike.defvjp(_spike_fwd, _spike_bwd)

        def lif_mean(cur):

            def step(mem, _):
                reset = jax.lax.stop_gradient(spike(mem - THR))
                mem = BETA * mem + cur - reset * THR
                return (mem, spike(mem - THR))
            _, spk = jax.lax.scan(step, jnp.zeros_like(cur), None, length=SPIKE_STEPS)
            return spk.mean(axis=0)
        B, S, D = x.shape
        H = NUM_HEADS
        Hd = D // H
        proj = lambda w, b: (x @ w + b).reshape(B, S, H, Hd).transpose(0, 2, 1, 3)
        q, k, v = (proj(q_w, q_b), proj(k_w, k_b), proj(v_w, v_b))
        q_agg, k_agg, v_agg = (lif_mean(q), lif_mean(k), lif_mean(v))
        scores = jnp.einsum('bhqd,bhkd->bhqk', q_agg, k_agg) / jnp.sqrt(jnp.float32(Hd))
        attn = jax.nn.softmax(scores, axis=-1)
        out = jnp.einsum('bhqk,bhkd->bhqd', attn, v_agg)
        out = out.transpose(0, 2, 1, 3).reshape(B, S, D)
        return out @ o_w + o_b

    def _L1_ffn_ref(x, router_w, wg_r, wu_r, wd_r, wg_s, wu_s, wd_s):
        import jax, jax.numpy as jnp
        import numpy as np
        HIDDEN = 128
        N_ROUTED = 16
        N_SHARED = 2
        TOP_K = 2
        MID_R = HIDDEN // 4
        MID_S = HIDDEN // 2
        orig_shape = x.shape
        flat = x.reshape(-1, orig_shape[-1])
        gs = jnp.einsum('td,ndm->tnm', flat, wg_s)
        us = jnp.einsum('td,ndm->tnm', flat, wu_s)
        out = jnp.einsum('tnm,nmd->td', jax.nn.silu(gs) * us, wd_s)
        logits = (flat @ router_w).astype(jnp.float32)
        probs = jax.nn.softmax(logits, axis=-1)
        weights, indices = jax.lax.top_k(probs, TOP_K)
        weights = weights / (weights.sum(axis=-1, keepdims=True) + 1e-09)
        weights = weights.astype(x.dtype)
        comb = jnp.sum(jax.nn.one_hot(indices, N_ROUTED, dtype=x.dtype) * weights[..., None], axis=1)
        g = jnp.einsum('td,edm->tem', flat, wg_r)
        u = jnp.einsum('td,edm->tem', flat, wu_r)
        h = jax.nn.silu(g) * u
        h = h * comb[:, :, None]
        out = out + jnp.einsum('tem,emd->td', h, wd_r)
        return out.reshape(orig_shape)
    x = L0_attn_x
    x = _layernorm(x + _L0_attn_ref(x, L0_attn_Wq, L0_attn_Wk, L0_attn_Wv, L0_attn_Wo, L0_attn_Wg, L0_attn_bg, L0_attn_Wog), axis=-1)
    x = _layernorm(x + _L0_ffn_ref(x, L0_ffn_weight, L0_ffn_bias), axis=-1)
    x = _layernorm(x + _L1_attn_ref(x, L1_attn_q_w, L1_attn_q_b, L1_attn_k_w, L1_attn_k_b, L1_attn_v_w, L1_attn_v_b, L1_attn_o_w, L1_attn_o_b), axis=-1)
    x = _layernorm(x + _L1_ffn_ref(x, L1_ffn_router_w, L1_ffn_wg_r, L1_ffn_wu_r, L1_ffn_wd_r, L1_ffn_wg_s, L1_ffn_wu_s, L1_ffn_wd_s), axis=-1)
    return x

_drawn_inputs = setup_inputs


def setup_inputs(seed=0):
    import zlib

    import numpy as np

    out = dict(_drawn_inputs(seed))
    spreads = {'L0_attn_bg': (0.0, 0.8)}
    factors = {'L0_attn_Wq': 8.0,
     'L0_attn_Wk': 8.0,
     'L0_attn_Wv': 8.0,
     'L0_attn_Wo': 8.0,
     'L0_attn_Wg': 8.0,
     'L0_attn_Wog': 8.0,
     'L1_attn_q_w': 8.0,
     'L1_attn_q_b': 8.0,
     'L1_attn_k_w': 8.0,
     'L1_attn_k_b': 8.0,
     'L1_attn_v_w': 4.57,
     'L1_attn_v_b': 4.612,
     'L1_ffn_router_w': 8.0,
     'L1_ffn_wg_r': 8.0,
     'L1_ffn_wu_r': 8.0,
     'L1_ffn_wd_r': 8.0,
     'L1_ffn_wg_s': 8.0,
     'L1_ffn_wu_s': 8.0,
     'L1_ffn_wd_s': 8.0}
    for name, (base, spread) in spreads.items():
        noise = np.random.default_rng([zlib.crc32(name.encode()), seed]).standard_normal(out[name].shape)
        drawn = base * np.exp(spread * noise) if base else spread * noise
        out[name] = jnp.asarray(drawn.astype(out[name].dtype))
    for name, factor in factors.items():
        out[name] = (out[name] * factor).astype(out[name].dtype)
    return out
```

```python
from contextlib import ExitStack

import concourse.bass as bass
from concourse import mybir

ALU = mybir.AluOpType
ACT = mybir.ActivationFunctionType
AX = mybir.AxisListType
F32 = mybir.dt.float32
BF16 = mybir.dt.bfloat16
U32 = mybir.dt.uint32
RMAX = bass.bass_isa.ReduceOp.max

P = 128
B, S, D = 8, 256, 128
C = S // P
H, DV = 8, 32
GATE_NORM = 16.0
G2 = H * DV // P
HPB = P // DV
NH, HD = 16, 8
QG = 4
NE, ME = 16, 32
NBLK = 5
EPB = P // ME
EPS = 1e-5
FP8_MAX = 448.0
STEPS = 4


def lif_thresholds():
    import numpy as np
    beta, thr = np.float32(0.95), np.float32(1.0)

    def spikes(cur):
        mem, n = np.float32(0.0), 0
        for _ in range(STEPS):
            reset = thr if mem > thr else np.float32(0.0)
            mem = np.float32(np.float32(np.float32(beta * mem) + cur) - reset)
            n += int(mem > thr)
        return n

    steps = []
    for want in range(1, STEPS + 1):
        lo, hi = np.float32(0.125), np.float32(2.0)
        while np.nextafter(lo, hi) < hi:
            mid = np.float32((np.float64(lo) + np.float64(hi)) / 2)
            if spikes(mid) >= want:
                hi = mid
            else:
                lo = mid
        steps.append(float(lo))
    return steps


def wait_apart(eng, semaphore, value, met):
    value = value if isinstance(value, int) else eng.to_reg(value)
    eng.wait_ge(*met)
    eng.wait_ge(semaphore, value)


class Chain:

    def __init__(self, eng, sem, index, per):
        self.eng, self.sem, self.index, self.per, self.k = eng, sem, index, per, 0

    def __call__(self, ins, met=None):
        self.k += 1
        ins.then_inc(self.sem, 1)
        value = self.index * self.per + self.k
        if met is None:
            self.eng.wait_ge(self.sem, value)
        else:
            wait_apart(self.eng, self.sem, value, met)

    def end(self):
        assert self.k == self.per, f"{self.k} links, {self.per} counted on"


def fused_layers(nc, a, out):
    x_dram = a["x"].rearrange("b (c p) d -> b p c d", p=P)
    out_dram = out.rearrange("b (c p) d -> b p c d", p=P)

    with ExitStack() as ctx:
        def sb(name, shape, dt=F32):
            return ctx.enter_context(nc.sbuf_tensor(name, shape, dt))

        def sem(name):
            return ctx.enter_context(nc.semaphore(name))

        wqT = sb("wqT", [P, H, P]); wkT = sb("wkT", [P, H, P])
        wvg = sb("wvg", [P, H * DV + H]); wog = sb("wog", [P, H * DV]); wo = sb("wo", [P, G2, D])
        rows = sb("rows", [P, H + 3 * D])
        cols = sb("cols", [P, 2])
        cst = sb("cst", [P, 3 * P + 4 + NE + (NBLK - 1) * P])
        ffw = sb("ffw", [P, D])
        wqkvo = sb("wqkvo", [P, 4, D])
        wr = sb("wr", [P, NE]); wup = sb("wup", [P, NBLK, 2, P]); wdn = sb("wdn", [P, NBLK, D])
        bg_r, fb_r = rows[:, 0:H], rows[:, H:H + D]
        vb_r, ob_r = rows[:, H + D:H + 2 * D], rows[:, H + 2 * D:H + 3 * D]
        ident, later, upto = cst[:, 0:P], cst[:, P:2 * P], cst[:, 2 * P:3 * P]
        gmask = cst[:, 3 * P:3 * P + 4]
        rev = cst[:, 3 * P + 4:3 * P + 4 + NE]
        esel = cst[0:NE, 3 * P + 4 + NE:]
        identb = sb("identb", [P, P], BF16)
        amat = sb("amat", [P, H, P])
        wfT = sb("wfT", [P, D], BF16)
        half = sb("half", [P, 2])

        xa = sb("xa", [P, B * C, D])
        la = sb("la", [P, B * C, H])
        lz = sb("lz", [P, 4, B * C, H])
        amax = sb("amax", [P, B + 8])
        sw = sb("sw", [P, 4]); sx = sb("sx", [P, 4]); scl = sb("scl", [P, 1])
        wq_t = sb("wq_t", [P, 4, D])

        xs = sb("xs", [P, 2, C, D]); xT = sb("xT", [P, 2, S])
        gT = sb("gT", [P, 2, H, S]); vs = sb("vs", [P, 2, C, H * DV])
        rr = sb("rr", [P, C, H, P]); dd = sb("dd", [P, C, H, P]); pp = sb("pp", [P, C, H, P])
        laB = sb("laB", [P, H * DV]); wv = sb("wv", [P, H]); vw = sb("vw", [P, H * DV])
        el = sb("el", [P, G2, P]); ogt = sb("ogt", [P, G2, S]); st = sb("st", [P, H * DV])
        t0 = sb("t0", [P, G2, P]); t1 = sb("t1", [P, G2, P]); oT = sb("oT", [P, G2, S])
        rs = sb("rs", [P, C, D]); bn = sb("bn", [P, C, 6]); mv = sb("mv", [P, C, 2]); rstd = sb("rstd", [P, 2, C])

        qy = sb("qy", [P, C, D]); qe = sb("qe", [P, C, D]); qm = sb("qm", [P, C, D]); qt = sb("qt", [P, C, D])
        q8 = sb("q8", [P, C, D], BF16); q8T = sb("q8T", [P, S], BF16)
        fb = sb("fb", [P, C, D], BF16)
        x2T = sb("x2T", [P, S]); cur = sb("cur", [P, 3, S])
        n1 = sb("n1", [P, 3, S], BF16); n2 = sb("n2", [P, 3, S], BF16)
        qn = sb("qn", [P, 2, S], BF16); kn = sb("kn", [P, S], BF16); km = sb("km", [P, 2, QG, S], BF16)
        va = sb("va", [P, 2, C, NH, 32])
        ee = sb("ee", [P, 2, 4, C, S])
        tq = sb("tq", [P, QG, C * 4, 32]); rd = sb("rd", [P, QG, C * 4]); on = sb("on", [P, C * 4, QG, HD])
        aT = sb("aT", [P, S])
        arA = sb("arA", [P, C, D]); abn = sb("abn", [P, C, 6]); amv = sb("amv", [P, C, 2]); ars = sb("ars", [P, 2, C])
        crA = sb("crA", [P, C, D]); cbn = sb("cbn", [P, C, 6]); cmv = sb("cmv", [P, C, 2]); crs = sb("crs", [P, 2, C])
        drA = sb("drA", [P, C, D]); dbn = sb("dbn", [P, C, 6]); dmv = sb("dmv", [P, C, 2]); drs = sb("drs", [P, 2, C])
        x3T = sb("x3T", [P, S])
        lg = sb("lg", [P, 8, C, NE]); ls = sb("ls", [P, 8, C]); comb = sb("comb", [P, C, NE])
        cT = sb("cT", [NE, S]); cB = sb("cB", [P, NBLK - 1, S])
        th = sb("th", [P, 2, S]); ha = sb("ha", [P, 2, S]); hb = sb("hb", [P, NBLK, S]); hc = sb("hc", [P, NBLK, S])
        yo = sb("yo", [P, 2, C, D])

        bank = [ctx.enter_context(nc.psum_tensor(f"bank{i}", [P, 512], F32)) for i in range(8)]
        two = [bank[0], bank[2]]

        w_in = sem("w_in"); w2_in = sem("w2_in"); c_in = sem("c_in")
        x0_in = [sem("x0_in_even"), sem("x0_in_odd")]; x0T_ps = sem("x0T_ps"); x0T_sb = sem("x0T_sb"); z_ps = sem("z_ps"); z_sb = sem("z_sb")
        am_ps = sem("am_ps"); am_sb = sem("am_sb"); gate = sem("gate"); la_sb = sem("la_sb"); setup = sem("setup")
        half_sb = sem("half_sb")
        wmax = sem("wmax"); wmax_all = sem("wmax_all"); wf_sb = sem("wf_sb")
        xmax = sem("xmax"); xmax_all = sem("xmax_all"); dve_one = sem("dve_one"); act_one = sem("act_one")
        x_in = [sem("x_in_even"), sem("x_in_odd")]
        xT_ps = sem("xT_ps"); v_ps = sem("v_ps"); g_ps = sem("g_ps"); ax_ps = sem("ax_ps"); we_ps = sem("we_ps")
        og_ps = sem("og_ps"); s_ps = sem("s_ps"); st_ps = sem("st_ps"); o_ps = sem("o_ps"); y_ps = sem("y_ps")
        xT_sb = sem("xT_sb"); g_sb = sem("g_sb"); d_sb = sem("d_sb"); we_sb = sem("we_sb"); og_sb = sem("og_sb")
        st_sb = sem("st_sb"); v_sb = sem("v_sb"); p_sb = sem("p_sb"); oT_sb = sem("oT_sb"); r1_sb = sem("r1_sb")
        laB_sb = sem("laB_sb"); r_sb = sem("r_sb"); dm_sb = sem("dm_sb"); vw_sb = sem("vw_sb")
        mv_sb = sem("mv_sb"); rstd_sb = sem("rstd_sb"); c_oT = sem("c_oT"); c_ln = sem("c_ln"); c_pow = sem("c_pow")

        q8_sb = sem("q8_sb"); q8T_ps = sem("q8T_ps"); q8T_sb = sem("q8T_sb"); f_ps = sem("f_ps"); f_rd = sem("f_rd")
        x2_sb = sem("x2_sb"); x2T_ps = sem("x2T_ps"); x2T_sb = sem("x2T_sb"); qk_ps = sem("qk_ps"); qk_sb = sem("qk_sb")
        vv_ps = sem("vv_ps"); vv_sb = sem("vv_sb"); qkv_sb = sem("qkv_sb")
        sc_ps = sem("sc_ps"); e_sb = sem("e_sb"); pv_ps = sem("pv_ps"); tr_sb = sem("tr_sb"); aT_sb = sem("aT_sb")
        w_ps = sem("w_ps"); w_rd = sem("w_rd"); x3_sb = sem("x3_sb"); x3T_ps = sem("x3T_ps"); x3T_sb = sem("x3T_sb")
        lg_ps = sem("lg_ps"); lg_rd = sem("lg_rd"); lge = sem("lge"); cmb_sb = sem("cmb_sb"); cT_ps = sem("cT_ps")
        cT_sb = sem("cT_sb"); cB_ps = sem("cB_ps"); cB_sb = sem("cB_sb"); up_ps = sem("up_ps"); th_sb = sem("th_sb")
        hb_sb = sem("hb_sb"); hc_sb = sem("hc_sb"); dn_ps = sem("dn_ps"); dn_rd = sem("dn_rd"); yo_sb = sem("yo_sb")
        out_done = sem("out_done")
        amv_sb = sem("amv_sb"); ars_sb = sem("ars_sb"); cmv_sb = sem("cmv_sb"); crs_sb = sem("crs_sb")
        dmv_sb = sem("dmv_sb"); drs_sb = sem("drs_sb")
        k_q = sem("k_q"); k_a = sem("k_a"); k_lif = sem("k_lif"); k_n = sem("k_n"); k_c = sem("k_c")
        k_top = sem("k_top"); k_up = sem("k_up"); k_d = sem("k_d")
        k_pa = sem("k_pa"); k_pc = sem("k_pc"); k_pd = sem("k_pd"); k_fin = sem("k_fin")

        block = ctx.enter_context(nc.Block())

        def batches(eng, body):
            body(0, 0, False, False)
            body(1, 1, True, False)
            with eng.Fori(1, B // 2) as m:
                body(m * 2, 0, True, True)
                body(m * 2 + 1, 1, True, True)

        def steps(eng, body):
            body(-1, 1)
            body(0, 0)
            with eng.Fori(0, B // 2 - 1) as m:
                body(m * 2 + 1, 1)
                body(m * 2 + 2, 0)
            body(B - 1, 1)
            body(B, 0)

        def loads(b, par):
            return b * 8 - 8 * par + 16

        def parts(i):
            if isinstance(i, int):
                return 0 <= i + 1 < B, 0 <= i < B, 0 <= i - 1 < B
            return True, True, True

        @block.sync
        def _(sp):
            for dst, name in ((cst, "cst"), (rows, "rows"), (wvg, "wvg")):
                sp.dma_start(dst[:], a[name]).then_inc(c_in, 16)

            def first(b, par, p1, p2):
                if p2:
                    sp.wait_ge(x0T_ps, b - 1)
                sp.dma_start(xs[:, par], x_dram[bass.ds(b, 1)].rearrange("a p c d -> p (a c) d")).then_inc(x0_in[par], 16)

            batches(sp, first)
            for dst, name in ((wqkvo, "wqkvo"), (cols, "cols"), (wr, "wr"), (wup, "wup"), (wdn, "wdn")):
                sp.dma_start(dst[:], a[name]).then_inc(w2_in, 16)

            sp.wait_ge(x0T_ps, B)

            def load(b, par, p1, p2):
                if p2:
                    sp.wait_ge(r1_sb, b - 1)
                sp.dma_start(xs[:, par], x_dram[bass.ds(b, 1)].rearrange("a p c d -> p (a c) d")).then_inc(x_in[par], 16)

            batches(sp, load)

            def store(b, par, p1, p2):
                sp.wait_ge(yo_sb, b + 1)
                sp.dma_start(out_dram[bass.ds(b, 1)].rearrange("a p c d -> p (a c) d"), yo[:, par]).then_inc(out_done, 16)

            batches(sp, store)
            sp.wait_ge(out_done, 16 * B)

        @block.tensor
        def _(pe):
            pe.wait_ge(c_in, 48)

            def z_of(b, par):
                pe.wait_ge(x0T_sb, b + 1)
                for c in range(C):
                    ins = nc.tensor.matmul(bank[6 + par][:, c * H:(c + 1) * H], xT[:, par, c * P:(c + 1) * P],
                                           wvg[:, H * DV:], start=True, stop=True)
                ins.then_inc(z_ps, 1)

            def gate_pass(b, par, p1, p2):
                pe.wait_ge(x0_in[par], loads(b, par))
                if p2:
                    pe.wait_ge(x0T_sb, b - 1)
                for c in range(C):
                    ins = nc.tensor.transpose(bank[4 + par][:, c * P:(c + 1) * P], xs[:, par, c, :], ident)
                ins.then_inc(x0T_ps, 1)
                if p1:
                    if p2:
                        pe.wait_ge(z_sb, b - 2)
                    z_of(b - 1, 1 - par)

            batches(pe, gate_pass)
            pe.wait_ge(z_sb, B - 2)
            z_of(B - 1, (B - 1) % 2)

            pe.wait_ge(w_in, 16 * 5)
            for h in range(H):
                ins = nc.tensor.matmul(bank[h // 4][:, (h % 4) * P:(h % 4 + 1) * P], wqT[:, h, :], wkT[:, h, :],
                                       start=True, stop=True)
            ins.then_inc(am_ps, 1)
            pe.wait_ge(am_sb, 1)
            pe.wait_ge(la_sb, 1)
            pe.wait_ge(setup, 2)

            def tail(b, par):
                pe.wait_ge(v_sb, b + 1)
                pe.wait_ge(p_sb, b * 2 + 2)
                for c in range(C):
                    for g in range(G2):
                        for j in range(HPB):
                            h = g * HPB + j
                            ins = nc.tensor.matmul(bank[6][DV * j:DV * (j + 1), (c * G2 + g) * P:(c * G2 + g + 1) * P],
                                                   vs[:, par, c, h * DV:(h + 1) * DV], pp[:, c, h, :], start=True, stop=True)
                pe.wait_ge(st_sb, b + 1)
                for g in range(G2):
                    for j in range(HPB):
                        h = g * HPB + j
                        ins = nc.tensor.matmul(bank[7][DV * j:DV * (j + 1), g * P:(g + 1) * P],
                                               st[:, h * DV:(h + 1) * DV], gT[:, par, h, P:S], start=True, stop=True)
                ins.then_inc(o_ps, 1)
                pe.wait_ge(oT_sb, b + 1)
                for c in range(C):
                    for g in range(G2):
                        ins = nc.tensor.matmul(bank[7][:, (2 + c) * P:(3 + c) * P], oT[:, g, c * P:(c + 1) * P], wo[:, g, :],
                                               start=(g == 0), stop=(g == G2 - 1))
                ins.then_inc(y_ps, 1)

            def attn(b, par, p1, p2):
                pe.wait_ge(x_in[par], loads(b, par))
                if p1:
                    pe.wait_ge(st_sb, b)
                for c in range(C):
                    ins = nc.tensor.transpose(bank[7][:, c * P:(c + 1) * P], xs[:, par, c, :], ident)
                ins.then_inc(xT_ps, 1)
                pe.wait_ge(xT_sb, b + 1)
                if p1:
                    pe.wait_ge(og_sb, b)
                for c in range(C):
                    ins = nc.tensor.matmul(bank[6][:, c * H * DV:(c + 1) * H * DV], xT[:, par, c * P:(c + 1) * P],
                                           wvg[:, 0:H * DV], start=True, stop=True)
                ins.then_inc(v_ps, 1)
                for r in range(4):
                    if p1 or r >= 2:
                        pe.wait_ge(g_sb, b * 4 + r - 1)
                    for k in range(2):
                        ins = nc.tensor.matmul(bank[4 + r % 2][:, k * S:(k + 1) * S], amat[:, 2 * r + k, :], xT[:, par, :],
                                               start=True, stop=True)
                    ins.then_inc(g_ps, 1)
                if p1:
                    pe.wait_ge(v_sb, b + 1)
                    tail(b - 1, 1 - par)

                def decay(c):
                    if p1 or c:
                        pe.wait_ge(d_sb, b * 2 + c)
                    pe.wait_ge(r_sb, b * 2 + c + 1)
                    for k in range(2):
                        ins = nc.tensor.matmul(bank[2 + k][:, :], later, rr[:, c, 4 * k:4 * k + 4, :], start=True, stop=True)
                    ins.then_inc(ax_ps, 1)

                def scores(c):
                    if p1 or c:
                        pe.wait_ge(p_sb, b * 2 + c)
                    for k in range(2):
                        ins = nc.tensor.matmul(bank[k][:, :], xT[:, par, c * P:(c + 1) * P],
                                               gT[:, par, 4 * k:4 * k + 4, c * P:(c + 1) * P], start=True, stop=True)
                    ins.then_inc(s_ps, 1)

                decay(0)
                if p1:
                    pe.wait_ge(r1_sb, b)
                nc.tensor.matmul(bank[7][:, 256:256 + H], later, la[:, bass.ds(b * 2, 1), :].rearrange("p a h -> p (a h)"),
                                 start=True, stop=True)
                pe.wait_ge(laB_sb, b + 1)
                for g in range(G2):
                    ins = nc.tensor.matmul(bank[7][:, g * P:(g + 1) * P], laB[:, g * P:(g + 1) * P], upto,
                                           start=True, stop=True)
                ins.then_inc(we_ps, 1)
                if p1:
                    pe.wait_ge(oT_sb, b)
                else:
                    pe.wait_ge(v_sb, b + 1)
                for g in range(G2):
                    ins = nc.tensor.matmul(bank[6][:, g * S:(g + 1) * S], wog[:, g * P:(g + 1) * P], xT[:, par, :],
                                           start=True, stop=True)
                ins.then_inc(og_ps, 1)
                pe.wait_ge(g_sb, b * 4 + 4)
                scores(0)
                decay(1)
                pe.wait_ge(vw_sb, b + 1)
                pe.wait_ge(we_sb, b + 1)
                nc.tensor.matmul(bank[7][:, 0:H * DV], xs[:, par, 0, :], vw[:], start=True, stop=True).then_inc(st_ps, 1)
                scores(1)

            batches(pe, attn)
            pe.wait_ge(og_sb, B)
            tail(B - 1, (B - 1) % 2)

            pe.wait_ge(wf_sb, 1)
            pe.wait_ge(w2_in, 16 * 5)
            pe.wait_ge(r1_sb, B)

            def score_half(i, par, g, half_):
                for q in (2 * half_, 2 * half_ + 1):
                    for c in range(C):
                        ins = nc.tensor.matmul(bank[q][:, c * S:(c + 1) * S],
                                               km[32 * q:32 * q + 32, par, g, c * P:(c + 1) * P],
                                               qn[32 * q:32 * q + 32, par, :], start=True, stop=True)
                ins.then_inc(sc_ps, 1)

            def score(i, par, g):
                if g == 0:
                    pe.wait_ge(qkv_sb, i + 1)
                for half_ in range(2):
                    n = i * 8 + 2 * g + half_ - 1
                    if not (isinstance(n, int) and n < 1):
                        pe.wait_ge(e_sb, n)
                    score_half(i, par, g, half_)

            def values(i, par, g):
                pe.wait_ge(e_sb, i * 8 + 2 * g + 2)
                n = i * 2 + g // 2 - 1
                if g % 2 == 0 and not (isinstance(n, int) and n < 1):
                    pe.wait_ge(tr_sb, n)
                for c in range(C):
                    for q in range(4):
                        ins = nc.tensor.matmul(bank[4 + g // 2][32 * q:32 * q + 32, (g % 2) * S:(g % 2 + 1) * S],
                                               va[:, par, c, 4 * q + g, :], ee[:, g % 2, q, c, :],
                                               start=(c == 0), stop=(c == C - 1), skip_group_check=True)
                ins.then_inc(pv_ps, 1)

            def step(i, par):
                ahead, core, behind = parts(i)
                aa, cc = i + 1, i - 1
                if core:
                    score(i, par, 0)
                if behind:
                    values(cc, 1 - par, 3)
                if ahead:
                    pe.wait_ge(q8_sb, aa + 1)
                    if not (isinstance(i, int) and i < 2):
                        pe.wait_ge(hb_sb, cc * NBLK)
                    bt = bank[6][:, 0:P].bitcast(BF16)
                    for c in range(C):
                        ins = nc.tensor.transpose(bt[:, c * P:(c + 1) * P], q8[:, c, :], identb[:])
                    ins.then_inc(q8T_ps, 1)
                    pe.wait_ge(q8T_sb, aa + 1)
                    if not (isinstance(i, int) and i < 2):
                        pe.wait_ge(dn_rd, cc)
                    for c in range(C):
                        ins = nc.tensor.matmul(bank[7][:, c * P:(c + 1) * P], q8T[:, c * P:(c + 1) * P], wfT[:],
                                               start=True, stop=True)
                    ins.then_inc(f_ps, 1)
                if core:
                    score(i, par, 1)
                    values(i, par, 0)
                if behind:
                    pe.wait_ge(aT_sb, cc + 1)
                    if not ahead:
                        pe.wait_ge(hb_sb, cc * NBLK)
                    for c in range(C):
                        ins = nc.tensor.matmul(bank[6][:, c * P:(c + 1) * P], aT[:, c * P:(c + 1) * P], wqkvo[:, 3, :],
                                               start=True, stop=True)
                    ins.then_inc(w_ps, 1)
                if ahead:
                    pe.wait_ge(x2_sb, aa + 1)
                    for c in range(C):
                        ins = nc.tensor.transpose(bank[7][:, c * P:(c + 1) * P], arA[:, c, :], ident)
                    ins.then_inc(x2T_ps, 1)
                if core:
                    score(i, par, 2)
                    values(i, par, 1)
                if behind:
                    pe.wait_ge(x3_sb, cc + 1)
                    for c in range(C):
                        ins = nc.tensor.transpose(bank[6][:, c * P:(c + 1) * P], crA[:, c, :], ident)
                    ins.then_inc(x3T_ps, 1)
                if ahead:
                    pe.wait_ge(x2T_sb, aa + 1)
                    for n in range(2):
                        ins = nc.tensor.matmul(bank[7][:, n * S:(n + 1) * S], wqkvo[:, n, :], x2T[:], start=True, stop=True)
                    ins.then_inc(qk_ps, 1)
                if behind:
                    pe.wait_ge(x3T_sb, cc + 1)
                    for c in range(C):
                        ins = nc.tensor.matmul(bank[6][:, 256 + c * NE:256 + (c + 1) * NE], x3T[:, c * P:(c + 1) * P], wr[:],
                                               start=True, stop=True)
                    ins.then_inc(lg_ps, 1)
                    pe.wait_ge(lg_rd, cc + 1)
                if ahead:
                    for c in range(C):
                        ins = nc.tensor.matmul(bank[6][:, c * P:(c + 1) * P], x2T[:, c * P:(c + 1) * P], wqkvo[:, 2, :],
                                               start=True, stop=True)
                    ins.then_inc(vv_ps, 1)
                if core:
                    score(i, par, 3)
                    values(i, par, 2)
                if behind:
                    def up(k, bk):
                        for n in range(2):
                            ins = nc.tensor.matmul(bank[bk][:, n * S:(n + 1) * S], wup[:, k, n, :], x3T[:], start=True, stop=True)
                        ins.then_inc(up_ps, 1)

                    def spread(k, bk):
                        for n in range(2):
                            ins = nc.tensor.matmul(bank[bk][:, n * S:(n + 1) * S], esel[:, (2 * k + n) * P:(2 * k + n + 1) * P],
                                                   cT[:], start=True, stop=True)
                        ins.then_inc(cB_ps, 1)

                    if ahead:
                        pe.wait_ge(qk_sb, aa + 1)
                    else:
                        pe.wait_ge(dn_rd, cc)
                    up(0, 7)
                    pe.wait_ge(cmb_sb, cc + 1)
                    if ahead:
                        pe.wait_ge(vv_sb, aa + 1)
                    for c in range(C):
                        ins = nc.tensor.transpose(bank[6][0:NE, c * P:(c + 1) * P], comb[:, c, :], ident)
                    ins.then_inc(cT_ps, 1)
                    pe.wait_ge(cT_sb, cc + 1)
                    pe.wait_ge(hb_sb, cc * NBLK + 1)
                    spread(0, 7)
                    up(1, 6)
                    pe.wait_ge(cB_sb, cc * 2 + 1)
                    up(2, 7)
                    pe.wait_ge(hb_sb, cc * NBLK + 2)
                    spread(1, 6)
                    pe.wait_ge(hb_sb, cc * NBLK + 3)
                    up(3, 7)
                    pe.wait_ge(cB_sb, cc * 2 + 2)
                    up(4, 6)
                    pe.wait_ge(hb_sb, cc * NBLK + 4)
                    for c in range(C):
                        for k in range(NBLK):
                            if c == 0 and k:
                                pe.wait_ge(hc_sb, cc * (NBLK - 1) + k)
                            src = hc if k else hb
                            ins = nc.tensor.matmul(bank[7][:, c * P:(c + 1) * P], src[:, k, c * P:(c + 1) * P], wdn[:, k, :],
                                                   start=(k == 0), stop=(k == NBLK - 1))
                    ins.then_inc(dn_ps, 1)

            steps(pe, step)

        @block.scalar
        def _(act):
            for dst, name in ((ffw, "ffw"), (wqT, "wqT"), (wkT, "wkT"), (wog, "wog"), (wo, "wo")):
                act.dma_start(dst[:], a[name]).then_inc(w_in, 16)

            def gate_pass(b, par, p1, p2):
                act.wait_ge(x0T_ps, b + 1)
                if p2:
                    act.wait_ge(z_ps, b - 1)
                nc.scalar.activation(xT[:, par, :], bank[4 + par][:, 0:S], ACT.Copy).then_inc(x0T_sb, 1)

            batches(act, gate_pass)
            act.wait_ge(am_ps, 1)
            for k in range(2):
                ins = nc.scalar.activation(amat[:, 4 * k:4 * k + 4, :], bank[k][:, :].rearrange("p (h d) -> p h d", h=4),
                                           ACT.Copy, scale=float(P) ** -0.5)
            ins.then_inc(am_sb, 1)
            act.wait_ge(z_sb, B)
            nc.scalar.activation(lz[:, 1], lz[:, 0], ACT.Abs, scale=1.0 / GATE_NORM).then_inc(act_one, 1)
            nc.scalar.activation(lz[:, 3], lz[:, 0], ACT.Relu, scale=-1.0 / GATE_NORM)
            act.wait_ge(act_one, 1)
            nc.scalar.activation(lz[:, 2], lz[:, 1], ACT.Exp, scale=-1.0).then_inc(act_one, 1)
            act.wait_ge(act_one, 2)
            nc.scalar.activation(lz[:, 1], lz[:, 2], ACT.Ln, bias=1.0).then_inc(gate, 1)

            def attn(b, par, p1, p2):
                act.wait_ge(xT_ps, b + 1)
                if p2:
                    act.wait_ge(s_ps, b * 2 - 2)
                nc.scalar.activation(xT[:, par, :], bank[7][:, 0:S], ACT.Copy).then_inc(xT_sb, 1)
                if p2:
                    act.wait_ge(o_ps, b - 1)
                for r in range(4):
                    act.wait_ge(g_ps, b * 4 + r + 1)
                    nc.scalar.activation(gT[:, par, 2 * r:2 * r + 2, :],
                                         bank[4 + r % 2][:, :].rearrange("p (h t) -> p h t", h=2), ACT.Copy).then_inc(g_sb, 1)

                def decay(c):
                    act.wait_ge(ax_ps, b * 2 + c + 1)
                    if p1:
                        act.wait_ge(p_sb, b * 2 + c - 1)
                    for k in range(2):
                        ins = nc.scalar.activation(dd[:, c, 4 * k:4 * k + 4, :],
                                                   bank[2 + k][:, :].rearrange("p (h t) -> p h t", h=4), ACT.Exp)
                    ins.then_inc(d_sb, 1)

                decay(0)
                act.wait_ge(we_ps, b + 1)
                if p1:
                    act.wait_ge(vw_sb, b)
                    act.wait_ge(oT_sb, b)
                nc.scalar.activation(wv[:], bank[7][:, 256:256 + H], ACT.Exp)
                nc.scalar.activation(el[:], bank[7][:, 0:256].rearrange("p (g t) -> p g t", g=G2), ACT.Exp).then_inc(we_sb, 1)
                act.wait_ge(og_ps, b + 1)
                nc.scalar.activation(ogt[:], bank[6][:, :].rearrange("p (g t) -> p g t", g=G2), ACT.Tanh, scale=0.5)\
                    .then_inc(og_sb, 1)
                decay(1)
                act.wait_ge(st_ps, b + 1)
                if p1:
                    act.wait_ge(o_ps, b)
                nc.scalar.activation(st[:], bank[7][:, 0:H * DV], ACT.Copy).then_inc(st_sb, 1)

            batches(act, attn)

            def exps(i, par, g):
                n = i * 4 + g - 1
                if not (isinstance(n, int) and n < 1):
                    act.wait_ge(pv_ps, n)
                for h_ in range(2):
                    act.wait_ge(sc_ps, i * 8 + 2 * g + h_ + 1)
                    for q in (2 * h_, 2 * h_ + 1):
                        ins = nc.scalar.activation(ee[:, g % 2, q], bank[q][:, :].rearrange("p (c t) -> p c t", c=C),
                                                   ACT.Exp, scale=1.0 / (STEPS * STEPS * float(HD) ** 0.5))
                    ins.then_inc(e_sb, 1)

            def step(i, par):
                ahead, core, behind = parts(i)
                aa, cc = i + 1, i - 1
                if core:
                    exps(i, par, 0)
                if ahead:
                    act.wait_ge(q8T_ps, aa + 1)
                    if not (isinstance(i, int) and i < 0):
                        act.wait_ge(f_ps, aa)
                    nc.scalar.activation(q8T[:], bank[6][:, 0:P].bitcast(BF16), ACT.Copy).then_inc(q8T_sb, 1)
                if core:
                    exps(i, par, 1)
                if ahead:
                    act.wait_ge(x2T_ps, aa + 1)
                    if not (isinstance(i, int) and i < 0):
                        act.wait_ge(vv_ps, aa)
                    nc.scalar.activation(x2T[:], bank[7][:, 0:S], ACT.Copy).then_inc(x2T_sb, 1)
                if core:
                    exps(i, par, 2)
                if behind:
                    act.wait_ge(x3T_ps, cc + 1)
                    if not (isinstance(i, int) and i < 2):
                        act.wait_ge(up_ps, cc * NBLK)
                    nc.scalar.activation(x3T[:], bank[6][:, 0:S], ACT.Copy).then_inc(x3T_sb, 1)
                if ahead:
                    act.wait_ge(qk_ps, aa + 1)
                    if not (isinstance(i, int) and i < 0):
                        act.wait_ge(qkv_sb, aa)
                    for n in range(2):
                        ins = nc.scalar.activation(cur[:, n, :], bank[7][:, n * S:(n + 1) * S], ACT.Identity, bias=cols[:, n:n + 1])
                    ins.then_inc(qk_sb, 1)
                if behind:
                    act.wait_ge(lg_rd, cc + 1)
                    nc.scalar.activation(lg[:, 1], lg[:, 0], ACT.Exp).then_inc(lge, 1)
                if core:
                    exps(i, par, 3)
                if behind:
                    def tanh(k, bk):
                        act.wait_ge(up_ps, cc * NBLK + k + 1)
                        act.wait_ge(hb_sb, cc * NBLK + max(k - 1, 0))
                        nc.scalar.activation(th[:, k % 2], bank[bk][:, 0:S], ACT.Tanh, scale=0.5).then_inc(th_sb, 1)

                    def spread(k, bk):
                        act.wait_ge(cB_ps, cc * 2 + k + 1)
                        act.wait_ge(hc_sb, cc * (NBLK - 1))
                        nc.scalar.activation(cB[:, 2 * k:2 * k + 2], bank[bk][:, :].rearrange("p (n t) -> p n t", n=2),
                                             ACT.Copy).then_inc(cB_sb, 1)

                    tanh(0, 7)
                    act.wait_ge(cT_ps, cc + 1)
                    if not (isinstance(i, int) and i < 2):
                        act.wait_ge(cB_ps, cc * 2)
                    nc.scalar.activation(cT[:], bank[6][0:NE, 0:S], ACT.Copy).then_inc(cT_sb, 1)
                    spread(0, 7)
                    tanh(1, 6)
                    tanh(2, 7)
                    spread(1, 6)
                    tanh(3, 7)
                    tanh(4, 6)

            steps(act, step)

        @block.gpsimd
        def _(gp):
            nc.gpsimd.memset(half[:], -0.5).then_inc(half_sb, 1)
            nc.gpsimd.memset(va[:], 0.0).then_inc(half_sb, 1)
            gp.wait_ge(half_sb, 2)
            nc.gpsimd.memset(va[:, :, :, :, HD:HD + 1], float(STEPS)).then_inc(half_sb, 1)
            gp.wait_ge(half_sb, 3)
            gp.wait_ge(wmax, 1)
            nc.gpsimd.partition_all_reduce(sw[:, 1:2], sw[:, 0:1], P, RMAX).then_inc(wmax_all, 1)
            gp.wait_ge(la_sb, 1)

            def rsqrt(var, tmp, dst, chain, done):
                chain(nc.gpsimd.tensor_scalar(tmp, var, EPS, None, ALU.add))
                nc.gpsimd.tensor_tensor(dst, tmp, half[:, 0:C], ALU.pow).then_inc(done, 1)

            def norm1(b):
                wait_apart(gp, mv_sb, b + 1, (half_sb, 3))
                ch = Chain(gp, c_pow, b, 1)
                rsqrt(mv[:, :, 1], rstd[:, 0], rstd[:, 1], ch, rstd_sb)
                ch.end()

            def attn(b, par, p1, p2):
                if p1:
                    gp.wait_ge(we_ps, b)
                nc.gpsimd.tensor_copy(laB[:].rearrange("p (h v) -> p h v", h=H),
                                      la[:, bass.ds(b * 2 + 1, 1), :].rearrange("p a h -> p (a h)").unsqueeze(2)
                                      .to_broadcast([P, H, DV])).then_inc(laB_sb, 1)
                for c in range(C):
                    if p1:
                        wait_apart(gp, ax_ps, b * 2 + c - 1, (half_sb, 3))
                    nc.gpsimd.tensor_tensor(rr[:, c], upto.unsqueeze(1).to_broadcast([P, H, P]),
                                            la[:, bass.ds(b * 2 + c, 1), :].rearrange("p a h -> p (a h)").unsqueeze(2)
                                            .to_broadcast([P, H, P]), ALU.mult).then_inc(r_sb, 1)
                if p1:
                    norm1(b - 1)

                def mask(c):
                    gp.wait_ge(d_sb, b * 2 + c + 1)
                    nc.gpsimd.tensor_tensor(dd[:, c], dd[:, c], upto.unsqueeze(1).to_broadcast([P, H, P]), ALU.mult)\
                        .then_inc(dm_sb, 1)

                mask(0)
                gp.wait_ge(we_sb, b + 1)
                gp.wait_ge(v_sb, b + 1)
                if p1:
                    gp.wait_ge(st_ps, b)
                nc.gpsimd.tensor_tensor(vw[:].rearrange("p (h v) -> p h v", h=H),
                                        vs[:, par, 0, :].rearrange("p (h v) -> p h v", h=H),
                                        wv[:].unsqueeze(2).to_broadcast([P, H, DV]), ALU.mult).then_inc(vw_sb, 1)
                mask(1)

            batches(gp, attn)
            norm1(B - 1)
            gp.wait_ge(xmax, 1)
            nc.gpsimd.partition_all_reduce(sx[:, 1:2], sx[:, 0:1], P, RMAX).then_inc(xmax_all, 1)

            def step(i, par):
                ahead, core, behind = parts(i)
                aa, cc = i + 1, i - 1
                if ahead:
                    wait_apart(gp, amv_sb, aa + 1, (half_sb, 3))
                    ch = Chain(gp, k_pa, aa, 1)
                    rsqrt(amv[:, :, 1], ars[:, 0], ars[:, 1], ch, ars_sb)
                if behind:
                    wait_apart(gp, cmv_sb, cc + 1, (half_sb, 3))
                    ch = Chain(gp, k_pc, cc, 1)
                    rsqrt(cmv[:, :, 1], crs[:, 0], crs[:, 1], ch, crs_sb)
                    for k in range(1, NBLK):
                        gp.wait_ge(hb_sb, cc * NBLK + k + 1)
                        gp.wait_ge(cB_sb, cc * 2 + (k - 1) // 2 + 1)
                        if not (isinstance(cc, int) and cc < 1):
                            gp.wait_ge(dn_ps, cc)
                        nc.gpsimd.tensor_tensor(hc[:, k], hb[:, k], cB[:, k - 1], ALU.mult).then_inc(hc_sb, 1)
                    wait_apart(gp, dmv_sb, cc + 1, (half_sb, 3))
                    ch = Chain(gp, k_pd, cc, 1)
                    rsqrt(dmv[:, :, 1], drs[:, 0], drs[:, 1], ch, drs_sb)

            steps(gp, step)

        @block.vector
        def _(dve):
            V = nc.vector

            def quantize(ch, src, scale, y, e, m, t, dst):
                ch(V.tensor_scalar(y, src, scale, FP8_MAX, ALU.mult, ALU.min))
                ch(V.tensor_scalar(e.bitcast(U32), y.bitcast(U32), 0x7F800000, None, ALU.bitwise_and))
                ch(V.tensor_scalar(m, e, 2.0 ** -6, 1.5 * 2.0 ** 20, ALU.max, ALU.mult))
                ch(V.scalar_tensor_tensor(t, y, -FP8_MAX, m, ALU.max, ALU.add))
                return V.tensor_tensor(dst, t, m, ALU.subtract)

            def scale_of(ch, s):
                ch(V.tensor_scalar(s[:, 0:1], s[:, 1:2], 1e-12, None, ALU.max))
                ch(V.reciprocal(s[:, 1:2], s[:, 0:1]))
                ch(V.tensor_scalar(s[:, 2:3], s[:, 1:2], FP8_MAX, FP8_MAX, ALU.mult, ALU.min))
                ch(V.reciprocal(s[:, 3:4], s[:, 2:3]))

            one = Chain(dve, dve_one, 0, 16)
            dve.wait_ge(c_in, 48)

            def gate_pass(b, par, p1, p2):
                dve.wait_ge(z_ps, b + 1)
                V.tensor_tensor(lz[:, 0, bass.ds(b * 2, 2), :], bank[6 + par][:, 0:C * H].rearrange("p (c h) -> p c h", c=C),
                                bg_r.unsqueeze(1).to_broadcast([P, C, H]), ALU.add).then_inc(z_sb, 1)

            batches(dve, gate_pass)
            V.tensor_copy(identb[:], ident).then_inc(setup, 1)
            dve.wait_ge(w_in, 16 * 5)
            one(V.tensor_scalar(wo[:], wo[:], 0.5, None, ALU.mult))
            V.tensor_reduce(sw[:, 0:1], ffw[:], AX.X, ALU.max, apply_absolute_value=True).then_inc(wmax, 1)
            dve.wait_ge(gate, 1)
            V.scalar_tensor_tensor(la[:], lz[:, 3], -1.0, lz[:, 1], ALU.mult, ALU.subtract).then_inc(la_sb, 1)
            dve.wait_ge(wmax_all, 1)
            scale_of(one, sw)
            ins = quantize(one, ffw[:], sw[:, 2:3], wq_t[:, 0], wq_t[:, 1], wq_t[:, 2], wq_t[:, 3], wfT[:])
            ins.then_inc(setup, 1)
            dve.wait_ge(w2_in, 16 * 5)
            V.tensor_scalar(wdn[:, 0, :], wdn[:, 0, :], 0.5, None, ALU.mult).then_inc(wf_sb, 1)

            def norm(ch, r, bnb, mvb, mv_done, rs_, rs_ready, index, write):
                for c in range(C):
                    ins = V.bn_stats(bnb[:, c, :], r[:, c, :])
                ch(ins, met=(c_in, 48))
                for c in range(C):
                    ins = V.bn_aggr(mvb[:, c, :], bnb[:, c, :])
                ins.then_inc(mv_done, 1)
                dve.wait_ge(rs_ready, index + 1)
                for c in range(C):
                    ins = write(c, mvb[:, c, 0:1], rs_[:, 1, c:c + 1])
                return ins

            def tail(b, par):
                dve.wait_ge(o_ps, b + 1)
                dve.wait_ge(we_sb, b + 1)
                dve.wait_ge(og_sb, b + 1)
                ch = Chain(dve, c_oT, b, 2)
                intra = bank[6][:, :].rearrange("p (c g t) -> p c g t", c=C, g=G2)
                ch(V.tensor_tensor(t0[:], bank[7][:, 0:256].rearrange("p (g t) -> p g t", g=G2), el[:], ALU.mult))
                ch(V.tensor_tensor(t1[:], t0[:], intra[:, 1], ALU.add))
                V.scalar_tensor_tensor(oT[:, :, 0:P], ogt[:, :, 0:P], 1.0, intra[:, 0], ALU.add, ALU.mult)
                V.scalar_tensor_tensor(oT[:, :, P:S], ogt[:, :, P:S], 1.0, t1[:], ALU.add, ALU.mult).then_inc(oT_sb, 1)
                ch.end()
                dve.wait_ge(y_ps, b + 1)
                ch = Chain(dve, c_ln, b, 2)
                V.tensor_tensor(rs[:], bank[7][:, 256:512].rearrange("p (c d) -> p c d", c=C), xs[:, par], ALU.add)\
                    .then_inc(r1_sb, 1)
                dve.wait_ge(r1_sb, b + 1)
                xo = xa[:, bass.ds(b * 2, 2), :]
                ch(norm(ch, rs, bn, mv, mv_sb, rstd, rstd_sb, b,
                        lambda c, m, r: V.tensor_scalar(xa[:, bass.ds(b * 2 + c, 1), :], rs[:, c:c + 1, :], m, r,
                                                        ALU.subtract, ALU.mult)))
                V.tensor_reduce(amax[:, bass.ds(b, 1)], xo, AX.XY, ALU.max, apply_absolute_value=True)
                ch.end()

            def attn(b, par, p1, p2):
                dve.wait_ge(v_ps, b + 1)
                if p2:
                    dve.wait_ge(o_ps, b - 1)
                    dve.wait_ge(vw_sb, b - 1)
                V.tensor_copy(vs[:, par], bank[6][:, :].rearrange("p (c n) -> p c n", c=C)).then_inc(v_sb, 1)
                if p1:
                    tail(b - 1, 1 - par)
                for c in range(C):
                    dve.wait_ge(s_ps, b * 2 + c + 1)
                    dve.wait_ge(dm_sb, b * 2 + c + 1)
                    for k in range(2):
                        ins = V.tensor_tensor(pp[:, c, 4 * k:4 * k + 4, :], bank[k][:, :].rearrange("p (h t) -> p h t", h=4),
                                              dd[:, c, 4 * k:4 * k + 4, :], ALU.mult)
                    ins.then_inc(p_sb, 1)

            batches(dve, attn)
            tail(B - 1, (B - 1) % 2)

            one(V.tensor_scalar(amax[:, B:B + 1], amax[:, 0:1], 0.0, None, ALU.add))
            V.tensor_reduce(sx[:, 0:1], amax[:, 0:B], AX.X, ALU.max).then_inc(xmax, 1)
            dve.wait_ge(xmax_all, 1)
            scale_of(one, sx)
            one(V.tensor_tensor(scl[:], sx[:, 3:4], sw[:, 3:4], ALU.mult))
            dve.wait_ge(half_sb, 3)

            thr = lif_thresholds()

            def quant(aa):
                ch = Chain(dve, k_q, aa, 4)
                quantize(ch, xa[:, bass.ds(aa * 2, 2), :], sx[:, 2:3], qy[:], qe[:], qm[:], qt[:], q8[:]).then_inc(q8_sb, 1)
                ch.end()

            def ffn(aa):
                dve.wait_ge(f_ps, aa + 1)
                ch = Chain(dve, k_a, aa, 3)
                V.scalar_tensor_tensor(fb[:], bank[7][:, 0:S].rearrange("p (c d) -> p c d", c=C), scl[:, 0:1],
                                       fb_r.unsqueeze(1).to_broadcast([P, C, D]), ALU.mult, ALU.add).then_inc(f_rd, 1)
                dve.wait_ge(f_rd, aa + 1)
                ch(V.tensor_tensor(qy[:], fb[:], xa[:, bass.ds(aa * 2, 2), :], ALU.add))
                if not (isinstance(aa, int) and aa < 1):
                    dve.wait_ge(x2T_ps, aa)
                ch(norm(ch, qy, abn, amv, amv_sb, ars, ars_sb, aa,
                        lambda c, m, r: V.tensor_scalar(arA[:, c, :], qy[:, c, :], m, r, ALU.subtract, ALU.mult)))
                V.tensor_tensor(xa[:, bass.ds(aa * 2, 2), :], arA[:], ob_r.unsqueeze(1).to_broadcast([P, C, D]), ALU.add)\
                    .then_inc(x2_sb, 1)
                ch.end()

            def take_v(aa):
                dve.wait_ge(vv_ps, aa + 1)
                V.tensor_tensor(cur[:, 2, :].rearrange("p (c d) -> p c d", c=C),
                                bank[6][:, 0:S].rearrange("p (c d) -> p c d", c=C),
                                vb_r.unsqueeze(1).to_broadcast([P, C, D]), ALU.add).then_inc(vv_sb, 1)

            def lif(aa, par):
                dve.wait_ge(vv_sb, aa + 1)
                dve.wait_ge(qk_sb, aa + 1)
                ch = Chain(dve, k_lif, aa, 4)
                ch(V.tensor_scalar(n1[:], cur[:], thr[0], None, ALU.is_gt))
                ch(V.scalar_tensor_tensor(n2[:], cur[:], thr[1], n1[:], ALU.is_gt, ALU.add))
                ch(V.scalar_tensor_tensor(n1[:], cur[:], thr[2], n2[:], ALU.is_gt, ALU.add))
                if not (isinstance(aa, int) and aa < 2):
                    dve.wait_ge(pv_ps, aa * 4 - 4)
                V.scalar_tensor_tensor(qn[:, par], cur[:, 0], thr[3], n1[:, 0], ALU.is_gt, ALU.add)
                ch(V.scalar_tensor_tensor(kn[:], cur[:, 1], thr[3], n1[:, 1], ALU.is_gt, ALU.add))
                V.scalar_tensor_tensor(va[:, par, :, :, 0:HD], cur[:, 2].rearrange("p (c h d) -> p c h d", c=C, h=NH), thr[3],
                                       n1[:, 2].rearrange("p (c h d) -> p c h d", c=C, h=NH), ALU.is_gt, ALU.add)
                for g in range(QG):
                    ins = V.tensor_scalar(km[:, par, g], kn[:], gmask[:, g:g + 1], None, ALU.mult)
                ins.then_inc(qkv_sb, 1)
                ch.end()

            def turn(i, pair):
                dve.wait_ge(pv_ps, i * 4 + 2 * pair + 2)
                if not (isinstance(i, int) and i < 1):
                    dve.wait_ge(aT_sb, i)
                V.transpose(tq[:, 2 * pair:2 * pair + 2].rearrange("p g b r -> p (g b r)"), bank[4 + pair][:, :]).then_inc(tr_sb, 1)

            def attend(cc):
                dve.wait_ge(tr_sb, cc * 2 + 2)
                ch = Chain(dve, k_n, cc, 2)
                ch(V.reciprocal(rd[:], tq[:, :, :, HD]))
                ch(V.tensor_tensor(on[:].rearrange("p b g d -> p g b d"), tq[:, :, :, 0:HD],
                                   rd[:].unsqueeze(3).to_broadcast([P, QG, C * 4, HD]), ALU.mult))
                if not (isinstance(cc, int) and cc < 1):
                    dve.wait_ge(w_ps, cc)
                V.transpose(aT[:], on[:].rearrange("p b g d -> p (b g d)")).then_inc(aT_sb, 1)
                ch.end()

            def project(cc):
                dve.wait_ge(w_ps, cc + 1)
                ch = Chain(dve, k_c, cc, 2)
                V.tensor_tensor(rs[:], bank[6][:, 0:S].rearrange("p (c d) -> p c d", c=C), xa[:, bass.ds(cc * 2, 2), :], ALU.add)\
                    .then_inc(w_rd, 1)
                dve.wait_ge(w_rd, cc + 1)
                if not (isinstance(cc, int) and cc < 1):
                    dve.wait_ge(x3T_ps, cc)
                ch(norm(ch, rs, cbn, cmv, cmv_sb, crs, crs_sb, cc,
                        lambda c, m, r: V.tensor_scalar(crA[:, c, :], rs[:, c, :], m, r, ALU.subtract, ALU.mult)))
                V.tensor_copy(crA[:, 0, 0:0 + 1], crA[:, 0, 0:1]).then_inc(x3_sb, 1)
                ch.end()

            def logits(cc):
                dve.wait_ge(lg_ps, cc + 1)
                ch = Chain(dve, k_top, cc, 12)
                lp = bank[6][:, 256:256 + C * NE].rearrange("p (c e) -> p c e", c=C)
                ch(V.tensor_reduce(ls[:, 0], lp, AX.X, ALU.max))
                V.tensor_tensor(lg[:, 0], lp, ls[:, 0].unsqueeze(2).to_broadcast([P, C, NE]), ALU.subtract).then_inc(lg_rd, 1)
                dve.wait_ge(lg_rd, cc + 1)
                return ch

            def top2(cc, ch):
                bc = lambda t: t.unsqueeze(2).to_broadcast([P, C, NE])
                rv = rev.unsqueeze(1).to_broadcast([P, C, NE])
                d, e, k1, s1, d2, k2, s2, es = (lg[:, n] for n in range(8))
                ch(V.scalar_tensor_tensor(k1, d, 0.0, rv, ALU.is_equal, ALU.mult))
                ch(V.tensor_reduce(ls[:, 1], k1, AX.X, ALU.max))
                ch(V.tensor_tensor(s1, k1, bc(ls[:, 1]), ALU.is_equal))
                ch(V.scalar_tensor_tensor(d2, s1, -1e30, d, ALU.mult, ALU.add))
                ch(V.tensor_reduce(ls[:, 2], d2, AX.X, ALU.max))
                ch(V.tensor_tensor(s2, d2, bc(ls[:, 2]), ALU.is_equal))
                ch(V.tensor_tensor(k2, s2, rv, ALU.mult))
                ch(V.tensor_reduce(ls[:, 3], k2, AX.X, ALU.max))
                ch(V.tensor_tensor(s2, k2, bc(ls[:, 3]), ALU.is_equal))
                ch(V.tensor_tensor(k1, s1, s2, ALU.add))
                dve.wait_ge(lge, cc + 1)
                V.tensor_reduce(ls[:, 4], e, AX.X, ALU.add)
                ch(V.tensor_tensor(es, e, k1, ALU.mult))
                ch.end()
                ch = Chain(dve, k_up, cc, 3)
                ch(V.tensor_reduce(ls[:, 5], es, AX.X, ALU.add))
                ch(V.scalar_tensor_tensor(ls[:, 6], ls[:, 4], 1e-9, ls[:, 5], ALU.mult, ALU.add))
                ch(V.reciprocal(ls[:, 7], ls[:, 6]))
                if not (isinstance(cc, int) and cc < 1):
                    dve.wait_ge(cT_ps, cc)
                V.scalar_tensor_tensor(comb[:], es, 0.5, bc(ls[:, 7]), ALU.mult, ALU.mult).then_inc(cmb_sb, 1)
                ch.end()

            def hidden(cc, k, bk):
                dve.wait_ge(th_sb, cc * NBLK + k + 1)
                V.scalar_tensor_tensor(ha[:, k % 2], th[:, k % 2], 1.0, bank[bk][:, 0:S], ALU.add, ALU.mult)\
                    .then_inc(k_d, 1)
                dve.wait_ge(k_d, cc * NBLK + k + 1)
                if k == 0:
                    dve.wait_ge(hc_sb, cc * (NBLK - 1))
                    dve.wait_ge(dn_ps, cc)
                V.tensor_tensor(hb[:, k], ha[:, k % 2], bank[bk][:, S:2 * S], ALU.mult).then_inc(hb_sb, 1)

            def finish(cc, par):
                dve.wait_ge(dn_ps, cc + 1)
                ch = Chain(dve, k_fin, cc, 1)
                V.tensor_tensor(drA[:], bank[7][:, 0:S].rearrange("p (c d) -> p c d", c=C), crA[:], ALU.add).then_inc(dn_rd, 1)
                dve.wait_ge(dn_rd, cc + 1)
                dve.wait_ge(out_done, cc * 16)
                norm(ch, drA, dbn, dmv, dmv_sb, drs, drs_sb, cc,
                     lambda c, m, r: V.tensor_scalar(yo[:, par, c, :], drA[:, c, :], m, r, ALU.subtract, ALU.mult))\
                    .then_inc(yo_sb, 1)
                ch.end()

            def step(i, par):
                ahead, core, behind = parts(i)
                aa, cc = i + 1, i - 1
                if ahead:
                    quant(aa)
                if behind:
                    turn(cc, 1)
                    attend(cc)
                if ahead:
                    ffn(aa)
                if behind:
                    project(cc)
                if core:
                    turn(i, 0)
                if behind:
                    top = logits(cc)
                if ahead:
                    take_v(aa)
                if behind:
                    top2(cc, top)
                    hidden(cc, 0, 7)
                    hidden(cc, 1, 6)
                if ahead:
                    lif(aa, 1 - par)
                if behind:
                    hidden(cc, 2, 7)
                    hidden(cc, 3, 7)
                    hidden(cc, 4, 6)
                    finish(cc, 1 - par)

            steps(dve, step)


def kernel(**inputs):
    import numpy as np
    import concourse.bacc as bacc
    from concourse.bass_utils import run_bass_kernel_spmd

    w = {k: np.asarray(v) for k, v in inputs.items()}
    heads = lambda m: m.reshape(D, H, P).transpose(2, 1, 0)
    wide = lambda m: m.transpose(1, 0, 2).reshape(D, -1)
    blocks = lambda m: m.reshape(-1, P, D).transpose(1, 0, 2)
    gates = np.concatenate([wide(w["L1_ffn_wg_s"]), wide(w["L1_ffn_wg_r"])], 1).reshape(D, NBLK, 1, P)
    ups = np.concatenate([wide(w["L1_ffn_wu_s"]), wide(w["L1_ffn_wu_r"])], 1).reshape(D, NBLK, 1, P)
    p = np.arange(P)
    esel = np.zeros((P, NBLK - 1, EPB, ME), np.float32)
    for e in range(NE):
        esel[e, e // EPB, e % EPB, :] = 1.0
    cst = np.concatenate([
        np.eye(P), p[:, None] > p[None, :], p[:, None] <= p[None, :],
        (p[:, None] // HD) % QG == np.arange(QG)[None, :],
        np.broadcast_to(np.arange(NE, 0, -1)[None, :], (P, NE)),
        esel.reshape(P, -1)], 1).astype(np.float32)
    arrays = {
        "x": w["L0_attn_x"],
        "cst": cst,
        "rows": np.broadcast_to(np.concatenate([w["L0_attn_bg"], w["L0_ffn_bias"], w["L1_attn_v_b"], w["L1_attn_o_b"]])[None, :],
                                (P, H + 3 * D)),
        "cols": np.stack([w["L1_attn_q_b"], w["L1_attn_k_b"]], 1),
        "wqT": heads(w["L0_attn_Wq"]), "wkT": heads(w["L0_attn_Wk"]),
        "wvg": np.concatenate([w["L0_attn_Wv"], w["L0_attn_Wg"]], 1),
        "wog": w["L0_attn_Wog"], "wo": blocks(w["L0_attn_Wo"]),
        "ffw": w["L0_ffn_weight"].T,
        "wqkvo": np.stack([w["L1_attn_q_w"], w["L1_attn_k_w"], w["L1_attn_v_w"], w["L1_attn_o_w"]], 1),
        "wr": w["L1_ffn_router_w"],
        "wup": np.concatenate([gates, ups], 2),
        "wdn": np.concatenate([blocks(w["L1_ffn_wd_s"].reshape(-1, D)), blocks(w["L1_ffn_wd_r"].reshape(-1, D))], 1),
    }
    arrays = {k: np.ascontiguousarray(v) for k, v in arrays.items()}
    nc = bacc.Bacc("TRN2", target_bir_lowering=False, num_devices=1)
    aps = {k: nc.dram_tensor(k + "_dram", v.shape, mybir.dt.from_np(v.dtype), kind="ExternalInput").ap()
           for k, v in arrays.items()}
    out = nc.dram_tensor("out_dram", (B, S, D), F32, kind="ExternalOutput").ap()
    fused_layers(nc, aps, out)
    r = run_bass_kernel_spmd(nc, [{k + "_dram": v for k, v in arrays.items()}], core_ids=[0])
    return r.results[0]["out_dram"]
```

```python
from contextlib import ExitStack

import concourse.bass as bass
from concourse import mybir

ALU = mybir.AluOpType
ACT = mybir.ActivationFunctionType
AX = mybir.AxisListType
F32 = mybir.dt.float32
BF16 = mybir.dt.bfloat16
U32 = mybir.dt.uint32
RMAX = bass.bass_isa.ReduceOp.max

P = 128
B, S, D = 8, 256, 128
C = S // P
H, DV = 8, 32
GATE_NORM = 16.0
G2 = H * DV // P
HPB = P // DV
NH, HD = 16, 8
QG = 4
NE, ME = 16, 32
NBLK = 5
EPB = P // ME
EPS = 1e-5
FP8_MAX = 448.0
STEPS = 4


def lif_thresholds():
    import numpy as np
    beta, thr = np.float32(0.95), np.float32(1.0)

    def spikes(cur):
        mem, n = np.float32(0.0), 0
        for _ in range(STEPS):
            reset = thr if mem > thr else np.float32(0.0)
            mem = np.float32(np.float32(np.float32(beta * mem) + cur) - reset)
            n += int(mem > thr)
        return n

    steps = []
    for want in range(1, STEPS + 1):
        lo, hi = np.float32(0.125), np.float32(2.0)
        while np.nextafter(lo, hi) < hi:
            mid = np.float32((np.float64(lo) + np.float64(hi)) / 2)
            if spikes(mid) >= want:
                hi = mid
            else:
                lo = mid
        steps.append(float(lo))
    return steps


def wait_apart(eng, semaphore, value, met):
    value = value if isinstance(value, int) else eng.to_reg(value)
    eng.wait_ge(*met)
    eng.wait_ge(semaphore, value)


class Chain:

    def __init__(self, eng, sem, index, per):
        self.eng, self.sem, self.index, self.per, self.k = eng, sem, index, per, 0

    def link(self, ins):
        self.k += 1
        ins.then_inc(self.sem, 1)

    def meet(self):
        self.eng.wait_ge(self.sem, self.index * self.per + self.k)

    def __call__(self, ins, met=None):
        self.link(ins)
        value = self.index * self.per + self.k
        if met is None:
            self.eng.wait_ge(self.sem, value)
        else:
            wait_apart(self.eng, self.sem, value, met)

    def end(self):
        assert self.k == self.per, f"{self.k} links, {self.per} counted on"


def fused_layers(nc, a, out):
    x_dram = a["x"].rearrange("b (c p) d -> b p c d", p=P)
    out_dram = out.rearrange("b (c p) d -> b p c d", p=P)

    with ExitStack() as ctx:
        def sb(name, shape, dt=F32):
            return ctx.enter_context(nc.sbuf_tensor(name, shape, dt))

        def sem(name):
            return ctx.enter_context(nc.semaphore(name))

        wqT = sb("wqT", [P, H, P]); wkT = sb("wkT", [P, H, P])
        wvg = sb("wvg", [P, H * DV + H]); wog = sb("wog", [P, H * DV]); wo = sb("wo", [P, G2, D])
        rows = sb("rows", [P, H + 3 * D])
        cols = sb("cols", [P, 2])
        cst = sb("cst", [P, 3 * P + 4 + NE + H + (NBLK - 1) * P])
        ffw = sb("ffw", [P, D])
        wqkvo = sb("wqkvo", [P, 4, D])
        wr = sb("wr", [P, NE]); wup = sb("wup", [P, NBLK, 2, P]); wdn = sb("wdn", [P, NBLK, D])
        bg_r, fb_r = rows[:, 0:H], rows[:, H:H + D]
        vb_r, ob_r = rows[:, H + D:H + 2 * D], rows[:, H + 2 * D:H + 3 * D]
        ident, later, upto = cst[:, 0:P], cst[:, P:2 * P], cst[:, 2 * P:3 * P]
        gmask = cst[:, 3 * P:3 * P + 4]
        rev = cst[:, 3 * P + 4:3 * P + 4 + NE]
        head_of = cst[:, 3 * P + 4 + NE:3 * P + 4 + NE + H]
        esel = cst[0:3 * NE, 3 * P + 4 + NE + H:]
        identb = sb("identb", [P, P], BF16)
        shut = sb("shut", [P, P], BF16)
        eselb = sb("eselb", [3 * NE, (NBLK - 1) * P], BF16)
        amat = sb("amat", [P, H, P])
        wfT = sb("wfT", [P, D], BF16)
        half = sb("half", [P, 2])

        xa = sb("xa", [P, B * C, D])
        la = sb("la", [P, B * C, H])
        lz = sb("lz", [P, 4, B * C, H])
        cum = sb("cum", [P, 2, B * C, H])
        lp = sb("lp", [P, B * C, P], BF16)
        lpT = sb("lpT", [P, B * C, P], BF16); lnT = sb("lnT", [P, B * C, P], BF16)
        oneh = sb("oneh", [P, H, P], BF16)
        amax = sb("amax", [P, B + 8])
        sw = sb("sw", [P, 4]); sx = sb("sx", [P, 4]); scl = sb("scl", [P, 1])
        wq_t = sb("wq_t", [P, 2, D])
        q8 = sb("q8", [P, B * C, D], BF16)

        xs = sb("xs", [P, 2, C, D]); xT = sb("xT", [P, 2, S])
        gT = sb("gT", [P, 2, H, S]); vs = sb("vs", [P, 2, C, H * DV])
        dd = sb("dd", [P, C, H, P]); pp = sb("pp", [P, C, H, P])
        laB = sb("laB", [P, H * DV]); wv = sb("wv", [P, H]); vw = sb("vw", [P, H * DV])
        el = sb("el", [P, G2, P]); ogt = sb("ogt", [P, G2, S]); st = sb("st", [P, H * DV])
        t0 = sb("t0", [P, G2, P]); t1 = sb("t1", [P, G2, P]); oT = sb("oT", [P, G2, S])
        rs = sb("rs", [P, C, D]); bn = sb("bn", [P, C, 6]); mv = sb("mv", [P, C, 2]); rstd = sb("rstd", [P, 2, C])

        qy = sb("qy", [P, C, D]); q8T = sb("q8T", [P, S], BF16)
        fb = sb("fb", [P, C, D], BF16)
        x2T = sb("x2T", [P, S]); cur = sb("cur", [P, 3, S])
        n1 = sb("n1", [P, 3, S], BF16); n2 = sb("n2", [P, 3, S], BF16)
        qn = sb("qn", [P, 2, S], BF16); kn = sb("kn", [P, S], BF16); km = sb("km", [P, 2, QG, S], BF16)
        va = sb("va", [P, 2, C, NH, 32])
        ee = sb("ee", [P, 2, 4, C, S])
        tq = sb("tq", [P, QG, C * 4, 32]); rd = sb("rd", [P, QG, C * 4]); on = sb("on", [P, C * 4, QG, HD])
        aT = sb("aT", [P, S])
        arA = sb("arA", [P, C, D]); abn = sb("abn", [P, C, 6]); amv = sb("amv", [P, C, 2]); ars = sb("ars", [P, 2, C])
        crA = sb("crA", [P, 2, C, D]); cbn = sb("cbn", [P, C, 6]); cmv = sb("cmv", [P, C, 2]); crs = sb("crs", [P, 2, C])
        drA = sb("drA", [P, C, D]); dbn = sb("dbn", [P, C, 6]); dmv = sb("dmv", [P, C, 2]); drs = sb("drs", [P, 2, C])
        x3T = sb("x3T", [P, 2, S]); cr = sb("cr", [P, C, D])
        lg = sb("lg", [P, 8, C, NE]); ls = sb("ls", [P, 8, C]); comb = sb("comb", [P, C, NE])
        comb3 = sb("comb3", [P, C, 3, NE], BF16); crest = sb("crest", [P, C, NE])
        cT = sb("cT", [3 * NE, S], BF16); cB = sb("cB", [P, NBLK - 1, S])
        th = sb("th", [P, 2, S]); ha = sb("ha", [P, 2, S]); hb = sb("hb", [P, NBLK, S]); hc = sb("hc", [P, NBLK, S])
        yo = sb("yo", [P, 2, C, D])

        bank = [ctx.enter_context(nc.psum_tensor(f"bank{i}", [P, 512], F32)) for i in range(8)]
        two = [bank[0], bank[2]]

        w_in = sem("w_in"); w2_in = sem("w2_in"); c_in = sem("c_in")
        x0_in = [sem("x0_in_even"), sem("x0_in_odd")]; x0T_ps = sem("x0T_ps"); x0T_sb = sem("x0T_sb"); z_ps = sem("z_ps"); z_sb = sem("z_sb")
        am_ps = sem("am_ps"); am_sb = sem("am_sb"); gate = sem("gate"); la_sb = sem("la_sb"); setup = sem("setup")
        half_sb = sem("half_sb")
        wmax = sem("wmax"); wmax_all = sem("wmax_all"); wf_sb = sem("wf_sb")
        xmax = sem("xmax"); xmax_all = sem("xmax_all"); dve_one = sem("dve_one"); act_one = sem("act_one")
        x_in = [sem("x_in_even"), sem("x_in_odd")]
        xT_ps = sem("xT_ps"); v_ps = sem("v_ps"); g_ps = sem("g_ps"); ax_ps = sem("ax_ps"); we_ps = sem("we_ps")
        og_ps = sem("og_ps"); s_ps = sem("s_ps"); st_ps = sem("st_ps"); o_ps = sem("o_ps"); y_ps = sem("y_ps")
        xT_sb = sem("xT_sb"); g_sb = sem("g_sb"); d_sb = sem("d_sb"); we_sb = sem("we_sb"); og_sb = sem("og_sb")
        st_sb = sem("st_sb"); v_sb = sem("v_sb"); p_sb = sem("p_sb"); oT_sb = sem("oT_sb"); r1_sb = sem("r1_sb")
        laB_sb = sem("laB_sb"); cum_ps = sem("cum_ps"); lp_sb = sem("lp_sb"); lp_ps = sem("lp_ps"); lpT_sb = sem("lpT_sb"); vw_sb = sem("vw_sb")
        mv_sb = sem("mv_sb"); rstd_sb = sem("rstd_sb"); c_oT = sem("c_oT"); c_ln = sem("c_ln"); c_pow = sem("c_pow")

        q8_sb = sem("q8_sb"); q8T_ps = sem("q8T_ps"); q8T_sb = sem("q8T_sb"); f_ps = sem("f_ps"); f_rd = sem("f_rd")
        x2_sb = sem("x2_sb"); x2T_ps = sem("x2T_ps"); x2T_sb = sem("x2T_sb"); qk_ps = sem("qk_ps"); qk_sb = sem("qk_sb")
        vv_ps = sem("vv_ps"); vv_sb = sem("vv_sb"); qk_n = sem("qk_n"); km_sb = sem("km_sb"); va_sb = sem("va_sb"); xo_sb = sem("xo_sb")
        
        sc_ps = sem("sc_ps"); e_sb = sem("e_sb"); pv_ps = sem("pv_ps"); tr_sb = sem("tr_sb"); aT_sb = sem("aT_sb")
        w_ps = sem("w_ps"); w_rd = sem("w_rd"); x3_sb = sem("x3_sb"); x3T_ps = sem("x3T_ps"); x3T_sb = sem("x3T_sb")
        lg_ps = sem("lg_ps"); lg_rd = sem("lg_rd"); lge = sem("lge"); cmb_sb = sem("cmb_sb"); cT_ps = sem("cT_ps")
        cT_sb = sem("cT_sb"); cB_ps = sem("cB_ps"); cB_sb = sem("cB_sb"); up_ps = sem("up_ps"); th_sb = sem("th_sb")
        hb_sb = sem("hb_sb"); hc_sb = sem("hc_sb"); dn_ps = sem("dn_ps"); dn_rd = sem("dn_rd"); yo_sb = sem("yo_sb")
        out_done = sem("out_done"); yo_free = sem("yo_free")
        amv_sb = sem("amv_sb"); ars_sb = sem("ars_sb"); cmv_sb = sem("cmv_sb"); crs_sb = sem("crs_sb")
        dmv_sb = sem("dmv_sb"); drs_sb = sem("drs_sb")
        k_q = sem("k_q"); k_a = sem("k_a"); k_lif = sem("k_lif"); k_n = sem("k_n"); k_c = sem("k_c")
        k_top = sem("k_top"); k_up = sem("k_up"); k_d = sem("k_d")
        c3_sb = sem("c3_sb"); k_c3 = sem("k_c3"); k_pa = sem("k_pa"); k_pc = sem("k_pc"); k_pd = sem("k_pd"); k_fin = sem("k_fin")

        block = ctx.enter_context(nc.Block())

        def batches(eng, body):
            body(0, 0, False, False)
            body(1, 1, True, False)
            with eng.Fori(1, B // 2) as m:
                body(m * 2, 0, True, True)
                body(m * 2 + 1, 1, True, True)

        def steps(eng, body):
            body(-1, 1)
            body(0, 0)
            body(1, 1)
            with eng.Fori(1, B // 2 - 1) as m:
                body(m * 2, 0)
                body(m * 2 + 1, 1)
            for i in range(B - 2, B + 2):
                body(i, i % 2)

        def loads(b, par):
            return b * 8 - 8 * par + 16

        def parts(i):
            if isinstance(i, int):
                return tuple(0 <= n < B for n in (i + 1, i, i - 1, i - 2))
            return True, True, True, True

        @block.sync
        def _(sp):
            for dst, name in ((cst, "cst"), (rows, "rows"), (wvg, "wvg")):
                sp.dma_start(dst[:], a[name]).then_inc(c_in, 16)

            def first(b, par, p1, p2):
                if p2:
                    sp.wait_ge(x0T_ps, b - 1)
                sp.dma_start(xs[:, par], x_dram[bass.ds(b, 1)].rearrange("a p c d -> p (a c) d")).then_inc(x0_in[par], 16)

            batches(sp, first)
            for dst, name in ((wqkvo, "wqkvo"), (cols, "cols"), (wr, "wr"), (wup, "wup"), (wdn, "wdn")):
                sp.dma_start(dst[:], a[name]).then_inc(w2_in, 16)

            sp.wait_ge(x0T_ps, B)

            def load(b, par, p1, p2):
                if p2:
                    sp.wait_ge(r1_sb, b - 1)
                sp.dma_start(xs[:, par], x_dram[bass.ds(b, 1)].rearrange("a p c d -> p (a c) d")).then_inc(x_in[par], 16)

            batches(sp, load)

            def store(b, par, p1, p2):
                sp.wait_ge(yo_sb, b + 1)
                sp.dma_start(out_dram[bass.ds(b, 1)].rearrange("a p c d -> p (a c) d"), yo[:, par]).then_inc(out_done, 16)
                sp.wait_ge(out_done, b * 16 + 16)
                sp.sem_inc(yo_free, 1)

            sp.sem_inc(yo_free, 2)
            batches(sp, store)

        @block.tensor
        def _(pe):
            pe.wait_ge(c_in, 48)

            def z_of(b, par):
                pe.wait_ge(x0T_sb, b + 1)
                for c in range(C):
                    ins = nc.tensor.matmul(bank[6 + par][:, c * H:(c + 1) * H], xT[:, par, c * P:(c + 1) * P],
                                           wvg[:, H * DV:], start=True, stop=True)
                ins.then_inc(z_ps, 1)

            def gate_pass(b, par, p1, p2):
                pe.wait_ge(x0_in[par], loads(b, par))
                if p2:
                    pe.wait_ge(x0T_sb, b - 1)
                for c in range(C):
                    ins = nc.tensor.transpose(bank[4 + par][:, c * P:(c + 1) * P], xs[:, par, c, :], ident)
                ins.then_inc(x0T_ps, 1)
                if p1:
                    if p2:
                        pe.wait_ge(z_sb, b - 1)
                    z_of(b - 1, 1 - par)

            batches(pe, gate_pass)
            pe.wait_ge(z_sb, B - 2)
            z_of(B - 1, (B - 1) % 2)

            pe.wait_ge(w_in, 16 * 5)
            for h in range(H):
                ins = nc.tensor.matmul(bank[h // 4][:, (h % 4) * P:(h % 4 + 1) * P], wqT[:, h, :], wkT[:, h, :],
                                       start=True, stop=True)
            ins.then_inc(am_ps, 1)
            pe.wait_ge(am_sb, 1)
            pe.wait_ge(la_sb, 1)
            nc.tensor.matmul(bank[2][:, 0:B * C * H], upto, la[:].rearrange("p n h -> p (n h)"), start=True, stop=True)\
                .then_inc(cum_ps, 1)
            pe.wait_ge(setup, 2)
            pe.wait_ge(lp_sb, 1)

            def sums_by_row(b, par, p1, p2):
                if p2:
                    pe.wait_ge(lpT_sb, b - 1)
                bt = bank[par][:, 0:P].bitcast(BF16)
                for c in range(C):
                    ins = nc.tensor.transpose(bt[:, c * P:(c + 1) * P],
                                              lp[:, bass.ds(b * 2 + c, 1), :].rearrange("p a d -> p (a d)"), identb[:])
                ins.then_inc(lp_ps, 1)

            batches(pe, sums_by_row)
            pe.wait_ge(lpT_sb, B)

            def inside(b, par):
                pe.wait_ge(p_sb, b * 2 + 2)
                for c in range(C):
                    for g in range(G2):
                        for j in range(HPB):
                            h = g * HPB + j
                            ins = nc.tensor.matmul(bank[6][DV * j:DV * (j + 1), (c * G2 + g) * P:(c * G2 + g + 1) * P],
                                                   vs[:, par, c, h * DV:(h + 1) * DV], pp[:, c, h, :], start=True, stop=True)

            def across(b, par):
                pe.wait_ge(st_sb, b + 1)
                for g in range(G2):
                    for j in range(HPB):
                        h = g * HPB + j
                        ins = nc.tensor.matmul(bank[7][DV * j:DV * (j + 1), g * P:(g + 1) * P],
                                               st[:, h * DV:(h + 1) * DV], gT[:, par, h, P:S], start=True, stop=True)
                ins.then_inc(o_ps, 1)

            def out_proj(b):
                pe.wait_ge(oT_sb, b + 1)
                for c in range(C):
                    for g in range(G2):
                        ins = nc.tensor.matmul(bank[7][:, (2 + c) * P:(3 + c) * P], oT[:, g, c * P:(c + 1) * P], wo[:, g, :],
                                               start=(g == 0), stop=(g == G2 - 1))
                ins.then_inc(y_ps, 1)

            def attn(b, par, p1, p2):
                pe.wait_ge(x_in[par], loads(b, par))
                if p1:
                    pe.wait_ge(st_sb, b)
                for c in range(C):
                    ins = nc.tensor.transpose(bank[7][:, c * P:(c + 1) * P], xs[:, par, c, :], ident)
                ins.then_inc(xT_ps, 1)
                if p1:
                    pe.wait_ge(og_sb, b)
                    inside(b - 1, 1 - par)
                pe.wait_ge(xT_sb, b + 1)
                if p1:
                    across(b - 1, 1 - par)
                    pe.wait_ge(g_sb, b * 4)
                for c in range(C):
                    ins = nc.tensor.matmul(bank[4][:, c * H * DV:(c + 1) * H * DV], xT[:, par, c * P:(c + 1) * P],
                                           wvg[:, 0:H * DV], start=True, stop=True)
                ins.then_inc(v_ps, 1)
                for r in range(4):
                    if r == 1:
                        pe.wait_ge(v_sb, b + 1)
                    if r >= 2:
                        pe.wait_ge(g_sb, b * 4 + r - 1)
                    for k in range(2):
                        ins = nc.tensor.matmul(bank[5 - r % 2][:, k * S:(k + 1) * S], amat[:, 2 * r + k, :], xT[:, par, :],
                                               start=True, stop=True)
                    ins.then_inc(g_ps, 1)

                def decay(c):
                    if p1 or c:
                        pe.wait_ge(d_sb, b * 2 + c)
                    chunk = bass.ds(b * 2 + c, 1)
                    for h in range(H):
                        pair = bank[2 + h // 4][:, h % 4 * P:(h % 4 + 1) * P]
                        nc.tensor.matmul(pair, identb[:], shut[:], start=True, stop=False)
                        nc.tensor.matmul(pair, lnT[:, chunk, :].rearrange("p a s -> p (a s)"), oneh[:, h, :],
                                         start=False, stop=False)
                        ins = nc.tensor.matmul(pair, oneh[:, h, :], lpT[:, chunk, :].rearrange("p a t -> p (a t)"),
                                               start=False, stop=True)
                    ins.then_inc(ax_ps, 1)

                def scores(c):
                    if p1 or c:
                        pe.wait_ge(p_sb, b * 2 + c)
                    for k in range(2):
                        ins = nc.tensor.matmul(bank[k][:, :], xT[:, par, c * P:(c + 1) * P],
                                               gT[:, par, 4 * k:4 * k + 4, c * P:(c + 1) * P], start=True, stop=True)
                    ins.then_inc(s_ps, 1)

                decay(0)
                if p1:
                    out_proj(b - 1)
                for g in range(G2):
                    ins = nc.tensor.matmul(bank[6][:, g * S:(g + 1) * S], wog[:, g * P:(g + 1) * P], xT[:, par, :],
                                           start=True, stop=True)
                ins.then_inc(og_ps, 1)
                pe.wait_ge(g_sb, b * 4 + 4)
                scores(0)
                if p1:
                    pe.wait_ge(r1_sb, b)
                nc.tensor.matmul(bank[7][:, 256:256 + H], later, la[:, bass.ds(b * 2, 1), :].rearrange("p a h -> p (a h)"),
                                 start=True, stop=True)
                pe.wait_ge(laB_sb, b + 1)
                for g in range(G2):
                    ins = nc.tensor.matmul(bank[7][:, g * P:(g + 1) * P], laB[:, g * P:(g + 1) * P], upto,
                                           start=True, stop=True)
                ins.then_inc(we_ps, 1)
                decay(1)
                scores(1)
                pe.wait_ge(vw_sb, b + 1)
                pe.wait_ge(we_sb, b + 1)
                nc.tensor.matmul(bank[7][:, 0:H * DV], xs[:, par, 0, :], vw[:], start=True, stop=True).then_inc(st_ps, 1)

            batches(pe, attn)
            pe.wait_ge(og_sb, B)
            inside(B - 1, (B - 1) % 2)
            across(B - 1, (B - 1) % 2)
            out_proj(B - 1)

            pe.wait_ge(wf_sb, 1)
            pe.wait_ge(w2_in, 16 * 5)
            pe.wait_ge(r1_sb, B)

            def score_half(i, par, g, half_):
                for q in (2 * half_, 2 * half_ + 1):
                    for c in range(C):
                        ins = nc.tensor.matmul(bank[q][:, c * S:(c + 1) * S],
                                               km[32 * q:32 * q + 32, par, g, c * P:(c + 1) * P],
                                               qn[32 * q:32 * q + 32, par, :], start=True, stop=True)
                ins.then_inc(sc_ps, 1)

            def score(i, par, g):
                if g == 0:
                    pe.wait_ge(km_sb, i + 1)
                for half_ in range(2):
                    n = i * 8 + 2 * g + half_ - 1
                    if not (isinstance(n, int) and n < 1):
                        pe.wait_ge(e_sb, n)
                    score_half(i, par, g, half_)

            def values(i, par, g):
                if g == 0:
                    pe.wait_ge(va_sb, i + 1)
                pe.wait_ge(e_sb, i * 8 + 2 * g + 2)
                if g == 2:
                    pe.wait_ge(tr_sb, i * 2 + 1)
                if g == 0 and not (isinstance(i, int) and i < 1):
                    pe.wait_ge(tr_sb, i * 2)
                for c in range(C):
                    for q in range(4):
                        ins = nc.tensor.matmul(bank[4][32 * q:32 * q + 32, (g % 2) * S:(g % 2 + 1) * S],
                                               va[:, par, c, 4 * q + g, :], ee[:, g % 2, q, c, :],
                                               start=(c == 0), stop=(c == C - 1), skip_group_check=True)
                ins.then_inc(pv_ps, 1)

            def step(i, par):
                ahead, core, behind, experts = parts(i)
                aa, cc, mm = i + 1, i - 1, i - 2

                def up(k, bk):
                    for n in range(2):
                        ins = nc.tensor.matmul(bank[bk][:, n * S:(n + 1) * S], wup[:, k, n, :], x3T[:, par, :], start=True, stop=True)
                    ins.then_inc(up_ps, 1)

                def spread(k):
                    for n in range(2):
                        ins = nc.tensor.matmul(bank[6][:, n * S:(n + 1) * S], eselb[:, (2 * k + n) * P:(2 * k + n + 1) * P],
                                               cT[:], start=True, stop=True)
                    ins.then_inc(cB_ps, 1)

                if core:
                    score(i, par, 0)
                if experts:
                    up(0, 7)
                if behind:
                    values(cc, 1 - par, 3)
                if ahead:
                    if isinstance(i, int) and i < 0:
                        pe.wait_ge(q8_sb, 1)
                    else:
                        pe.wait_ge(q8_sb, 2)
                        pe.wait_ge(vv_sb, aa)
                    if behind and not (isinstance(i, int) and i < 2):
                        pe.wait_ge(lg_rd, cc)
                    bt = bank[5][:, 0:P].bitcast(BF16)
                    for c in range(C):
                        ins = nc.tensor.transpose(bt[:, c * P:(c + 1) * P],
                                                  q8[:, bass.ds(aa * 2 + c, 1), :].rearrange("p a d -> p (a d)"), identb[:])
                    ins.then_inc(q8T_ps, 1)
                if experts:
                    wait_apart(pe, dn_rd, mm + 1, (c_in, 48))
                    pe.wait_ge(c3_sb, mm + 1)
                    ct = bank[6][:, 0:P].bitcast(BF16)
                    for c in range(C):
                        ins = nc.tensor.transpose(ct[0:3 * NE, c * P:(c + 1) * P], comb3[:, c].rearrange("p k e -> p (k e)"), identb[:])
                    ins.then_inc(cT_ps, 1)
                if ahead:
                    pe.wait_ge(q8T_sb, aa + 1)
                    for c in range(C):
                        ins = nc.tensor.matmul(bank[5][:, c * P:(c + 1) * P], q8T[:, c * P:(c + 1) * P], wfT[:],
                                               start=True, stop=True)
                    ins.then_inc(f_ps, 1)
                if experts:
                    pe.wait_ge(cT_sb, mm + 1)
                    spread(0)
                    pe.wait_ge(hb_sb, mm * NBLK + 1)
                    up(1, 7)
                if core:
                    score(i, par, 1)
                    values(i, par, 0)
                if behind:
                    pe.wait_ge(aT_sb, cc + 1)
                    if ahead:
                        pe.wait_ge(f_rd, aa + 1)
                    else:
                        pe.wait_ge(vv_sb, B)
                        pe.wait_ge(lg_rd, cc)
                    for c in range(C):
                        ins = nc.tensor.matmul(bank[5][:, c * P:(c + 1) * P], aT[:, c * P:(c + 1) * P], wqkvo[:, 3, :],
                                               start=True, stop=True)
                    ins.then_inc(w_ps, 1)
                if experts:
                    pe.wait_ge(cB_sb, mm * 2 + 1)
                    spread(1)
                    pe.wait_ge(hb_sb, mm * NBLK + 2)
                    up(2, 7)
                if ahead:
                    pe.wait_ge(x2_sb, aa + 1)
                    if behind:
                        pe.wait_ge(w_rd, cc + 1)
                    for c in range(C):
                        ins = nc.tensor.transpose(bank[5][:, c * P:(c + 1) * P], arA[:, c, :], ident)
                    ins.then_inc(x2T_ps, 1)
                if core:
                    score(i, par, 2)
                if ahead:
                    pe.wait_ge(x2T_sb, aa + 1)
                    for n in range(2):
                        ins = nc.tensor.matmul(bank[5][:, n * S:(n + 1) * S], wqkvo[:, n, :], x2T[:], start=True, stop=True)
                    ins.then_inc(qk_ps, 1)
                if core:
                    values(i, par, 1)
                if experts:
                    pe.wait_ge(cB_sb, mm * 2 + 2)
                    up(3, 6)
                if ahead:
                    pe.wait_ge(qk_sb, aa + 1)
                    for c in range(C):
                        ins = nc.tensor.matmul(bank[5][:, c * P:(c + 1) * P], x2T[:, c * P:(c + 1) * P], wqkvo[:, 2, :],
                                               start=True, stop=True)
                    ins.then_inc(vv_ps, 1)
                if experts:
                    pe.wait_ge(hb_sb, mm * NBLK + 3)
                    up(4, 7)
                if behind:
                    pe.wait_ge(x3_sb, cc + 1)
                    if ahead:
                        pe.wait_ge(vv_sb, aa + 1)
                    for c in range(C):
                        ins = nc.tensor.transpose(bank[5][:, c * P:(c + 1) * P], crA[:, 1 - par, c, :], ident)
                    ins.then_inc(x3T_ps, 1)
                if core:
                    score(i, par, 3)
                if core:
                    values(i, par, 2)
                if behind:
                    pe.wait_ge(x3T_sb, cc + 1)
                    for c in range(C):
                        ins = nc.tensor.matmul(bank[5][:, c * NE:(c + 1) * NE], x3T[:, 1 - par, c * P:(c + 1) * P], wr[:],
                                               start=True, stop=True)
                    ins.then_inc(lg_ps, 1)
                if experts:
                    pe.wait_ge(hb_sb, mm * NBLK + 4)
                    for c in range(C):
                        for k in range(NBLK):
                            if c == 0 and k:
                                pe.wait_ge(hc_sb, mm * (NBLK - 1) + k)
                            src = hc if k else hb
                            ins = nc.tensor.matmul(bank[6][:, c * P:(c + 1) * P], src[:, k, c * P:(c + 1) * P], wdn[:, k, :],
                                                   start=(k == 0), stop=(k == NBLK - 1))
                    ins.then_inc(dn_ps, 1)

            steps(pe, step)

        @block.scalar
        def _(act):
            for dst, name in ((ffw, "ffw"), (wqT, "wqT"), (wkT, "wkT"), (wog, "wog"), (wo, "wo")):
                act.dma_start(dst[:], a[name]).then_inc(w_in, 16)

            def gate_pass(b, par, p1, p2):
                act.wait_ge(x0T_ps, b + 1)
                if p2:
                    act.wait_ge(z_ps, b - 1)
                nc.scalar.activation(xT[:, par, :], bank[4 + par][:, 0:S], ACT.Copy).then_inc(x0T_sb, 1)

            batches(act, gate_pass)
            act.wait_ge(am_ps, 1)
            for k in range(2):
                ins = nc.scalar.activation(amat[:, 4 * k:4 * k + 4, :], bank[k][:, :].rearrange("p (h d) -> p h d", h=4),
                                           ACT.Copy, scale=float(P) ** -0.5)
            ins.then_inc(am_sb, 1)
            act.wait_ge(z_sb, B)
            nc.scalar.activation(lz[:, 1], lz[:, 0], ACT.Abs, scale=1.0 / GATE_NORM).then_inc(act_one, 1)
            nc.scalar.activation(lz[:, 3], lz[:, 0], ACT.Relu, scale=-1.0 / GATE_NORM)
            act.wait_ge(act_one, 1)
            nc.scalar.activation(lz[:, 2], lz[:, 1], ACT.Exp, scale=-1.0).then_inc(act_one, 1)
            act.wait_ge(act_one, 2)
            nc.scalar.activation(lz[:, 1], lz[:, 2], ACT.Ln, bias=1.0).then_inc(gate, 1)

            def sums_by_row(b, par, p1, p2):
                act.wait_ge(lp_ps, b + 1)
                bt = bank[par][:, 0:P].bitcast(BF16).rearrange("p (c t) -> p c t", c=C)
                nc.scalar.activation(lpT[:, bass.ds(b * 2, 2), :], bt, ACT.Copy)
                nc.scalar.activation(lnT[:, bass.ds(b * 2, 2), :], bt, ACT.Copy, scale=-1.0).then_inc(lpT_sb, 1)

            batches(act, sums_by_row)

            def attn(b, par, p1, p2):
                act.wait_ge(xT_ps, b + 1)
                if p2:
                    act.wait_ge(s_ps, b * 2 - 2)
                nc.scalar.activation(xT[:, par, :], bank[7][:, 0:S], ACT.Copy).then_inc(xT_sb, 1)
                act.wait_ge(v_ps, b + 1)
                if p2:
                    act.wait_ge(o_ps, b - 1)
                    act.wait_ge(vw_sb, b - 1)
                nc.scalar.activation(vs[:, par], bank[4][:, :].rearrange("p (c n) -> p c n", c=C), ACT.Copy).then_inc(v_sb, 1)
                for r in range(4):
                    act.wait_ge(g_ps, b * 4 + r + 1)
                    nc.scalar.activation(gT[:, par, 2 * r:2 * r + 2, :],
                                         bank[5 - r % 2][:, :].rearrange("p (h t) -> p h t", h=2), ACT.Copy).then_inc(g_sb, 1)

                def decay(c):
                    act.wait_ge(ax_ps, b * 2 + c + 1)
                    if p1:
                        act.wait_ge(p_sb, b * 2 + c - 1)
                    for k in range(2):
                        ins = nc.scalar.activation(dd[:, c, 4 * k:4 * k + 4, :],
                                                   bank[2 + k][:, :].rearrange("p (h t) -> p h t", h=4), ACT.Exp)
                    ins.then_inc(d_sb, 1)

                decay(0)
                if p1:
                    act.wait_ge(vw_sb, b)
                    act.wait_ge(oT_sb, b)
                act.wait_ge(og_ps, b + 1)
                nc.scalar.activation(ogt[:], bank[6][:, :].rearrange("p (g t) -> p g t", g=G2), ACT.Tanh, scale=0.5)\
                    .then_inc(og_sb, 1)
                act.wait_ge(we_ps, b + 1)
                nc.scalar.activation(wv[:], bank[7][:, 256:256 + H], ACT.Exp)
                nc.scalar.activation(el[:], bank[7][:, 0:256].rearrange("p (g t) -> p g t", g=G2), ACT.Exp).then_inc(we_sb, 1)
                decay(1)
                act.wait_ge(st_ps, b + 1)
                if p1:
                    act.wait_ge(o_ps, b)
                nc.scalar.activation(st[:], bank[7][:, 0:H * DV], ACT.Copy).then_inc(st_sb, 1)

            batches(act, attn)

            def exps(i, par, g):
                n = i * 4 + g - 1
                if not (isinstance(n, int) and n < 1):
                    act.wait_ge(pv_ps, n)
                for h_ in range(2):
                    act.wait_ge(sc_ps, i * 8 + 2 * g + h_ + 1)
                    for q in (2 * h_, 2 * h_ + 1):
                        ins = nc.scalar.activation(ee[:, g % 2, q], bank[q][:, :].rearrange("p (c t) -> p c t", c=C),
                                                   ACT.Exp, scale=1.0 / (STEPS * STEPS * float(HD) ** 0.5))
                    ins.then_inc(e_sb, 1)

            def step(i, par):
                ahead, core, behind, experts = parts(i)
                aa, cc, mm = i + 1, i - 1, i - 2

                def tanh(k, bk):
                    act.wait_ge(up_ps, mm * NBLK + k + 1)
                    if k >= 2:
                        act.wait_ge(hb_sb, mm * NBLK + k - 1)
                    nc.scalar.activation(th[:, k % 2], bank[bk][:, 0:S], ACT.Tanh, scale=0.5).then_inc(th_sb, 1)

                def spread(k):
                    act.wait_ge(cB_ps, mm * 2 + k + 1)
                    nc.scalar.activation(cB[:, 2 * k:2 * k + 2], bank[6][:, :].rearrange("p (n t) -> p n t", n=2),
                                         ACT.Copy).then_inc(cB_sb, 1)

                if core:
                    exps(i, par, 0)
                if experts:
                    tanh(0, 7)
                if ahead:
                    act.wait_ge(q8T_ps, aa + 1)
                    if not (isinstance(i, int) and i < 0):
                        act.wait_ge(f_ps, aa)
                    nc.scalar.activation(q8T[:], bank[5][:, 0:P].bitcast(BF16), ACT.Copy).then_inc(q8T_sb, 1)
                if experts:
                    act.wait_ge(cT_ps, mm + 1)
                    nc.scalar.activation(cT[:], bank[6][0:3 * NE, 0:P].bitcast(BF16), ACT.Copy).then_inc(cT_sb, 1)
                    spread(0)
                    tanh(1, 7)
                if core:
                    exps(i, par, 1)
                if experts:
                    spread(1)
                    tanh(2, 7)
                if ahead:
                    act.wait_ge(x2T_ps, aa + 1)
                    if not (isinstance(i, int) and i < 0):
                        act.wait_ge(vv_ps, aa)
                    nc.scalar.activation(x2T[:], bank[5][:, 0:S], ACT.Copy).then_inc(x2T_sb, 1)
                if core:
                    exps(i, par, 2)
                if ahead:
                    act.wait_ge(qk_ps, aa + 1)
                    if not (isinstance(i, int) and i < 0):
                        act.wait_ge(qk_n, aa)
                    for n in range(2):
                        ins = nc.scalar.activation(cur[:, n, :], bank[5][:, n * S:(n + 1) * S], ACT.Identity, bias=cols[:, n:n + 1])
                    ins.then_inc(qk_sb, 1)
                if experts:
                    tanh(3, 6)
                    tanh(4, 7)
                if behind:
                    act.wait_ge(x3T_ps, cc + 1)
                    nc.scalar.activation(x3T[:, 1 - par], bank[5][:, 0:S], ACT.Copy).then_inc(x3T_sb, 1)
                if core:
                    exps(i, par, 3)
                if ahead:
                    act.wait_ge(qk_n, aa + 1)
                    if not (isinstance(aa, int) and aa < 2):
                        act.wait_ge(pv_ps, aa * 4 - 4)
                    for g in range(QG):
                        ins = nc.scalar.activation(km[:, 1 - par, g], kn[:], ACT.Copy, scale=gmask[:, g:g + 1])
                    ins.then_inc(km_sb, 1)
                if behind:
                    act.wait_ge(lg_rd, cc + 1)
                    nc.scalar.activation(lg[:, 1], lg[:, 0], ACT.Exp).then_inc(lge, 1)

            steps(act, step)

        @block.gpsimd
        def _(gp):
            nc.gpsimd.memset(half[:], -0.5).then_inc(half_sb, 1)
            nc.gpsimd.memset(va[:], 0.0).then_inc(half_sb, 1)
            gp.wait_ge(half_sb, 2)
            nc.gpsimd.memset(va[:, :, :, :, HD:HD + 1], float(STEPS)).then_inc(half_sb, 1)
            gp.wait_ge(half_sb, 3)
            gp.wait_ge(wmax, 1)
            nc.gpsimd.partition_all_reduce(sw[:, 1:2], sw[:, 0:1], P, RMAX).then_inc(wmax_all, 1)
            gp.wait_ge(la_sb, 1)

            def rsqrt(var, tmp, dst, chain, done):
                chain(nc.gpsimd.tensor_scalar(tmp, var, EPS, None, ALU.add))
                nc.gpsimd.tensor_tensor(dst, tmp, half[:, 0:C], ALU.pow).then_inc(done, 1)

            def norm1(b):
                wait_apart(gp, mv_sb, b + 1, (half_sb, 3))
                ch = Chain(gp, c_pow, b, 1)
                rsqrt(mv[:, :, 1], rstd[:, 0], rstd[:, 1], ch, rstd_sb)
                ch.end()

            def attn(b, par, p1, p2):
                if p1:
                    gp.wait_ge(we_ps, b)
                nc.gpsimd.tensor_copy(laB[:].rearrange("p (h v) -> p h v", h=H),
                                      la[:, bass.ds(b * 2 + 1, 1), :].rearrange("p a h -> p (a h)").unsqueeze(2)
                                      .to_broadcast([P, H, DV])).then_inc(laB_sb, 1)
                if p1:
                    norm1(b - 1)
                gp.wait_ge(we_sb, b + 1)
                gp.wait_ge(v_sb, b + 1)
                if p1:
                    gp.wait_ge(st_ps, b)
                nc.gpsimd.tensor_tensor(vw[:].rearrange("p (h v) -> p h v", h=H),
                                        vs[:, par, 0, :].rearrange("p (h v) -> p h v", h=H),
                                        wv[:].unsqueeze(2).to_broadcast([P, H, DV]), ALU.mult).then_inc(vw_sb, 1)

            batches(gp, attn)
            norm1(B - 1)
            gp.wait_ge(xmax, 1)
            nc.gpsimd.partition_all_reduce(sx[:, 1:2], sx[:, 0:1], P, RMAX).then_inc(xmax_all, 1)

            def step(i, par):
                ahead, core, behind, experts = parts(i)
                aa, cc, mm = i + 1, i - 1, i - 2

                def weigh(k):
                    gp.wait_ge(hb_sb, mm * NBLK + k + 1)
                    gp.wait_ge(cB_sb, mm * 2 + (k - 1) // 2 + 1)
                    nc.gpsimd.tensor_tensor(hc[:, k], hb[:, k], cB[:, k - 1], ALU.mult).then_inc(hc_sb, 1)

                if ahead:
                    wait_apart(gp, amv_sb, aa + 1, (half_sb, 3))
                    rsqrt(amv[:, :, 1], ars[:, 0], ars[:, 1], Chain(gp, k_pa, aa, 1), ars_sb)
                if experts:
                    weigh(1)
                if ahead:
                    wait_apart(gp, x2_sb, aa + 1, (half_sb, 3))
                    nc.gpsimd.tensor_tensor(xa[:, bass.ds(aa * 2, 2), :], arA[:], ob_r.unsqueeze(1).to_broadcast([P, C, D]),
                                            ALU.add).then_inc(xo_sb, 1)
                if behind:
                    wait_apart(gp, cmv_sb, cc + 1, (half_sb, 3))
                    rsqrt(cmv[:, :, 1], crs[:, 0], crs[:, 1], Chain(gp, k_pc, cc, 1), crs_sb)
                if experts:
                    for k in range(2, NBLK):
                        weigh(k)
                if behind:
                    wait_apart(gp, cmb_sb, cc + 1, (half_sb, 3))
                    ch = Chain(gp, k_c3, cc, 3)
                    ch(nc.gpsimd.tensor_copy(comb3[:, :, 0], comb[:]))
                    ch(nc.gpsimd.tensor_tensor(crest[:], comb[:], comb3[:, :, 0], ALU.subtract), met=(half_sb, 3))
                    ch(nc.gpsimd.tensor_copy(comb3[:, :, 1], crest[:]))
                    nc.gpsimd.tensor_tensor(comb3[:, :, 2], crest[:], comb3[:, :, 1], ALU.subtract).then_inc(c3_sb, 1)
                    ch.end()
                if experts:
                    wait_apart(gp, dmv_sb, mm + 1, (half_sb, 3))
                    ch = Chain(gp, k_pd, mm, 2)
                    ch(nc.gpsimd.tensor_scalar(drs[:, 0], dmv[:, :, 1], EPS, None, ALU.add))
                    ch(nc.gpsimd.tensor_tensor(drs[:, 1], drs[:, 0], half[:, 0:C], ALU.pow), met=(half_sb, 3))
                    ch.end()
                    wait_apart(gp, yo_free, mm + 1, (half_sb, 3))
                    for c in range(C):
                        ins = nc.gpsimd.tensor_scalar(yo[:, par, c:c + 1, :], drA[:, c:c + 1, :], dmv[:, c, 0:1], drs[:, 1, c:c + 1],
                                                      ALU.subtract, ALU.mult)
                    ins.then_inc(yo_sb, 1)

            steps(gp, step)

        @block.vector
        def _(dve):
            V = nc.vector

            def quantize(ch, src, scale, y, m, dst):
                ch(V.tensor_scalar(y, src, scale, FP8_MAX, ALU.mult, ALU.min))
                ch(V.tensor_scalar(m.bitcast(U32), y.bitcast(U32), 0x7F800000, None, ALU.bitwise_and))
                ch(V.tensor_scalar(m, m, 2.0 ** -6, 1.5 * 2.0 ** 20, ALU.max, ALU.mult))
                ch(V.scalar_tensor_tensor(y, y, -FP8_MAX, m, ALU.max, ALU.add))
                return V.tensor_tensor(dst, y, m, ALU.subtract)

            def scale_of(ch, s):
                ch(V.tensor_scalar(s[:, 0:1], s[:, 1:2], 1e-12, None, ALU.max))
                ch(V.reciprocal(s[:, 1:2], s[:, 0:1]))
                ch(V.tensor_scalar(s[:, 2:3], s[:, 1:2], FP8_MAX, FP8_MAX, ALU.mult, ALU.min))
                ch(V.reciprocal(s[:, 3:4], s[:, 2:3]))

            one = Chain(dve, dve_one, 0, 100)
            dve.wait_ge(c_in, 48)

            def gate_pass(b, par, p1, p2):
                dve.wait_ge(z_ps, b + 1)
                V.tensor_tensor(lz[:, 0, bass.ds(b * 2, 2), :], bank[6 + par][:, 0:C * H].rearrange("p (c h) -> p c h", c=C),
                                bg_r.unsqueeze(1).to_broadcast([P, C, H]), ALU.add).then_inc(z_sb, 1)

            batches(dve, gate_pass)
            V.tensor_copy(eselb[:], esel)
            V.tensor_scalar(shut[:], later, -1e30, None, ALU.mult)
            V.tensor_copy(identb[:], ident).then_inc(setup, 1)
            dve.wait_ge(w_in, 16 * 5)
            one(V.tensor_scalar(wo[:], wo[:], 0.5, None, ALU.mult))
            V.tensor_reduce(sw[:, 0:1], ffw[:], AX.X, ALU.max, apply_absolute_value=True).then_inc(wmax, 1)
            dve.wait_ge(gate, 1)
            V.scalar_tensor_tensor(la[:], lz[:, 3], -1.0, lz[:, 1], ALU.mult, ALU.subtract).then_inc(la_sb, 1)
            V.tensor_copy(oneh[:], head_of.unsqueeze(2).to_broadcast([P, H, P]))
            one(V.memset(lp[:], 0.0))
            dve.wait_ge(cum_ps, 1)
            l32 = bank[2][:, 0:B * C * H].rearrange("p (n h) -> p n h", h=H)
            one(V.tensor_copy(lp[:, :, 0:H], l32))
            one(V.tensor_tensor(cum[:, 0], l32, lp[:, :, 0:H], ALU.subtract))
            one(V.tensor_copy(lp[:, :, H:2 * H], cum[:, 0]))
            one(V.tensor_tensor(cum[:, 1], cum[:, 0], lp[:, :, H:2 * H], ALU.subtract))
            V.tensor_copy(lp[:, :, 2 * H:3 * H], cum[:, 1]).then_inc(lp_sb, 1)
            dve.wait_ge(wmax_all, 1)
            scale_of(one, sw)
            ins = quantize(one, ffw[:], sw[:, 2:3], wq_t[:, 0], wq_t[:, 1], wfT[:])
            ins.then_inc(setup, 1)
            dve.wait_ge(w2_in, 16 * 5)
            V.tensor_scalar(wdn[:, 0, :], wdn[:, 0, :], 0.5, None, ALU.mult).then_inc(wf_sb, 1)

            def stats(ch, r, bnb, mvb, mv_done):
                for c in range(C):
                    ins = V.bn_stats(bnb[:, c, :], r[:, c, :])
                ch(ins, met=(c_in, 48))
                for c in range(C):
                    ins = V.bn_aggr(mvb[:, c, :], bnb[:, c, :])
                ins.then_inc(mv_done, 1)

            def scaled(r, mvb, rs_, rs_ready, index, to):
                dve.wait_ge(rs_ready, index + 1)
                for c in range(C):
                    ins = V.tensor_scalar(to(c), r[:, c:c + 1, :], mvb[:, c, 0:1], rs_[:, 1, c:c + 1], ALU.subtract, ALU.mult)
                return ins

            def tail(b, par):
                dve.wait_ge(o_ps, b + 1)
                dve.wait_ge(we_sb, b + 1)
                dve.wait_ge(og_sb, b + 1)
                ch = Chain(dve, c_oT, b, 2)
                intra = bank[6][:, :].rearrange("p (c g t) -> p c g t", c=C, g=G2)
                ch(V.tensor_tensor(t0[:], bank[7][:, 0:256].rearrange("p (g t) -> p g t", g=G2), el[:], ALU.mult))
                ch(V.tensor_tensor(t1[:], t0[:], intra[:, 1], ALU.add))
                V.scalar_tensor_tensor(oT[:, :, 0:P], ogt[:, :, 0:P], 1.0, intra[:, 0], ALU.add, ALU.mult)
                V.scalar_tensor_tensor(oT[:, :, P:S], ogt[:, :, P:S], 1.0, t1[:], ALU.add, ALU.mult).then_inc(oT_sb, 1)
                ch.end()
                dve.wait_ge(y_ps, b + 1)
                ch = Chain(dve, c_ln, b, 2)
                V.tensor_tensor(rs[:], bank[7][:, 256:512].rearrange("p (c d) -> p c d", c=C), xs[:, par], ALU.add)\
                    .then_inc(r1_sb, 1)
                dve.wait_ge(r1_sb, b + 1)
                xo = xa[:, bass.ds(b * 2, 2), :]
                stats(ch, rs, bn, mv, mv_sb)
                ch(scaled(rs, mv, rstd, rstd_sb, b, lambda c: xa[:, bass.ds(b * 2 + c, 1), :]))
                V.tensor_reduce(amax[:, bass.ds(b, 1)], xo, AX.XY, ALU.max, apply_absolute_value=True)
                ch.end()

            def attn(b, par, p1, p2):
                if p1:
                    tail(b - 1, 1 - par)
                for c in range(C):
                    dve.wait_ge(s_ps, b * 2 + c + 1)
                    dve.wait_ge(d_sb, b * 2 + c + 1)
                    for k in range(2):
                        ins = V.tensor_tensor(pp[:, c, 4 * k:4 * k + 4, :], bank[k][:, :].rearrange("p (h t) -> p h t", h=4),
                                              dd[:, c, 4 * k:4 * k + 4, :], ALU.mult)
                    ins.then_inc(p_sb, 1)

            batches(dve, attn)
            tail(B - 1, (B - 1) % 2)

            one(V.tensor_scalar(amax[:, B:B + 1], amax[:, 0:1], 0.0, None, ALU.add))
            V.tensor_reduce(sx[:, 0:1], amax[:, 0:B], AX.X, ALU.max).then_inc(xmax, 1)
            dve.wait_ge(xmax_all, 1)
            scale_of(one, sx)
            one(V.tensor_tensor(scl[:], sx[:, 3:4], sw[:, 3:4], ALU.mult))
            dve.wait_ge(half_sb, 3)

            thr = lif_thresholds()

            def quant(n, b0, b1):
                y, m = (gT[:, k].rearrange("p h t -> p (h t)")[:, 0:(b1 - b0) * S].rearrange("p (c d) -> p c d", d=D)
                        for k in range(2))
                ch = Chain(dve, k_q, n, 4)
                quantize(ch, xa[:, b0 * C:b1 * C, :], sx[:, 2:3], y, m, q8[:, b0 * C:b1 * C, :]).then_inc(q8_sb, 1)
                ch.end()

            def ffn_a(aa):
                dve.wait_ge(f_ps, aa + 1)
                V.scalar_tensor_tensor(fb[:], bank[5][:, 0:S].rearrange("p (c d) -> p c d", c=C), scl[:, 0:1],
                                       fb_r.unsqueeze(1).to_broadcast([P, C, D]), ALU.mult, ALU.add).then_inc(f_rd, 1)
                dve.wait_ge(f_rd, aa + 1)
                ch = Chain(dve, k_a, aa, 2)
                ch(V.tensor_tensor(qy[:], fb[:], xa[:, bass.ds(aa * 2, 2), :], ALU.add))
                stats(ch, qy, abn, amv, amv_sb)
                return ch

            def ffn_b(aa, ch):
                if not (isinstance(aa, int) and aa < 1):
                    dve.wait_ge(x2T_ps, aa)
                    dve.wait_ge(xo_sb, aa)
                scaled(qy, amv, ars, ars_sb, aa, lambda c: arA[:, c:c + 1, :]).then_inc(x2_sb, 1)
                ch.end()

            def take_v(aa):
                dve.wait_ge(vv_ps, aa + 1)
                V.tensor_tensor(cur[:, 2, :].rearrange("p (c d) -> p c d", c=C),
                                bank[5][:, 0:S].rearrange("p (c d) -> p c d", c=C),
                                vb_r.unsqueeze(1).to_broadcast([P, C, D]), ALU.add).then_inc(vv_sb, 1)

            def over(n, lo, hi):
                to, before = (n1, n2) if n % 2 == 0 else (n2, n1)
                if n == 0:
                    return V.tensor_scalar(to[:, lo:hi], cur[:, lo:hi], thr[0], None, ALU.is_gt)
                return V.scalar_tensor_tensor(to[:, lo:hi], cur[:, lo:hi], thr[n], before[:, lo:hi], ALU.is_gt, ALU.add)

            def spikes_qk(aa, par):
                if not (isinstance(aa, int) and aa < 2):
                    dve.wait_ge(sc_ps, aa * 8 - 8)
                if not (isinstance(aa, int) and aa < 1):
                    dve.wait_ge(km_sb, aa)
                V.scalar_tensor_tensor(qn[:, par], cur[:, 0], thr[3], n1[:, 0], ALU.is_gt, ALU.add)
                V.scalar_tensor_tensor(kn[:], cur[:, 1], thr[3], n1[:, 1], ALU.is_gt, ALU.add).then_inc(qk_n, 1)

            def spikes_v(aa, par):
                if not (isinstance(aa, int) and aa < 2):
                    dve.wait_ge(pv_ps, aa * 4 - 4)
                V.scalar_tensor_tensor(va[:, par, :, :, 0:HD], cur[:, 2].rearrange("p (c h d) -> p c h d", c=C, h=NH), thr[3],
                                       n1[:, 2].rearrange("p (c h d) -> p c h d", c=C, h=NH), ALU.is_gt, ALU.add)\
                    .then_inc(va_sb, 1)

            def turn(i, pair):
                dve.wait_ge(pv_ps, i * 4 + 2 * pair + 2)
                if not (isinstance(i, int) and i < 1):
                    dve.wait_ge(aT_sb, i)
                V.transpose(tq[:, 2 * pair:2 * pair + 2].rearrange("p g b r -> p (g b r)"), bank[4][:, :]).then_inc(tr_sb, 1)

            def attend(cc):
                dve.wait_ge(tr_sb, cc * 2 + 2)
                ch = Chain(dve, k_n, cc, 2)
                ch(V.reciprocal(rd[:], tq[:, :, :, HD]))
                ch(V.tensor_tensor(on[:].rearrange("p b g d -> p g b d"), tq[:, :, :, 0:HD],
                                   rd[:].unsqueeze(3).to_broadcast([P, QG, C * 4, HD]), ALU.mult))
                V.transpose(aT[:], on[:].rearrange("p b g d -> p (b g d)")).then_inc(aT_sb, 1)
                ch.end()

            def project_a(cc):
                dve.wait_ge(w_ps, cc + 1)
                dve.wait_ge(xo_sb, cc + 1)
                V.tensor_tensor(cr[:], bank[5][:, 0:S].rearrange("p (c d) -> p c d", c=C), xa[:, bass.ds(cc * 2, 2), :], ALU.add)\
                    .then_inc(w_rd, 1)
                dve.wait_ge(w_rd, cc + 1)
                ch = Chain(dve, k_c, cc, 1)
                stats(ch, cr, cbn, cmv, cmv_sb)
                ch.end()

            def project_b(cc, par):
                scaled(cr, cmv, crs, crs_sb, cc, lambda c: crA[:, par, c:c + 1, :]).then_inc(x3_sb, 1)

            def logits(cc):
                dve.wait_ge(lg_ps, cc + 1)
                ch = Chain(dve, k_top, cc, 12)
                lp = bank[5][:, 0:C * NE].rearrange("p (c e) -> p c e", c=C)
                ch(V.tensor_reduce(ls[:, 0], lp, AX.X, ALU.max))
                V.tensor_tensor(lg[:, 0], lp, ls[:, 0].unsqueeze(2).to_broadcast([P, C, NE]), ALU.subtract).then_inc(lg_rd, 1)
                dve.wait_ge(lg_rd, cc + 1)
                return ch

            def top2(cc, ch):
                bc = lambda t: t.unsqueeze(2).to_broadcast([P, C, NE])
                rv = rev.unsqueeze(1).to_broadcast([P, C, NE])
                d, e, k1, s1, d2, k2, s2, es = (lg[:, n] for n in range(8))
                ch(V.scalar_tensor_tensor(k1, d, 0.0, rv, ALU.is_equal, ALU.mult))
                ch(V.tensor_reduce(ls[:, 1], k1, AX.X, ALU.max))
                ch(V.tensor_tensor(s1, k1, bc(ls[:, 1]), ALU.is_equal))
                ch(V.scalar_tensor_tensor(d2, s1, -1e30, d, ALU.mult, ALU.add))
                ch(V.tensor_reduce(ls[:, 2], d2, AX.X, ALU.max))
                ch(V.tensor_tensor(s2, d2, bc(ls[:, 2]), ALU.is_equal))
                ch(V.tensor_tensor(k2, s2, rv, ALU.mult))
                ch(V.tensor_reduce(ls[:, 3], k2, AX.X, ALU.max))
                ch(V.tensor_tensor(s2, k2, bc(ls[:, 3]), ALU.is_equal))
                ch(V.tensor_tensor(k1, s1, s2, ALU.add))
                dve.wait_ge(lge, cc + 1)
                V.tensor_reduce(ls[:, 4], e, AX.X, ALU.add)
                ch(V.tensor_tensor(es, e, k1, ALU.mult))
                ch.end()
                ch = Chain(dve, k_up, cc, 3)
                ch(V.tensor_reduce(ls[:, 5], es, AX.X, ALU.add))
                ch(V.scalar_tensor_tensor(ls[:, 6], ls[:, 4], 1e-9, ls[:, 5], ALU.mult, ALU.add))
                ch(V.reciprocal(ls[:, 7], ls[:, 6]))
                V.scalar_tensor_tensor(comb[:], es, 0.5, bc(ls[:, 7]), ALU.mult, ALU.mult).then_inc(cmb_sb, 1)
                ch.end()

            def gated(cc, k, bk):
                dve.wait_ge(th_sb, cc * NBLK + k + 1)
                V.scalar_tensor_tensor(ha[:, k % 2], th[:, k % 2], 1.0, bank[bk][:, 0:S], ALU.add, ALU.mult)\
                    .then_inc(k_d, 1)

            def hidden(cc, k, bk):
                dve.wait_ge(k_d, cc * NBLK + k + 1)
                V.tensor_tensor(hb[:, k], ha[:, k % 2], bank[bk][:, S:2 * S], ALU.mult).then_inc(hb_sb, 1)

            def finish_a(mm, par):
                dve.wait_ge(dn_ps, mm + 1)
                if not (isinstance(mm, int) and mm < 1):
                    dve.wait_ge(yo_sb, mm)
                V.tensor_tensor(drA[:], bank[6][:, 0:S].rearrange("p (c d) -> p c d", c=C), crA[:, par], ALU.add).then_inc(dn_rd, 1)
                dve.wait_ge(dn_rd, mm + 2)
                ch = Chain(dve, k_fin, mm, 1)
                stats(ch, drA, dbn, dmv, dmv_sb)
                ch.end()

            def step(i, par):
                ahead, core, behind, experts = parts(i)
                aa, cc, mm = i + 1, i - 1, i - 2
                if experts:
                    gated(mm, 0, 7)
                    hidden(mm, 0, 7)
                if behind:
                    turn(cc, 1)
                    attend(cc)
                if ahead:
                    links = ffn_a(aa)
                if experts:
                    gated(mm, 1, 7)
                    hidden(mm, 1, 7)
                if ahead:
                    ffn_b(aa, links)
                if behind:
                    project_a(cc)
                if experts:
                    gated(mm, 2, 7)
                    hidden(mm, 2, 7)
                if behind:
                    project_b(cc, 1 - par)
                if core:
                    turn(i, 0)
                if ahead:
                    dve.wait_ge(qk_sb, aa + 1)
                    lif = Chain(dve, k_lif, aa, 6)
                    lif.link(over(0, 0, 2))
                if experts:
                    gated(mm, 3, 6)
                if ahead:
                    take_v(aa)
                    lif.meet()
                    lif.link(over(1, 0, 2))
                if experts:
                    hidden(mm, 3, 6)
                if ahead:
                    lif.meet()
                    lif.link(over(2, 0, 2))
                    lif.meet()
                    spikes_qk(aa, 1 - par)
                if experts:
                    gated(mm, 4, 7)
                if ahead:
                    dve.wait_ge(vv_sb, aa + 1)
                    lif.link(over(0, 2, 3))
                if experts:
                    hidden(mm, 4, 7)
                if ahead:
                    lif.meet()
                    lif(over(1, 2, 3))
                    lif(over(2, 2, 3))
                    spikes_v(aa, 1 - par)
                    lif.end()
                if behind:
                    top2(cc, logits(cc))
                if experts:
                    finish_a(mm, par)
                if isinstance(i, int) and i < 0:
                    quant(1, 1, B)

            dve.sem_inc(dn_rd, 1)
            quant(0, 0, 1)
            steps(dve, step)


def kernel(**inputs):
    import numpy as np
    import concourse.bacc as bacc
    from concourse.bass_utils import run_bass_kernel_spmd

    w = {k: np.asarray(v) for k, v in inputs.items()}
    heads = lambda m: m.reshape(D, H, P).transpose(2, 1, 0)
    wide = lambda m: m.transpose(1, 0, 2).reshape(D, -1)
    blocks = lambda m: m.reshape(-1, P, D).transpose(1, 0, 2)
    gates = np.concatenate([wide(w["L1_ffn_wg_s"]), wide(w["L1_ffn_wg_r"])], 1).reshape(D, NBLK, 1, P)
    ups = np.concatenate([wide(w["L1_ffn_wu_s"]), wide(w["L1_ffn_wu_r"])], 1).reshape(D, NBLK, 1, P)
    p = np.arange(P)
    esel = np.zeros((P, NBLK - 1, EPB, ME), np.float32)
    for row in range(3 * NE):
        e = row % NE
        esel[row, e // EPB, e % EPB, :] = 1.0
    cst = np.concatenate([
        np.eye(P), p[:, None] > p[None, :], p[:, None] <= p[None, :],
        (p[:, None] // HD) % QG == np.arange(QG)[None, :],
        np.broadcast_to(np.arange(NE, 0, -1)[None, :], (P, NE)),
        (p[:, None] % H == np.arange(H)[None, :]) & (p[:, None] < 3 * H),
        esel.reshape(P, -1)], 1).astype(np.float32)
    arrays = {
        "x": w["L0_attn_x"],
        "cst": cst,
        "rows": np.broadcast_to(np.concatenate([w["L0_attn_bg"], w["L0_ffn_bias"], w["L1_attn_v_b"], w["L1_attn_o_b"]])[None, :],
                                (P, H + 3 * D)),
        "cols": np.stack([w["L1_attn_q_b"], w["L1_attn_k_b"]], 1),
        "wqT": heads(w["L0_attn_Wq"]), "wkT": heads(w["L0_attn_Wk"]),
        "wvg": np.concatenate([w["L0_attn_Wv"], w["L0_attn_Wg"]], 1),
        "wog": w["L0_attn_Wog"], "wo": blocks(w["L0_attn_Wo"]),
        "ffw": w["L0_ffn_weight"].T,
        "wqkvo": np.stack([w["L1_attn_q_w"], w["L1_attn_k_w"], w["L1_attn_v_w"], w["L1_attn_o_w"]], 1),
        "wr": w["L1_ffn_router_w"],
        "wup": np.concatenate([gates, ups], 2),
        "wdn": np.concatenate([blocks(w["L1_ffn_wd_s"].reshape(-1, D)), blocks(w["L1_ffn_wd_r"].reshape(-1, D))], 1),
    }
    arrays = {k: np.ascontiguousarray(v) for k, v in arrays.items()}
    nc = bacc.Bacc("TRN2", target_bir_lowering=False, num_devices=1)
    aps = {k: nc.dram_tensor(k + "_dram", v.shape, mybir.dt.from_np(v.dtype), kind="ExternalInput").ap()
           for k, v in arrays.items()}
    out = nc.dram_tensor("out_dram", (B, S, D), F32, kind="ExternalOutput").ap()
    fused_layers(nc, aps, out)
    r = run_bass_kernel_spmd(nc, [{k + "_dram": v for k, v in arrays.items()}], core_ids=[0])
    return r.results[0]["out_dram"]
```

```python
from contextlib import ExitStack

import concourse.bass as bass
from concourse import mybir

ALU = mybir.AluOpType
ACT = mybir.ActivationFunctionType
AX = mybir.AxisListType
F32 = mybir.dt.float32
BF16 = mybir.dt.bfloat16
U32 = mybir.dt.uint32
RMAX = bass.bass_isa.ReduceOp.max

P = 128
B, S, D = 8, 256, 128
C = S // P
H, DV = 8, 32
GATE_NORM = 16.0
G2 = H * DV // P
HPB = P // DV
NH, HD = 16, 8
QG = 4
NE, ME = 16, 32
NBLK = 5
EPB = P // ME
EPS = 1e-5
FLT_MAX = 3.4028234663852886e38
FP8_MAX = 448.0
STEPS = 4


def lif_thresholds():
    import numpy as np
    beta, thr = np.float32(0.95), np.float32(1.0)

    def spikes(cur):
        mem, n = np.float32(0.0), 0
        for _ in range(STEPS):
            reset = thr if mem > thr else np.float32(0.0)
            mem = np.float32(np.float32(np.float32(beta * mem) + cur) - reset)
            n += int(mem > thr)
        return n

    steps = []
    for want in range(1, STEPS + 1):
        lo, hi = np.float32(0.125), np.float32(2.0)
        while np.nextafter(lo, hi) < hi:
            mid = np.float32((np.float64(lo) + np.float64(hi)) / 2)
            if spikes(mid) >= want:
                hi = mid
            else:
                lo = mid
        steps.append(float(lo))
    return steps


def wait_apart(eng, semaphore, value, met):
    value = value if isinstance(value, int) else eng.to_reg(value)
    eng.wait_ge(*met)
    eng.wait_ge(semaphore, value)


class Chain:

    def __init__(self, eng, sem, index, per):
        self.eng, self.sem, self.index, self.per, self.k = eng, sem, index, per, 0

    def link(self, ins):
        self.k += 1
        ins.then_inc(self.sem, 1)

    def meet(self):
        self.eng.wait_ge(self.sem, self.index * self.per + self.k)

    def __call__(self, ins, met=None):
        self.link(ins)
        value = self.index * self.per + self.k
        if met is None:
            self.eng.wait_ge(self.sem, value)
        else:
            wait_apart(self.eng, self.sem, value, met)

    def end(self):
        assert self.k == self.per, f"{self.k} links, {self.per} counted on"


def fused_layers(nc, a, out):
    x_dram = a["x"].rearrange("b (c p) d -> b p c d", p=P)
    out_dram = out.rearrange("b (c p) d -> b p c d", p=P)

    with ExitStack() as ctx:
        def sb(name, shape, dt=F32):
            return ctx.enter_context(nc.sbuf_tensor(name, shape, dt))

        def sem(name):
            return ctx.enter_context(nc.semaphore(name))

        wqT = sb("wqT", [P, H, P]); wkT = sb("wkT", [P, H, P])
        wvg = sb("wvg", [P, H * DV + H]); wog = sb("wog", [P, H * DV]); wo = sb("wo", [P, G2, D])
        rows = sb("rows", [P, H + 3 * D])
        cols = sb("cols", [P, 2])
        cst = sb("cst", [P, 3 * P + 6 + H])
        ffw = sb("ffw", [P, D])
        wqkvo = sb("wqkvo", [P, 4, D])
        wr = sb("wr", [P, NE]); wup = sb("wup", [P, NBLK, 2, P]); wdn = sb("wdn", [P, NBLK, D])
        bg_r, fb_r = rows[:, 0:H], rows[:, H:H + D]
        vb_r, ob_r = rows[:, H + D:H + 2 * D], rows[:, H + 2 * D:H + 3 * D]
        ident, later, upto = cst[:, 0:P], cst[:, P:2 * P], cst[:, 2 * P:3 * P]
        gmask = cst[:, 3 * P:3 * P + 4]
        signs = cst[:, 3 * P + 4:3 * P + 6]
        head_of = cst[:, 3 * P + 6:3 * P + 6 + H]
        esel = sb("esel", [3 * NE, (NBLK - 1) * P])
        identb = sb("identb", [P, P], BF16)
        shut = sb("shut", [P, P], BF16)
        eselb = sb("eselb", [3 * NE, (NBLK - 1) * P], BF16)
        amat = sb("amat", [P, H, P])
        wfT = sb("wfT", [P, D], BF16)
        half = sb("half", [P, 2])

        xa = sb("xa", [P, B * C, D])
        la = sb("la", [P, B * C, H])
        lz = sb("lz", [P, 4, B * C, H])
        cum = sb("cum", [P, 2, B * C, H])
        lp = sb("lp", [P, B * C, P], BF16)
        lpT = sb("lpT", [P, B * C, P], BF16); fromT = sb("fromT", [P, B * C, P], BF16)
        toT = sb("toT", [P, C, H, P], BF16)
        headv = sb("headv", [P, H * DV], BF16)
        amax = sb("amax", [P, B])
        sw = sb("sw", [P, 4]); sx = sb("sx", [P, 4]); scl = sb("scl", [P, 1])
        wq_t = sb("wq_t", [P, 2, D])
        q8 = sb("q8", [P, B * C, D], BF16)

        xs = sb("xs", [P, 2, C, D]); xT = sb("xT", [P, 2, S])
        xTa = sb("xTa", [P, B, S])
        gT = sb("gT", [P, 2, H, S]); vs = sb("vs", [P, 2, C, H * DV])
        dd = sb("dd", [P, C, H, P]); pp = sb("pp", [P, C, H, P])
        wv = sb("wv", [P, H]); vw = sb("vw", [P, H * DV])
        el = sb("el", [P, G2, P]); ogt = sb("ogt", [P, G2, S]); st = sb("st", [P, H * DV])
        t0 = sb("t0", [P, G2, P]); t1 = sb("t1", [P, G2, P]); oT = sb("oT", [P, G2, S])
        rs = sb("rs", [P, C, D]); bn = sb("bn", [P, C, 6]); mv = sb("mv", [P, C, 2]); rstd = sb("rstd", [P, 2, C])

        qy = sb("qy", [P, C, D]); q8T = sb("q8T", [P, S], BF16)
        fb = sb("fb", [P, C, D], BF16)
        x2T = sb("x2T", [P, S]); cur = sb("cur", [P, 3, S])
        n1 = sb("n1", [P, 3, S], BF16); n2 = sb("n2", [P, 3, S], BF16)
        qn = sb("qn", [P, 2, S], BF16); kn = sb("kn", [P, S], BF16); km = sb("km", [P, 2, QG, S], BF16)
        va = sb("va", [P, 2, C, NH, 32])
        ee = sb("ee", [P, 2, 4, C, S])
        tq = sb("tq", [P, QG, C * 4, 32]); rd = sb("rd", [P, QG, C * 4]); on = sb("on", [P, C * 4, QG, HD])
        aT = sb("aT", [P, S])
        arA = sb("arA", [P, C, D]); abn = sb("abn", [P, C, 6]); amv = sb("amv", [P, C, 2]); ars = sb("ars", [P, 2, C])
        crA = sb("crA", [P, 2, C, D]); cbn = sb("cbn", [P, C, 6]); cmv = sb("cmv", [P, C, 2]); crs = sb("crs", [P, 2, C])
        drA = sb("drA", [P, C, D]); dbn = sb("dbn", [P, C, 6]); dmv = sb("dmv", [P, C, 2]); drs = sb("drs", [P, 2, C])
        x3T = sb("x3T", [P, 2, S]); cr = sb("cr", [P, C, D])
        lg = sb("lg", [P, 5, C, NE]); ls = sb("ls", [P, 4, C]); m8 = sb("m8", [P, C, 8]); two8 = sb("two8", [P, C, 8])
        comb = sb("comb", [P, C, NE])
        comb3 = sb("comb3", [P, C, 3, NE], BF16); crest = sb("crest", [P, C, NE])
        cT = sb("cT", [3 * NE, S], BF16); cB = sb("cB", [P, NBLK - 1, S])
        th = sb("th", [P, 2, S]); ha = sb("ha", [P, 2, S]); hb = sb("hb", [P, NBLK, S]); hc = sb("hc", [P, NBLK, S])
        yo = sb("yo", [P, 2, C, D])

        bank = [ctx.enter_context(nc.psum_tensor(f"bank{i}", [P, 512], F32)) for i in range(8)]

        wqk_in = sem("wqk_in"); w_in = sem("w_in"); w2_in = sem("w2_in"); c_in = sem("c_in")
        cst_in = sem("cst_in")
        x0_in = [sem("x0_in_first"), sem("x0_in_second")]; x0T_ps = sem("x0T_ps"); x0T_sb = sem("x0T_sb"); z_ps = sem("z_ps")
        z_sb = sem("z_sb")
        am_ps = sem("am_ps"); am_sb = sem("am_sb"); gate = sem("gate"); la_sb = sem("la_sb")
        ident_sb = sem("ident_sb")
        half_sb = sem("half_sb")
        wmax = sem("wmax"); wmax_all = sem("wmax_all"); wf_sb = sem("wf_sb")
        xmax = sem("xmax"); xmax_all = sem("xmax_all"); dve_one = sem("dve_one"); act_one = sem("act_one")
        x_in = [sem("x_in_even"), sem("x_in_odd")]
        v_ps = sem("v_ps"); g_ps = sem("g_ps"); ax_ps = sem("ax_ps"); we_ps = sem("we_ps")
        og_ps = sem("og_ps"); s_ps = sem("s_ps"); st_ps = sem("st_ps"); o_ps = sem("o_ps"); y_ps = sem("y_ps")
        xT_sb = sem("xT_sb"); g_sb = sem("g_sb"); d_sb = sem("d_sb"); we_sb = sem("we_sb")
        og_sb = sem("og_sb")
        st_sb = sem("st_sb"); v_sb = sem("v_sb"); p_sb = sem("p_sb"); oT_sb = sem("oT_sb")
        r1_sb = sem("r1_sb")
        cum_ps = sem("cum_ps"); lp_sb = sem("lp_sb"); lp_ps = sem("lp_ps"); to_sb = sem("to_sb")
        lpT_sb = sem("lpT_sb"); lpT2_sb = sem("lpT2_sb"); vw_sb = sem("vw_sb")
        mv_sb = sem("mv_sb"); rstd_sb = sem("rstd_sb"); c_oT = sem("c_oT"); c_ln = sem("c_ln")
        c_pow = sem("c_pow")

        q8_sb = sem("q8_sb"); q8T_ps = sem("q8T_ps"); q8T_sb = sem("q8T_sb"); f_ps = sem("f_ps")
        f_rd = sem("f_rd")
        x2_sb = sem("x2_sb"); x2T_ps = sem("x2T_ps"); x2T_sb = sem("x2T_sb"); qk_ps = sem("qk_ps")
        qk_sb = sem("qk_sb")
        vv_ps = sem("vv_ps"); vv_sb = sem("vv_sb"); qk_n = sem("qk_n"); km_sb = sem("km_sb")
        va_sb = sem("va_sb"); xo_sb = sem("xo_sb")
        sc_ps = sem("sc_ps"); e_sb = sem("e_sb"); pv_ps = sem("pv_ps"); tr_sb = sem("tr_sb")
        aT_sb = sem("aT_sb")
        w_ps = sem("w_ps"); w_rd = sem("w_rd"); x3_sb = sem("x3_sb"); x3T_ps = sem("x3T_ps")
        x3T_sb = sem("x3T_sb")
        lg_ps = sem("lg_ps"); lg_rd = sem("lg_rd"); lge = sem("lge"); cmb_sb = sem("cmb_sb")
        cT_ps = sem("cT_ps")
        cT_sb = sem("cT_sb"); cB_ps = sem("cB_ps"); cB_sb = sem("cB_sb"); up_ps = sem("up_ps")
        th_sb = sem("th_sb")
        hb_sb = sem("hb_sb"); hc_sb = sem("hc_sb"); dn_ps = sem("dn_ps"); dn_rd = sem("dn_rd")
        yo_sb = sem("yo_sb")
        out_done = sem("out_done"); yo_free = sem("yo_free")
        amv_sb = sem("amv_sb"); ars_sb = sem("ars_sb"); cmv_sb = sem("cmv_sb"); crs_sb = sem("crs_sb")
        dmv_sb = sem("dmv_sb")
        k_q = sem("k_q"); k_a = sem("k_a"); k_lif = sem("k_lif"); k_n = sem("k_n"); k_c = sem("k_c")
        k_top = sem("k_top"); k_up = sem("k_up"); k_d = sem("k_d")
        c3_sb = sem("c3_sb"); k_c3 = sem("k_c3"); k_pa = sem("k_pa"); k_pc = sem("k_pc")
        k_pd = sem("k_pd"); k_fin = sem("k_fin")

        def xg(k):
            return gT[:, 0].rearrange("p h t -> p (h t)")[:, k * B * C * D // 2:(k + 1) * B * C * D // 2].rearrange("p (n d) -> p n d", d=D)

        block = ctx.enter_context(nc.Block())

        def batches(eng, body):
            body(0, 0, False, False)
            body(1, 1, True, False)
            with eng.Fori(1, B // 2) as m:
                body(m * 2, 0, True, True)
                body(m * 2 + 1, 1, True, True)

        def steps(eng, body):
            body(-1, 1)
            body(0, 0)
            body(1, 1)
            with eng.Fori(1, B // 2 - 1) as m:
                body(m * 2, 0)
                body(m * 2 + 1, 1)
            for i in range(B - 2, B + 2):
                body(i, i % 2)

        def loads(b, par):
            return b * 8 - 8 * par + 16

        def alone(i):
            return isinstance(i, int) and i >= B

        def up_bank(i, k):
            return (7, 0, 1, 2, 3)[k] if alone(i) else (7, 6, 7, 7, 6)[k]

        def spread_bank(i, k):
            return 5 if k == 1 and alone(i - 1) else 6

        def parts(i):
            if isinstance(i, int):
                return tuple(0 <= n < B for n in (i + 1, i, i - 1, i - 2))
            return True, True, True, True

        @block.sync
        def _(sp):
            sp.dma_start(cst[:], a["cst"]).then_inc(cst_in, 16)
            for k in range(2):
                sp.dma_start(xg(k), x_dram[k * B // 2:(k + 1) * B // 2].rearrange("b p c d -> p (b c) d")).then_inc(x0_in[k], 16)
                if k == 0:
                    sp.dma_start(wvg[:], a["wvg"]).then_inc(c_in, 16)
            sp.dma_start(rows[:], a["rows"]).then_inc(c_in, 16)
            sp.dma_start(esel[:], a["esel"]).then_inc(w2_in, 16)
            for dst, name in ((wqkvo, "wqkvo"), (cols, "cols"), (wr, "wr"), (wup, "wup"), (wdn, "wdn")):
                sp.dma_start(dst[:], a[name]).then_inc(w2_in, 16)

            def load(b, par, p1, p2):
                if p2:
                    sp.wait_ge(r1_sb, b - 1)
                sp.dma_start(xs[:, par], x_dram[bass.ds(b, 1)].rearrange("a p c d -> p (a c) d")).then_inc(x_in[par], 16)

            batches(sp, load)

            def store(b, par, p1, p2):
                sp.wait_ge(yo_sb, b + 1)
                sp.dma_start(out_dram[bass.ds(b, 1)].rearrange("a p c d -> p (a c) d"), yo[:, par]).then_inc(out_done, 16)
                sp.wait_ge(out_done, b * 16 + 16)
                sp.sem_inc(yo_free, 1)

            sp.sem_inc(yo_free, 2)
            batches(sp, store)

        @block.tensor
        def _(pe):
            pe.wait_ge(cst_in, 16)

            def x_transposes(k):
                pe.wait_ge(x0_in[k // (B // 4)], 16)
                for c in range(2 * C):
                    ins = nc.tensor.transpose(bank[k][:, c * P:(c + 1) * P],
                                              xg(k // (B // 4))[:, k % (B // 4) * 2 * C + c, :], ident)
                ins.then_inc(x0T_ps, 1)

            for k in range(B // 4):
                x_transposes(k)
            pe.wait_ge(wqk_in, 32)
            for h in range(H):
                ins = nc.tensor.matmul(bank[5 + h // 4][:, (h % 4) * P:(h % 4 + 1) * P], wqT[:, h, :], wkT[:, h, :],
                                       start=True, stop=True)
            ins.then_inc(am_ps, 1)
            for k in range(B // 4, B // 2):
                x_transposes(k)
            pe.wait_ge(c_in, 32)
            for k in range(B // 2):
                pe.wait_ge(x0T_sb, k + 1)
                for c in range(2 * C * k, 2 * C * (k + 1)):
                    ins = nc.tensor.matmul(bank[7][:, c * H:(c + 1) * H], xTa[:, c // C, c % C * P:(c % C + 1) * P],
                                           wvg[:, H * DV:], start=True, stop=True)
            ins.then_inc(z_ps, 1)
            pe.wait_ge(w_in, 16 * 3)

            def running_sums():
                pe.wait_ge(la_sb, 1)
                nc.tensor.matmul(bank[7][:, 0:B * C * H], upto, la[:].rearrange("p n h -> p (n h)"), start=True, stop=True)\
                    .then_inc(cum_ps, 1)

            def sums_by_row():
                pe.wait_ge(ident_sb, 1)
                pe.wait_ge(lp_sb, 1)
                for k in range(2):
                    bt = bank[k][:, :].bitcast(BF16)
                    for n in range(B):
                        ins = nc.tensor.transpose(bt[:, n * P:(n + 1) * P], lp[:, k * B + n, :], identb[:])
                    ins.then_inc(lp_ps, 1)
                pe.wait_ge(lpT_sb, 2)

            def inside(b, par):
                pe.wait_ge(p_sb, b * 2 + 2)
                for c in range(C):
                    for g in range(G2):
                        for j in range(HPB):
                            h = g * HPB + j
                            ins = nc.tensor.matmul(bank[6][DV * j:DV * (j + 1), (c * G2 + g) * P:(c * G2 + g + 1) * P],
                                                   vs[:, par, c, h * DV:(h + 1) * DV], pp[:, c, h, :], start=True, stop=True)

            def across(b, par):
                pe.wait_ge(st_sb, b + 1)
                for g in range(G2):
                    for j in range(HPB):
                        h = g * HPB + j
                        ins = nc.tensor.matmul(bank[7][DV * j:DV * (j + 1), g * P:(g + 1) * P],
                                               st[:, h * DV:(h + 1) * DV], gT[:, par, h, P:S], start=True, stop=True)
                ins.then_inc(o_ps, 1)

            def out_proj(b):
                pe.wait_ge(oT_sb, b + 1)
                for c in range(C):
                    for g in range(G2):
                        ins = nc.tensor.matmul(bank[7][:, (2 + c) * P:(3 + c) * P], oT[:, g, c * P:(c + 1) * P], wo[:, g, :],
                                               start=(g == 0), stop=(g == G2 - 1))
                ins.then_inc(y_ps, 1)

            def attn(b, par, p1, p2):
                pe.wait_ge(xT_sb, b + 1)
                if p1:
                    pe.wait_ge(g_sb, b * 4)
                for c in range(C):
                    ins = nc.tensor.matmul(bank[4][:, c * H * DV:(c + 1) * H * DV], xT[:, par, c * P:(c + 1) * P],
                                           wvg[:, 0:H * DV], start=True, stop=True)
                ins.then_inc(v_ps, 1)
                if p1:
                    pe.wait_ge(og_sb, b)
                    inside(b - 1, 1 - par)
                    across(b - 1, 1 - par)
                if not p1:
                    pe.wait_ge(am_sb, 1)
                for r in range(4):
                    if not p1 and r == 2:
                        running_sums()
                    if r == 1:
                        pe.wait_ge(v_sb, b + 1)
                    if r >= 2:
                        pe.wait_ge(g_sb, b * 4 + r - 1)
                    for k in range(2):
                        ins = nc.tensor.matmul(bank[5 - r % 2][:, k * S:(k + 1) * S], amat[:, 2 * r + k, :], xT[:, par, :],
                                               start=True, stop=True)
                    ins.then_inc(g_ps, 1)

                def decay(c):
                    if p1 or c:
                        pe.wait_ge(d_sb, b * 2 + c)
                    chunk = bass.ds(b * 2 + c, 1)
                    pe.wait_ge(to_sb, b * 2 + c + 1)
                    for k in range(2):
                        nc.tensor.matmul(bank[2 + k][:, :], fromT[:, chunk, :].rearrange("p a s -> p (a s)"),
                                         toT[:, c, 4 * k:4 * k + 4, :], start=True, stop=True)
                        ins = nc.tensor.matmul(bank[2 + k][:, :].rearrange("p (h t) -> p h t", h=4)[:, :, 0:P // 2],
                                               identb[0:P // 2, :], shut[0:P // 2, 0:P // 2].unsqueeze(1).to_broadcast([P // 2, 4, P // 2]),
                                               start=False, stop=True, skip_group_check=True)
                    ins.then_inc(ax_ps, 1)

                def scores(c):
                    if p1 or c:
                        pe.wait_ge(p_sb, b * 2 + c)
                    for k in range(2):
                        ins = nc.tensor.matmul(bank[k][:, :], xT[:, par, c * P:(c + 1) * P],
                                               gT[:, par, 4 * k:4 * k + 4, c * P:(c + 1) * P], start=True, stop=True)
                    ins.then_inc(s_ps, 1)

                if not p1:
                    sums_by_row()
                decay(0)
                if p1:
                    out_proj(b - 1)
                pe.wait_ge(g_sb, b * 4 + 4)
                if not p1:
                    pe.wait_ge(lpT2_sb, 1)
                scores(0)
                if p1:
                    pe.wait_ge(r1_sb, b)
                nc.tensor.matmul(bank[7][:, 256:256 + H], fromT[:, bass.ds(b * 2, 1), :].rearrange("p a s -> p (a s)"),
                                 toT[:, 0, :, P - 1], start=True, stop=True)
                for g in range(G2):
                    ins = nc.tensor.matmul(bank[7][:, g * P:(g + 1) * P], headv[:, g * P:(g + 1) * P],
                                           lpT[:, bass.ds(b * 2 + 1, 1), :].rearrange("p a t -> p (a t)"), start=True, stop=True)
                ins.then_inc(we_ps, 1)
                decay(1)
                if p1:
                    pe.wait_ge(oT_sb, b)
                for g in range(G2):
                    ins = nc.tensor.matmul(bank[6][:, g * S:(g + 1) * S], wog[:, g * P:(g + 1) * P], xT[:, par, :],
                                           start=True, stop=True)
                ins.then_inc(og_ps, 1)
                scores(1)
                pe.wait_ge(vw_sb, b + 1)
                pe.wait_ge(x_in[par], loads(b, par))
                pe.wait_ge(we_sb, b + 1)
                nc.tensor.matmul(bank[7][:, 0:H * DV], xs[:, par, 0, :], vw[:], start=True, stop=True).then_inc(st_ps, 1)

            batches(pe, attn)
            pe.wait_ge(og_sb, B)
            inside(B - 1, (B - 1) % 2)
            across(B - 1, (B - 1) % 2)
            out_proj(B - 1)

            pe.wait_ge(wf_sb, 1)
            pe.wait_ge(w2_in, 16 * 6)
            pe.wait_ge(r1_sb, B)

            def score_half(i, par, g, half_):
                for q in (2 * half_, 2 * half_ + 1):
                    for c in range(C):
                        ins = nc.tensor.matmul(bank[q][:, c * S:(c + 1) * S],
                                               km[32 * q:32 * q + 32, par, g, c * P:(c + 1) * P],
                                               qn[32 * q:32 * q + 32, par, :], start=True, stop=True)
                ins.then_inc(sc_ps, 1)

            def score(i, par, g):
                pe.wait_ge(km_sb, i * QG + g + 1)
                for half_ in range(2):
                    n = i * 8 + 2 * g + half_ - 1
                    if not (isinstance(n, int) and n < 1):
                        pe.wait_ge(e_sb, n)
                    score_half(i, par, g, half_)

            def values(i, par, g):
                if g == 0:
                    pe.wait_ge(va_sb, i + 1)
                pe.wait_ge(e_sb, i * 8 + 2 * g + 2)
                if g == 2:
                    pe.wait_ge(tr_sb, i * 2 + 1)
                if g == 0 and not (isinstance(i, int) and i < 1):
                    pe.wait_ge(tr_sb, i * 2)
                for c in range(C):
                    for q in range(4):
                        ins = nc.tensor.matmul(bank[4][32 * q:32 * q + 32, (g % 2) * S:(g % 2 + 1) * S],
                                               va[:, par, c, 4 * q + g, :], ee[:, g % 2, q, c, :],
                                               start=(c == 0), stop=(c == C - 1), skip_group_check=True)
                ins.then_inc(pv_ps, 1)

            def step(i, par):
                ahead, core, behind, experts = parts(i)
                aa, cc, mm = i + 1, i - 1, i - 2

                def up(k):
                    bk = up_bank(i, k)
                    for n in range(2):
                        ins = nc.tensor.matmul(bank[bk][:, n * S:(n + 1) * S], wup[:, k, n, :], x3T[:, par, :], start=True, stop=True)
                    ins.then_inc(up_ps, 1)

                def spread(k):
                    for n in range(2):
                        ins = nc.tensor.matmul(bank[spread_bank(i, k)][:, n * S:(n + 1) * S], eselb[:, (2 * k + n) * P:(2 * k + n + 1) * P],
                                               cT[:], start=True, stop=True)
                    ins.then_inc(cB_ps, 1)

                if core:
                    score(i, par, 0)
                if experts:
                    up(0)
                if ahead:
                    pe.wait_ge(q8_sb, i + 2 if isinstance(i, int) and i <= 1 else 4)
                    if not (isinstance(i, int) and i < 0):
                        pe.wait_ge(vv_sb, aa)
                    if behind and not (isinstance(i, int) and i < 2):
                        pe.wait_ge(lg_rd, cc)
                    bt = bank[5][:, 0:P].bitcast(BF16)
                    for c in range(C):
                        ins = nc.tensor.transpose(bt[:, c * P:(c + 1) * P],
                                                  q8[:, bass.ds(aa * 2 + c, 1), :].rearrange("p a d -> p (a d)"), identb[:])
                    ins.then_inc(q8T_ps, 1)
                if behind:
                    values(cc, 1 - par, 3)
                if ahead:
                    pe.wait_ge(q8T_sb, aa + 1)
                    for c in range(C):
                        ins = nc.tensor.matmul(bank[5][:, c * P:(c + 1) * P], q8T[:, c * P:(c + 1) * P], wfT[:],
                                               start=True, stop=True)
                    ins.then_inc(f_ps, 1)
                if experts:
                    wait_apart(pe, dn_rd, mm + 1, (c_in, 32))
                    up(1)
                if core:
                    score(i, par, 1)
                    values(i, par, 0)
                if experts:
                    if up_bank(i, 2) == up_bank(i, 0):
                        pe.wait_ge(hb_sb, mm * NBLK + 1)
                    up(2)
                    if alone(i):
                        up(3)
                        up(4)
                if behind:
                    pe.wait_ge(aT_sb, cc + 1)
                    if ahead:
                        pe.wait_ge(f_rd, aa + 1)
                    else:
                        pe.wait_ge(vv_sb, B)
                        pe.wait_ge(lg_rd, cc)
                    for c in range(C):
                        ins = nc.tensor.matmul(bank[5][:, c * P:(c + 1) * P], aT[:, c * P:(c + 1) * P], wqkvo[:, 3, :],
                                               start=True, stop=True)
                    ins.then_inc(w_ps, 1)
                if experts:
                    block1 = mm * NBLK + 2 if isinstance(mm, int) else pe.to_reg(mm * NBLK + 2)
                    wait_apart(pe, c3_sb, mm + 1, (c_in, 32))
                    if up_bank(i, 1) == 6:
                        pe.wait_ge(hb_sb, block1)
                    ct = bank[6][:, 0:P].bitcast(BF16)
                    for c in range(C):
                        ins = nc.tensor.transpose(ct[0:3 * NE, c * P:(c + 1) * P], comb3[:, c].rearrange("p k e -> p (k e)"), identb[:])
                    ins.then_inc(cT_ps, 1)
                    pe.wait_ge(cT_sb, mm + 1)
                    spread(0)
                if core and not experts:
                    score(i, par, 2)
                if ahead:
                    pe.wait_ge(x2_sb, aa + 1)
                    if behind:
                        pe.wait_ge(w_rd, cc + 1)
                    for c in range(C):
                        ins = nc.tensor.transpose(bank[5][:, c * P:(c + 1) * P], arA[:, c, :], ident)
                    ins.then_inc(x2T_ps, 1)
                if core and experts:
                    score(i, par, 2)
                if ahead:
                    pe.wait_ge(x2T_sb, aa + 1)
                    for n in range(2):
                        ins = nc.tensor.matmul(bank[5][:, n * S:(n + 1) * S], wqkvo[:, n, :], x2T[:], start=True, stop=True)
                    ins.then_inc(qk_ps, 1)
                if core:
                    values(i, par, 1)
                if experts:
                    if not alone(i - 1):
                        pe.wait_ge(cB_sb, mm * 2 + 1)
                    else:
                        pe.wait_ge(lg_rd, B)
                    spread(1)
                    if not alone(i):
                        pe.wait_ge(hb_sb, mm * NBLK + 3)
                        up(3)
                if ahead:
                    pe.wait_ge(qk_sb, aa + 1)
                    for c in range(C):
                        ins = nc.tensor.matmul(bank[5][:, c * P:(c + 1) * P], x2T[:, c * P:(c + 1) * P], wqkvo[:, 2, :],
                                               start=True, stop=True)
                    ins.then_inc(vv_ps, 1)
                if experts and not alone(i):
                    pe.wait_ge(cB_sb, mm * 2 + 2)
                    up(4)
                if core and not experts:
                    score(i, par, 3)
                if behind:
                    pe.wait_ge(x3_sb, cc + 1)
                    if ahead:
                        pe.wait_ge(vv_sb, aa + 1)
                    for c in range(C):
                        ins = nc.tensor.transpose(bank[5][:, c * P:(c + 1) * P], crA[:, 1 - par, c, :], ident)
                    ins.then_inc(x3T_ps, 1)
                if core and experts:
                    score(i, par, 3)
                if core:
                    values(i, par, 2)
                if behind:
                    pe.wait_ge(x3T_sb, cc + 1)
                    for c in range(C):
                        ins = nc.tensor.matmul(bank[5][:, c * NE:(c + 1) * NE], x3T[:, 1 - par, c * P:(c + 1) * P], wr[:],
                                               start=True, stop=True)
                    ins.then_inc(lg_ps, 1)
                if experts:
                    pe.wait_ge(hb_sb, mm * NBLK + 5)
                    pe.wait_ge(cB_sb, mm * 2 + 2)
                    for c in range(C):
                        for k in range(NBLK):
                            if c == 0 and k:
                                pe.wait_ge(hc_sb, mm * (NBLK - 1) + k)
                            src = hc if k else hb
                            ins = nc.tensor.matmul(bank[6][:, c * P:(c + 1) * P], src[:, k, c * P:(c + 1) * P], wdn[:, k, :],
                                                   start=(k == 0), stop=(k == NBLK - 1))
                    ins.then_inc(dn_ps, 1)

            steps(pe, step)

        @block.scalar
        def _(act):
            for dst, name in ((wqT, "wqT"), (wkT, "wkT")):
                act.dma_start(dst[:], a[name]).then_inc(wqk_in, 16)
            for dst, name in ((wog, "wog"), (wo, "wo"), (ffw, "ffw")):
                act.dma_start(dst[:], a[name]).then_inc(w_in, 16)

            def take_xTa(k):
                act.wait_ge(x0T_ps, k + 1)
                nc.scalar.activation(xTa[:, 2 * k:2 * k + 2, :], bank[k][:, :].rearrange("p (b t) -> p b t", b=2), ACT.Copy)\
                    .then_inc(x0T_sb, 1)

            for k in range(B // 4):
                take_xTa(k)
            act.wait_ge(am_ps, 1)
            for k in range(2):
                ins = nc.scalar.activation(amat[:, 4 * k:4 * k + 4, :], bank[5 + k][:, :].rearrange("p (h d) -> p h d", h=4),
                                           ACT.Copy, scale=float(P) ** -0.5)
            ins.then_inc(am_sb, 1)
            for k in range(B // 4, B // 2):
                take_xTa(k)
            act.wait_ge(z_sb, 1)
            nc.scalar.activation(lz[:, 1], lz[:, 0], ACT.Abs, scale=1.0 / GATE_NORM).then_inc(act_one, 1)
            nc.scalar.activation(lz[:, 3], lz[:, 0], ACT.Relu, scale=-1.0 / GATE_NORM)
            act.wait_ge(act_one, 1)
            nc.scalar.activation(lz[:, 2], lz[:, 1], ACT.Exp, scale=-1.0).then_inc(act_one, 1)
            act.wait_ge(act_one, 2)
            nc.scalar.activation(lz[:, 1], lz[:, 2], ACT.Ln, bias=1.0).then_inc(gate, 1)

            def sums_by_row():
                act.wait_ge(lp_ps, 1)
                bt = bank[0][:, :].bitcast(BF16).rearrange("p (n t) -> p n t", n=B)
                nc.scalar.activation(lpT[:, 0:B, :], bt, ACT.Copy).then_inc(lpT_sb, 1)
                nc.scalar.activation(fromT[:, 0:B, :], bt, ACT.Identity, scale=signs[:, 0:1], bias=signs[:, 1:2]).then_inc(lpT_sb, 1)

            def attn(b, par, p1, p2):
                act.wait_ge(v_ps, b + 1)
                if p2:
                    act.wait_ge(o_ps, b - 1)
                    act.wait_ge(vw_sb, b - 1)
                nc.scalar.activation(vs[:, par], bank[4][:, :].rearrange("p (c n) -> p c n", c=C), ACT.Copy).then_inc(v_sb, 1)
                for r in range(4):
                    act.wait_ge(g_ps, b * 4 + r + 1)
                    nc.scalar.activation(gT[:, par, 2 * r:2 * r + 2, :],
                                         bank[5 - r % 2][:, :].rearrange("p (h t) -> p h t", h=2), ACT.Copy).then_inc(g_sb, 1)

                def decay(c):
                    act.wait_ge(ax_ps, b * 2 + c + 1)
                    if p1:
                        act.wait_ge(p_sb, b * 2 + c - 1)
                    for k in range(2):
                        ins = nc.scalar.activation(dd[:, c, 4 * k:4 * k + 4, :],
                                                   bank[2 + k][:, :].rearrange("p (h t) -> p h t", h=4), ACT.Exp)
                    ins.then_inc(d_sb, 1)

                if not p1:
                    sums_by_row()
                decay(0)
                if p1:
                    act.wait_ge(vw_sb, b)
                    act.wait_ge(oT_sb, b)
                act.wait_ge(we_ps, b + 1)
                nc.scalar.activation(wv[:], bank[7][:, 256:256 + H], ACT.Exp)
                nc.scalar.activation(el[:], bank[7][:, 0:256].rearrange("p (g t) -> p g t", g=G2), ACT.Exp).then_inc(we_sb, 1)
                decay(1)
                act.wait_ge(og_ps, b + 1)
                nc.scalar.activation(ogt[:], bank[6][:, :].rearrange("p (g t) -> p g t", g=G2), ACT.Tanh, scale=0.5)\
                    .then_inc(og_sb, 1)
                act.wait_ge(st_ps, b + 1)
                if p1:
                    act.wait_ge(o_ps, b)
                nc.scalar.activation(st[:], bank[7][:, 0:H * DV], ACT.Copy).then_inc(st_sb, 1)

            batches(act, attn)

            def exps(i, par, g, halves=(0, 1)):
                n = i * 4 + g - 1
                if 0 in halves and not (isinstance(n, int) and n < 1):
                    act.wait_ge(pv_ps, n)
                for h_ in halves:
                    act.wait_ge(sc_ps, i * 8 + 2 * g + h_ + 1)
                    for q in (2 * h_, 2 * h_ + 1):
                        ins = nc.scalar.activation(ee[:, g % 2, q], bank[q][:, :].rearrange("p (c t) -> p c t", c=C),
                                                   ACT.Exp, scale=1.0 / (STEPS * STEPS * float(HD) ** 0.5))
                    ins.then_inc(e_sb, 1)

            def step(i, par):
                ahead, core, behind, experts = parts(i)
                aa, cc, mm = i + 1, i - 1, i - 2

                def tanh(k, bk):
                    act.wait_ge(up_ps, mm * NBLK + k + 1)
                    if k >= 2:
                        act.wait_ge(hb_sb, mm * NBLK + k - 1)
                    nc.scalar.activation(th[:, k % 2], bank[bk][:, 0:S], ACT.Tanh, scale=0.5).then_inc(th_sb, 1)

                def spread(k):
                    act.wait_ge(cB_ps, mm * 2 + k + 1)
                    nc.scalar.activation(cB[:, 2 * k:2 * k + 2], bank[spread_bank(i, k)][:, :].rearrange("p (n t) -> p n t", n=2),
                                         ACT.Copy).then_inc(cB_sb, 1)

                if core:
                    exps(i, par, 0, (0,))
                if experts:
                    tanh(0, up_bank(i, 0))
                if ahead:
                    act.wait_ge(q8T_ps, aa + 1)
                    if not (isinstance(i, int) and i < 0):
                        act.wait_ge(f_ps, aa)
                    nc.scalar.activation(q8T[:], bank[5][:, 0:P].bitcast(BF16), ACT.Copy).then_inc(q8T_sb, 1)
                if core:
                    exps(i, par, 0, (1,))
                if experts:
                    tanh(1, up_bank(i, 1))
                if core:
                    exps(i, par, 1)
                if experts:
                    tanh(2, up_bank(i, 2))
                    if alone(i - 1):
                        tanh(3, up_bank(i, 3))
                        tanh(4, up_bank(i, 4))
                    act.wait_ge(cT_ps, mm + 1)
                    nc.scalar.activation(cT[:], bank[6][0:3 * NE, 0:P].bitcast(BF16), ACT.Copy).then_inc(cT_sb, 1)
                    spread(0)
                if ahead:
                    act.wait_ge(x2T_ps, aa + 1)
                    if not (isinstance(i, int) and i < 0):
                        act.wait_ge(vv_ps, aa)
                    nc.scalar.activation(x2T[:], bank[5][:, 0:S], ACT.Copy).then_inc(x2T_sb, 1)
                if core:
                    exps(i, par, 2)
                if ahead:
                    act.wait_ge(qk_ps, aa + 1)
                    if not (isinstance(i, int) and i < 0):
                        act.wait_ge(qk_n, aa)
                    for n in range(2):
                        ins = nc.scalar.activation(cur[:, n, :], bank[5][:, n * S:(n + 1) * S], ACT.Identity, bias=cols[:, n:n + 1])
                    ins.then_inc(qk_sb, 1)
                if experts:
                    spread(1)
                if experts and not alone(i - 1):
                    tanh(3, up_bank(i, 3))
                    tanh(4, up_bank(i, 4))
                if behind:
                    act.wait_ge(x3T_ps, cc + 1)
                    nc.scalar.activation(x3T[:, 1 - par], bank[5][:, 0:S], ACT.Copy).then_inc(x3T_sb, 1)
                if core:
                    exps(i, par, 3)
                if ahead:
                    act.wait_ge(qk_n, aa + 1)
                    if not (isinstance(aa, int) and aa < 2):
                        act.wait_ge(pv_ps, aa * 4 - 4)
                    for g in range(QG):
                        nc.scalar.activation(km[:, 1 - par, g], kn[:], ACT.Copy, scale=gmask[:, g:g + 1]).then_inc(km_sb, 1)
                if behind:
                    act.wait_ge(k_top, cc * 6 + 2)
                    nc.scalar.activation(lg[:, 2], lg[:, 1], ACT.Exp).then_inc(lge, 1)

            steps(act, step)

        @block.gpsimd
        def _(gp):
            nc.gpsimd.memset(half[:], -0.5).then_inc(half_sb, 1)
            nc.gpsimd.memset(va[:], 0.0).then_inc(half_sb, 1)
            gp.wait_ge(half_sb, 2)
            nc.gpsimd.memset(va[:, :, :, :, HD:HD + 1], float(STEPS)).then_inc(half_sb, 1)
            gp.wait_ge(half_sb, 3)
            def take_xT(b, par, p1, p2):
                if p2:
                    wait_apart(gp, s_ps, b * 2 - 2, (half_sb, 3))
                nc.gpsimd.tensor_copy(xT[:, par, :], xTa[:, bass.ds(b, 1), :].rearrange("p a t -> p (a t)")).then_inc(xT_sb, 1)

            gp.wait_ge(x0T_sb, 1)
            take_xT(0, 0, False, False)
            gp.wait_ge(wmax, 1)
            nc.gpsimd.partition_all_reduce(sw[:, 1:2], sw[:, 0:1], P, RMAX).then_inc(wmax_all, 1)

            gp.wait_ge(la_sb, 1)

            def rsqrt(var, tmp, dst, chain, done):
                chain(nc.gpsimd.tensor_scalar(tmp, var, EPS, None, ALU.add))
                nc.gpsimd.tensor_tensor(dst, tmp, half[:, 0:C], ALU.pow).then_inc(done, 1)

            def sums_to(b, c):
                if c == 0:
                    wait_apart(gp, we_ps, b, (to_sb, 2))
                else:
                    wait_apart(gp, ax_ps, b * 2, (to_sb, 2))
                nc.gpsimd.tensor_tensor(toT[32:64, c], lpT[32:64, bass.ds(b * 2 + c, 1), :].rearrange("p a t -> p (a t)")
                                        .unsqueeze(1).to_broadcast([32, H, P]),
                                        head_of[32:64].unsqueeze(2).to_broadcast([32, H, P]), ALU.mult).then_inc(to_sb, 1)

            def norm1(b):
                wait_apart(gp, mv_sb, b + 1, (half_sb, 3))
                ch = Chain(gp, c_pow, b, 1)
                rsqrt(mv[:, :, 1], rstd[:, 0], rstd[:, 1], ch, rstd_sb)
                ch.end()

            def attn(b, par, p1, p2):
                if p1:
                    take_xT(b, par, p1, p2)
                    wait_apart(gp, xT_sb, b + 1, (lpT2_sb, 1))
                    sums_to(b, 0)
                    sums_to(b, 1)
                    wait_apart(gp, to_sb, b * 2 + 2, (lpT2_sb, 1))
                if p1:
                    norm1(b - 1)
                gp.wait_ge(we_sb, b + 1)
                gp.wait_ge(v_sb, b + 1)
                if p1:
                    gp.wait_ge(st_ps, b)
                nc.gpsimd.tensor_tensor(vw[:].rearrange("p (h v) -> p h v", h=H),
                                        vs[:, par, 0, :].rearrange("p (h v) -> p h v", h=H),
                                        wv[:].unsqueeze(2).to_broadcast([P, H, DV]), ALU.mult).then_inc(vw_sb, 1)

            batches(gp, attn)
            norm1(B - 1)
            gp.wait_ge(xmax, 1)
            nc.gpsimd.partition_all_reduce(sx[:, 1:2], sx[:, 0:1], P, RMAX).then_inc(xmax_all, 1)

            def step(i, par):
                ahead, core, behind, experts = parts(i)
                aa, cc, mm = i + 1, i - 1, i - 2

                def weigh(k):
                    gp.wait_ge(hb_sb, mm * NBLK + k + 1)
                    gp.wait_ge(cB_sb, mm * 2 + (k - 1) // 2 + 1)
                    nc.gpsimd.tensor_tensor(hc[:, k], hb[:, k], cB[:, k - 1], ALU.mult).then_inc(hc_sb, 1)

                def parts_of_weights(n):
                    wait_apart(gp, cmb_sb, n + 1, (half_sb, 3))
                    ch = Chain(gp, k_c3, n, 3)
                    ch(nc.gpsimd.tensor_copy(comb3[:, :, 0], comb[:]))
                    ch(nc.gpsimd.tensor_tensor(crest[:], comb[:], comb3[:, :, 0], ALU.subtract), met=(half_sb, 3))
                    ch(nc.gpsimd.tensor_copy(comb3[:, :, 1], crest[:]))
                    nc.gpsimd.tensor_tensor(comb3[:, :, 2], crest[:], comb3[:, :, 1], ALU.subtract).then_inc(c3_sb, 1)
                    ch.end()

                if experts and not alone(i - 1):
                    parts_of_weights(mm)
                if ahead:
                    wait_apart(gp, amv_sb, aa + 1, (half_sb, 3))
                    rsqrt(amv[:, :, 1], ars[:, 0], ars[:, 1], Chain(gp, k_pa, aa, 1), ars_sb)
                if experts and not alone(i):
                    weigh(1)
                if ahead:
                    wait_apart(gp, x2_sb, aa + 1, (half_sb, 3))
                    nc.gpsimd.tensor_tensor(xa[:, bass.ds(aa * 2, 2), :], arA[:], ob_r.unsqueeze(1).to_broadcast([P, C, D]),
                                            ALU.add).then_inc(xo_sb, 1)
                if behind:
                    wait_apart(gp, cmv_sb, cc + 1, (half_sb, 3))
                    rsqrt(cmv[:, :, 1], crs[:, 0], crs[:, 1], Chain(gp, k_pc, cc, 1), crs_sb)
                if experts and not alone(i - 1):
                    for k in range(1 if alone(i) else 2, NBLK):
                        weigh(k)
                if alone(i) and behind:
                    parts_of_weights(cc)
                if experts:
                    wait_apart(gp, dmv_sb, mm + 1, (half_sb, 3))
                    ch = Chain(gp, k_pd, mm, 2)
                    ch(nc.gpsimd.tensor_scalar(drs[:, 0], dmv[:, :, 1], EPS, None, ALU.add))
                    ch(nc.gpsimd.tensor_tensor(drs[:, 1], drs[:, 0], half[:, 0:C], ALU.pow), met=(half_sb, 3))
                    ch.end()
                if experts and not (isinstance(mm, int) and mm == B - 1):
                    wait_apart(gp, yo_free, mm + 1, (half_sb, 3))
                    for c in range(C):
                        ins = nc.gpsimd.tensor_scalar(yo[:, par, c:c + 1, :], drA[:, c:c + 1, :], dmv[:, c, 0:1], drs[:, 1, c:c + 1],
                                                      ALU.subtract, ALU.mult)
                    ins.then_inc(yo_sb, 1)

            steps(gp, step)

        @block.vector
        def _(dve):
            V = nc.vector

            def quantize(ch, src, scale, y, m, dst):
                ch(V.tensor_scalar(y, src, scale, FP8_MAX, ALU.mult, ALU.min))
                ch(V.tensor_scalar(m.bitcast(U32), y.bitcast(U32), 0x7F800000, None, ALU.bitwise_and))
                ch(V.tensor_scalar(m, m, 2.0 ** -6, 1.5 * 2.0 ** 20, ALU.max, ALU.mult))
                ch(V.scalar_tensor_tensor(y, y, -FP8_MAX, m, ALU.max, ALU.add))
                return V.tensor_tensor(dst, y, m, ALU.subtract)

            def scale_of(ch, s):
                ch(V.tensor_scalar(s[:, 0:1], s[:, 1:2], 1e-12, None, ALU.max))
                ch(V.reciprocal(s[:, 1:2], s[:, 0:1]))
                ch(V.tensor_scalar(s[:, 2:3], s[:, 1:2], FP8_MAX, FP8_MAX, ALU.mult, ALU.min))
                ch.link(V.reciprocal(s[:, 3:4], s[:, 2:3]))

            one = Chain(dve, dve_one, 0, 100)
            dve.wait_ge(cst_in, 16)
            one(V.tensor_scalar(shut[:], later, -1e30, None, ALU.mult))
            one(V.memset(headv[:], 0.0))
            V.tensor_copy(headv[0:32].rearrange("p (h v) -> p h v", h=H), head_of[0:32].unsqueeze(2).to_broadcast([32, H, DV]))
            for c in range(C):
                V.tensor_copy(toT[0:P // 2, c], head_of[0:P // 2].unsqueeze(2).to_broadcast([P // 2, H, P]))
            V.tensor_copy(identb[:], ident).then_inc(ident_sb, 1)
            for c in range(C):
                V.tensor_copy(toT[P // 2:P, c], shut[P // 2:P].unsqueeze(1).to_broadcast([P // 2, H, P]))
            V.memset(two8[:], -FLT_MAX)
            one(V.memset(lp[:, :, 0:P // 2], 0.0))
            V.tensor_copy(lp[:, :, P // 2:P], ident[:, P // 2:P].unsqueeze(1).to_broadcast([P, B * C, P // 2]))
            dve.wait_ge(c_in, 32)
            dve.wait_ge(z_ps, 1)
            V.tensor_tensor(lz[:, 0], bank[7][:, 0:B * C * H].rearrange("p (n h) -> p n h", h=H),
                            bg_r.unsqueeze(1).to_broadcast([P, B * C, H]), ALU.add).then_inc(z_sb, 1)
            dve.wait_ge(w_in, 16 * 3)
            one(V.tensor_scalar(wo[:], wo[:], 0.5, None, ALU.mult))
            V.tensor_reduce(sw[:, 0:1], ffw[:], AX.X, ALU.max, apply_absolute_value=True).then_inc(wmax, 1)
            dve.wait_ge(gate, 1)
            V.scalar_tensor_tensor(la[:], lz[:, 3], -1.0, lz[:, 1], ALU.mult, ALU.subtract).then_inc(la_sb, 1)
            dve.wait_ge(cum_ps, 1)
            l32 = bank[7][:, 0:B * C * H].rearrange("p (n h) -> p n h", h=H)
            one(V.tensor_copy(lp[:, :, 0:H], l32))
            one(V.tensor_tensor(cum[:, 0], l32, lp[:, :, 0:H], ALU.subtract))
            one(V.tensor_copy(lp[:, :, H:2 * H], cum[:, 0]))
            one(V.tensor_tensor(cum[:, 1], cum[:, 0], lp[:, :, H:2 * H], ALU.subtract))
            one(V.tensor_copy(lp[:, :, 2 * H:3 * H], cum[:, 1]))
            V.tensor_copy(lp[:, :, 32:32 + 3 * H], lp[:, :, 0:3 * H]).then_inc(lp_sb, 1)

            def first_sums_to(c):
                V.tensor_tensor(toT[32:64, c], lpT[32:64, c, :].unsqueeze(1).to_broadcast([32, H, P]),
                                head_of[32:64].unsqueeze(2).to_broadcast([32, H, P]), ALU.mult).then_inc(to_sb, 1)

            dve.wait_ge(lpT_sb, 1)
            first_sums_to(0)
            dve.wait_ge(lp_ps, 2)
            bt = bank[1][:, :].bitcast(BF16).rearrange("p (n t) -> p n t", n=B)
            V.tensor_copy(lpT[:, B:2 * B, :], bt)
            V.tensor_scalar(fromT[:, B:2 * B, :], bt, signs[:, 0:1], signs[:, 1:2], ALU.mult, ALU.add).then_inc(lpT2_sb, 1)
            first_sums_to(1)

            def stats(ch, r, bnb, mvb, mv_done):
                for c in range(C):
                    ins = V.bn_stats(bnb[:, c, :], r[:, c, :])
                ch(ins, met=(c_in, 32))
                for c in range(C):
                    ins = V.bn_aggr(mvb[:, c, :], bnb[:, c, :])
                ins.then_inc(mv_done, 1)

            def scaled(r, mvb, rs_, rs_ready, index, to):
                dve.wait_ge(rs_ready, index + 1)
                for c in range(C):
                    ins = V.tensor_scalar(to(c), r[:, c:c + 1, :], mvb[:, c, 0:1], rs_[:, 1, c:c + 1], ALU.subtract, ALU.mult)
                return ins

            def ffn_weight():
                dve.wait_ge(wmax_all, 1)
                scale_of(one, sw)
                quantize(one, ffw[:], sw[:, 2:3], wq_t[:, 0], wq_t[:, 1], wfT[:])
                dve.wait_ge(w2_in, 16 * 6)
                V.tensor_copy(eselb[:], esel[:])
                V.tensor_scalar(wdn[:, 0, :], wdn[:, 0, :], 0.5, None, ALU.mult).then_inc(wf_sb, 1)

            def gate_out(b):
                dve.wait_ge(o_ps, b + 1)
                dve.wait_ge(we_sb, b + 1)
                dve.wait_ge(og_sb, b + 1)
                ch = Chain(dve, c_oT, b, 2)
                intra = bank[6][:, :].rearrange("p (c g t) -> p c g t", c=C, g=G2)
                ch.link(V.tensor_tensor(t0[:], bank[7][:, 0:256].rearrange("p (g t) -> p g t", g=G2), el[:], ALU.mult))
                V.scalar_tensor_tensor(oT[:, :, 0:P], ogt[:, :, 0:P], 1.0, intra[:, 0], ALU.add, ALU.mult)
                ch.meet()
                ch(V.tensor_tensor(t1[:], t0[:], intra[:, 1], ALU.add))
                V.scalar_tensor_tensor(oT[:, :, P:S], ogt[:, :, P:S], 1.0, t1[:], ALU.add, ALU.mult).then_inc(oT_sb, 1)
                ch.end()

            def residual(b, par):
                dve.wait_ge(y_ps, b + 1)
                V.tensor_tensor(rs[:], bank[7][:, 256:512].rearrange("p (c d) -> p c d", c=C), xs[:, par], ALU.add)\
                    .then_inc(r1_sb, 1)
                dve.wait_ge(r1_sb, b + 1)
                ch = Chain(dve, c_ln, b, 3)
                stats(ch, rs, bn, mv, mv_sb)
                return ch

            def normal(b, ch):
                ch(scaled(rs, mv, rstd, rstd_sb, b, lambda c: xa[:, bass.ds(b * 2 + c, 1), :]))
                ch.link(V.tensor_reduce(amax[:, bass.ds(b, 1)], xa[:, bass.ds(b * 2, 2), :], AX.XY, ALU.max,
                                        apply_absolute_value=True))
                ch.end()

            def attn(b, par, p1, p2):
                if p1:
                    gate_out(b - 1)
                    ch = residual(b - 1, 1 - par)
                for c in range(C):
                    dve.wait_ge(s_ps, b * 2 + c + 1)
                    dve.wait_ge(d_sb, b * 2 + c + 1)
                    for k in range(2):
                        ins = V.tensor_tensor(pp[:, c, 4 * k:4 * k + 4, :], bank[k][:, :].rearrange("p (h t) -> p h t", h=4),
                                              dd[:, c, 4 * k:4 * k + 4, :], ALU.mult)
                    ins.then_inc(p_sb, 1)
                    if p1 and c == 0:
                        normal(b - 1, ch)
                if not p1:
                    ffn_weight()

            batches(dve, attn)
            gate_out(B - 1)
            normal(B - 1, residual(B - 1, (B - 1) % 2))

            dve.wait_ge(c_ln, B * 3)
            V.tensor_reduce(sx[:, 0:1], amax[:, 0:B], AX.X, ALU.max).then_inc(xmax, 1)
            dve.wait_ge(xmax_all, 1)
            scale_of(one, sx)
            dve.wait_ge(half_sb, 3)

            thr = lif_thresholds()

            def quant(n, b0, b1):
                y, m = (gT[:, k].rearrange("p h t -> p (h t)")[:, 0:(b1 - b0) * S].rearrange("p (c d) -> p c d", d=D)
                        for k in range(2))
                ch = Chain(dve, k_q, n, 4)
                quantize(ch, xa[:, b0 * C:b1 * C, :], sx[:, 2:3], y, m, q8[:, b0 * C:b1 * C, :]).then_inc(q8_sb, 1)
                ch.end()

            def take_ffn(aa):
                dve.wait_ge(f_ps, aa + 1)
                V.scalar_tensor_tensor(fb[:], bank[5][:, 0:S].rearrange("p (c d) -> p c d", c=C), scl[:, 0:1],
                                       fb_r.unsqueeze(1).to_broadcast([P, C, D]), ALU.mult, ALU.add).then_inc(f_rd, 1)

            def ffn_end(aa):
                if not (isinstance(aa, int) and aa < 1):
                    dve.wait_ge(x2T_ps, aa)
                    dve.wait_ge(xo_sb, aa)
                scaled(qy, amv, ars, ars_sb, aa, lambda c: arA[:, c:c + 1, :]).then_inc(x2_sb, 1)

            def take_v(aa):
                dve.wait_ge(vv_ps, aa + 1)
                V.tensor_tensor(cur[:, 2, :].rearrange("p (c d) -> p c d", c=C),
                                bank[5][:, 0:S].rearrange("p (c d) -> p c d", c=C),
                                vb_r.unsqueeze(1).to_broadcast([P, C, D]), ALU.add).then_inc(vv_sb, 1)

            def over(n, lo, hi):
                to, before = (n1, n2) if n % 2 == 0 else (n2, n1)
                if n == 0:
                    return V.tensor_scalar(to[:, lo:hi], cur[:, lo:hi], thr[0], None, ALU.is_gt)
                return V.scalar_tensor_tensor(to[:, lo:hi], cur[:, lo:hi], thr[n], before[:, lo:hi], ALU.is_gt, ALU.add)

            def spikes_qk(aa, par):
                if not (isinstance(aa, int) and aa < 2):
                    dve.wait_ge(sc_ps, aa * 8 - 8)
                if not (isinstance(aa, int) and aa < 1):
                    dve.wait_ge(km_sb, aa * QG)
                V.scalar_tensor_tensor(qn[:, par], cur[:, 0], thr[3], n1[:, 0], ALU.is_gt, ALU.add)
                V.scalar_tensor_tensor(kn[:], cur[:, 1], thr[3], n1[:, 1], ALU.is_gt, ALU.add).then_inc(qk_n, 1)

            def spikes_v(aa, par):
                if not (isinstance(aa, int) and aa < 2):
                    dve.wait_ge(pv_ps, aa * 4 - 4)
                V.scalar_tensor_tensor(va[:, par, :, :, 0:HD], cur[:, 2].rearrange("p (c h d) -> p c h d", c=C, h=NH), thr[3],
                                       n1[:, 2].rearrange("p (c h d) -> p c h d", c=C, h=NH), ALU.is_gt, ALU.add)\
                    .then_inc(va_sb, 1)

            def turn(i, pair):
                dve.wait_ge(pv_ps, i * 4 + 2 * pair + 2)
                if not (isinstance(i, int) and i < 1):
                    dve.wait_ge(aT_sb, i)
                V.transpose(tq[:, 2 * pair:2 * pair + 2].rearrange("p g b r -> p (g b r)"), bank[4][:, :]).then_inc(tr_sb, 1)

            def attention_sum(cc):
                dve.wait_ge(w_ps, cc + 1)
                dve.wait_ge(xo_sb, cc + 1)
                V.tensor_tensor(cr[:], bank[5][:, 0:S].rearrange("p (c d) -> p c d", c=C), xa[:, bass.ds(cc * 2, 2), :], ALU.add)\
                    .then_inc(w_rd, 1)

            def project_b(cc, par):
                scaled(cr, cmv, crs, crs_sb, cc, lambda c: crA[:, par, c:c + 1, :]).then_inc(x3_sb, 1)

            def per_token(t):
                return t.unsqueeze(2).to_broadcast([P, C, NE])

            def route_begin(cc):
                dve.wait_ge(lg_ps, cc + 1)
                V.tensor_copy(lg[:, 0], bank[5][:, 0:C * NE].rearrange("p (c e) -> p c e", c=C)).then_inc(lg_rd, 1)

            def route_largest(cc):
                wait_apart(dve, lg_rd, cc + 1, (c_in, 32))
                for c in range(C):
                    ins = V.max(m8[:, c, :], lg[:, 0, c, :])
                return ins

            def route_less():
                V.tensor_copy(two8[:, :, 0:2], m8[:, :, 0:2])
                return V.tensor_tensor(lg[:, 1], lg[:, 0], per_token(m8[:, :, 0]), ALU.subtract)

            def route_mark():
                for c in range(C):
                    ins = V.match_replace(lg[:, 4, c, :], two8[:, c, :], lg[:, 0, c, :], FLT_MAX)
                return ins

            def route_pick(cc):
                dve.wait_ge(lge, cc + 1)
                V.tensor_reduce(ls[:, 0], lg[:, 2], AX.X, ALU.add)
                return V.scalar_tensor_tensor(lg[:, 3], lg[:, 4], FLT_MAX, lg[:, 2], ALU.is_ge, ALU.mult)

            def route_sum():
                return V.tensor_reduce(ls[:, 1], lg[:, 3], AX.X, ALU.add)

            def route_norm():
                return V.scalar_tensor_tensor(ls[:, 2], ls[:, 0], 1e-9, ls[:, 1], ALU.mult, ALU.add)

            def route_inverse():
                return V.reciprocal(ls[:, 3], ls[:, 2])

            def route_weights():
                V.scalar_tensor_tensor(comb[:], lg[:, 3], 0.5, per_token(ls[:, 3]), ALU.mult, ALU.mult).then_inc(cmb_sb, 1)

            def gated(cc, k, bk):
                dve.wait_ge(th_sb, cc * NBLK + k + 1)
                V.scalar_tensor_tensor(ha[:, k % 2], th[:, k % 2], 1.0, bank[bk][:, 0:S], ALU.add, ALU.mult)\
                    .then_inc(k_d, 1)

            def hidden(cc, k, bk):
                dve.wait_ge(k_d, cc * NBLK + k + 1)
                V.tensor_tensor(hb[:, k], ha[:, k % 2], bank[bk][:, S:2 * S], ALU.mult).then_inc(hb_sb, 1)

            def weigh(mm, k):
                dve.wait_ge(hb_sb, mm * NBLK + k + 1)
                dve.wait_ge(cB_sb, mm * 2 + (k - 1) // 2 + 1)
                V.tensor_tensor(hc[:, k], hb[:, k], cB[:, k - 1], ALU.mult).then_inc(hc_sb, 1)

            def expert_sum(mm, par):
                dve.wait_ge(dn_ps, mm + 1)
                if not (isinstance(mm, int) and mm < 1):
                    dve.wait_ge(yo_sb, mm)
                V.tensor_tensor(drA[:], bank[6][:, 0:S].rearrange("p (c d) -> p c d", c=C), crA[:, par], ALU.add).then_inc(dn_rd, 1)

            def means(r, bnb):
                for c in range(C):
                    ins = V.bn_stats(bnb[:, c, :], r[:, c, :])
                return ins

            def variances(mvb, bnb, mv_done):
                for c in range(C):
                    ins = V.bn_aggr(mvb[:, c, :], bnb[:, c, :])
                ins.then_inc(mv_done, 1)

            def step(i, par):
                ahead, core, behind, experts = parts(i)
                aa, cc, mm = i + 1, i - 1, i - 2
                if experts:
                    route = Chain(dve, k_up, mm, 1)
                    gated(mm, 0, up_bank(i, 0))
                    dve.wait_ge(k_top, mm * 6 + 6)
                    route.link(route_inverse())
                    hidden(mm, 0, up_bank(i, 0))
                    route.meet()
                    route_weights()
                    route.end()
                if ahead:
                    take_ffn(aa)
                if behind:
                    turn(cc, 1)
                if ahead:
                    links = Chain(dve, k_a, aa, 2)
                    dve.wait_ge(f_rd, aa + 1)
                    links.link(V.tensor_tensor(qy[:], fb[:], xa[:, bass.ds(aa * 2, 2), :], ALU.add))
                if behind:
                    heads = Chain(dve, k_n, cc, 2)
                    dve.wait_ge(tr_sb, cc * 2 + 2)
                    heads.link(V.reciprocal(rd[:], tq[:, :, :, HD]))
                if ahead:
                    links.meet()
                    links.link(means(qy, abn))
                if behind:
                    heads.meet()
                    heads.link(V.tensor_tensor(on[:].rearrange("p b g d -> p g b d"), tq[:, :, :, 0:HD],
                                               rd[:].unsqueeze(3).to_broadcast([P, QG, C * 4, HD]), ALU.mult))
                if ahead:
                    wait_apart(dve, k_a, aa * 2 + 2, (c_in, 32))
                    variances(amv, abn, amv_sb)
                    links.end()
                if behind:
                    heads.meet()
                    V.transpose(aT[:], on[:].rearrange("p b g d -> p (b g d)")).then_inc(aT_sb, 1)
                    heads.end()
                if experts:
                    gated(mm, 1, up_bank(i, 1))
                    hidden(mm, 1, up_bank(i, 1))
                if ahead:
                    ffn_end(aa)
                if behind:
                    attention_sum(cc)
                if experts:
                    gated(mm, 2, up_bank(i, 2))
                if behind:
                    rest = Chain(dve, k_c, cc, 1)
                    dve.wait_ge(w_rd, cc + 1)
                    rest.link(means(cr, cbn))
                if experts:
                    hidden(mm, 2, up_bank(i, 2))
                if behind:
                    wait_apart(dve, k_c, cc + 1, (c_in, 32))
                    variances(cmv, cbn, cmv_sb)
                    rest.end()
                    project_b(cc, 1 - par)
                if isinstance(i, int) and i == 0:
                    quant(2, 2, 5)
                if core and (behind or not ahead):
                    turn(i, 0)
                if ahead:
                    dve.wait_ge(qk_sb, aa + 1)
                    lif = Chain(dve, k_lif, aa, 6)
                    lif.link(over(0, 0, 2))
                if experts:
                    gated(mm, 3, up_bank(i, 3))
                if ahead:
                    if behind:
                        take_v(aa)
                    lif.meet()
                    lif.link(over(1, 0, 2))
                if experts:
                    hidden(mm, 3, up_bank(i, 3))
                if ahead:
                    lif.meet()
                    lif.link(over(2, 0, 2))
                if experts:
                    gated(mm, 4, up_bank(i, 4))
                if ahead:
                    lif.meet()
                    spikes_qk(aa, 1 - par)
                    if core and not behind:
                        turn(i, 0)
                    if not behind:
                        take_v(aa)
                if experts:
                    hidden(mm, 4, up_bank(i, 4))
                beside = ahead and experts
                if ahead:
                    dve.wait_ge(vv_sb, aa + 1)
                    lif.link(over(0, 2, 3))
                if ahead and not beside:
                    lif.meet()
                    lif(over(1, 2, 3))
                    lif(over(2, 2, 3))
                    spikes_v(aa, 1 - par)
                    lif.end()
                if isinstance(i, int) and i == 0:
                    quant(3, 5, B)
                if behind:
                    route = Chain(dve, k_top, cc, 6)
                    route_begin(cc)
                if beside:
                    lif.meet()
                    lif.link(over(1, 2, 3))
                if behind:
                    route.link(route_largest(cc))
                if beside:
                    lif.meet()
                    lif.link(over(2, 2, 3))
                if behind:
                    route.meet()
                    route.link(route_less())
                if beside:
                    lif.meet()
                    spikes_v(aa, 1 - par)
                    lif.end()
                if behind:
                    wait_apart(dve, k_top, cc * 6 + 2, (c_in, 32))
                    route.link(route_mark())
                if alone(i - 1):
                    for k in range(1, NBLK):
                        weigh(mm, k)
                if experts:
                    expert_sum(mm, par)
                    final = Chain(dve, k_fin, mm, 1)
                if behind:
                    route.meet()
                    route.link(route_pick(cc))
                if experts:
                    dve.wait_ge(dn_rd, mm + 2)
                    final.link(means(drA, dbn))
                if behind:
                    route.meet()
                    route.link(route_sum())
                if experts:
                    wait_apart(dve, k_fin, mm + 1, (c_in, 32))
                    variances(dmv, dbn, dmv_sb)
                    final.end()
                if behind:
                    route.meet()
                    route.link(route_norm())
                    route.end()
                if isinstance(i, int) and i < 0:
                    quant(1, 1, 2)
                if isinstance(mm, int) and mm == B - 1:
                    dve.wait_ge(yo_free, mm + 1)
                    scaled(drA, dmv, drs, k_pd, 2 * B - 1, lambda c: yo[:, par, c:c + 1, :]).then_inc(yo_sb, 1)

            dve.sem_inc(dn_rd, 1)
            quant(0, 0, 1)
            one.meet()
            one(V.tensor_tensor(scl[:], sx[:, 3:4], sw[:, 3:4], ALU.mult))
            steps(dve, step)


def kernel(**inputs):
    import numpy as np
    import concourse.bacc as bacc
    from concourse.bass_utils import run_bass_kernel_spmd

    w = {k: np.asarray(v) for k, v in inputs.items()}
    heads = lambda m: m.reshape(D, H, P).transpose(2, 1, 0)
    wide = lambda m: m.transpose(1, 0, 2).reshape(D, -1)
    blocks = lambda m: m.reshape(-1, P, D).transpose(1, 0, 2)
    gates = np.concatenate([wide(w["L1_ffn_wg_s"]), wide(w["L1_ffn_wg_r"])], 1).reshape(D, NBLK, 1, P)
    ups = np.concatenate([wide(w["L1_ffn_wu_s"]), wide(w["L1_ffn_wu_r"])], 1).reshape(D, NBLK, 1, P)
    p = np.arange(P)
    esel = np.zeros((3 * NE, NBLK - 1, EPB, ME), np.float32)
    for row in range(3 * NE):
        e = row % NE
        esel[row, e // EPB, e % EPB, :] = 1.0
    cst = np.concatenate([
        np.eye(P), p[:, None] > p[None, :], p[:, None] <= p[None, :],
        (p[:, None] // HD) % QG == np.arange(QG)[None, :],
        1.0 * (p[:, None] >= 64) - (p[:, None] < 32), (p[:, None] >= 32) & (p[:, None] < 32 + 3 * H),
        (p[:, None] % H == np.arange(H)[None, :]) & (p[:, None] % 32 < 3 * H) & (p[:, None] < 64)], 1).astype(np.float32)
    arrays = {
        "x": w["L0_attn_x"],
        "cst": cst,
        "esel": esel.reshape(3 * NE, -1),
        "rows": np.broadcast_to(np.concatenate([w["L0_attn_bg"], w["L0_ffn_bias"], w["L1_attn_v_b"], w["L1_attn_o_b"]])[None, :],
                                (P, H + 3 * D)),
        "cols": np.stack([w["L1_attn_q_b"], w["L1_attn_k_b"]], 1),
        "wqT": heads(w["L0_attn_Wq"]), "wkT": heads(w["L0_attn_Wk"]),
        "wvg": np.concatenate([w["L0_attn_Wv"], w["L0_attn_Wg"]], 1),
        "wog": w["L0_attn_Wog"], "wo": blocks(w["L0_attn_Wo"]),
        "ffw": w["L0_ffn_weight"].T,
        "wqkvo": np.stack([w["L1_attn_q_w"], w["L1_attn_k_w"], w["L1_attn_v_w"], w["L1_attn_o_w"]], 1),
        "wr": w["L1_ffn_router_w"],
        "wup": np.concatenate([gates, ups], 2),
        "wdn": np.concatenate([blocks(w["L1_ffn_wd_s"].reshape(-1, D)), blocks(w["L1_ffn_wd_r"].reshape(-1, D))], 1),
    }
    arrays = {k: np.ascontiguousarray(v) for k, v in arrays.items()}
    nc = bacc.Bacc("TRN2", target_bir_lowering=False, num_devices=1)
    aps = {k: nc.dram_tensor(k + "_dram", v.shape, mybir.dt.from_np(v.dtype), kind="ExternalInput").ap()
           for k, v in arrays.items()}
    out = nc.dram_tensor("out_dram", (B, S, D), F32, kind="ExternalOutput").ap()
    fused_layers(nc, aps, out)
    r = run_bass_kernel_spmd(nc, [{k + "_dram": v for k, v in arrays.items()}], core_ids=[0])
    return r.results[0]["out_dram"]
```
